# Optimizing a Trainium2 kernel written in Bass

```python
import numpy as np
import jax
import jax.numpy as jnp

def _softmax(x, axis=-1):
    return jax.nn.softmax(x, axis=axis)

def _gelu(x):
    return jax.nn.gelu(x, approximate=True)

def _silu(x):
    return jax.nn.silu(x)

def _sigmoid(x):
    return jax.nn.sigmoid(x)

def _layernorm(x, axis=-1, eps=1e-05):
    m = jnp.mean(x, axis=axis, keepdims=True)
    v = jnp.var(x, axis=axis, keepdims=True)
    return (x - m) / jnp.sqrt(v + eps)

def _scatter_add(tgt, idx, src, axis=0):
    return tgt.at[idx].add(src)

def _segment_sum(src, seg, n):
    return jax.ops.segment_sum(src, seg, n)
kernel_name = 'mk_perceiver_d1_seqx_r4_802356'

def setup_inputs(seed: int=0):
    np.random.seed(seed)
    _w = jnp.asarray

    def _rec_inputs():
        import jax
        import jax.numpy as jnp
        _rk = jax.random.key(seed)
        x = 7.22e-05 + 1 * jax.random.normal(jax.random.fold_in(_rk, 1), (32, 64, 256), jnp.float32)
        _lenS = 64 - jax.random.randint(jax.random.fold_in(_rk, 7), (32,), 0, max(1, 64 // 4) + 1, jnp.int32)
        _lenS2 = 1601 - jax.random.randint(jax.random.fold_in(_rk, 8), (32,), 0, max(1, 1601 // 4) + 1, jnp.int32)
        _ctx_1024P = jax.random.normal(jax.random.fold_in(_rk, 11), (32, 16, 256), jnp.float32)
        _ctx_1024c = jax.random.dirichlet(jax.random.fold_in(_rk, 511), 0.3 * jnp.ones((16,), jnp.float32), (32, 1601))
        _ctx_1024t = jnp.einsum('bsk,bkd->bsd', _ctx_1024c, _ctx_1024P)
        _ctx_1024t = _ctx_1024t * jax.lax.rsqrt(jnp.mean(jnp.square(_ctx_1024t)) + 1e-12) * 0.953939
        ctx_1024 = 4.13588e-05 + 0.999923 * (_ctx_1024t + 0.3 * jax.random.normal(jax.random.fold_in(_rk, 611), (32, 1601, 256), jnp.float32))
        _validS = jnp.arange(64)[None, :] < _lenS[:, None]
        _validS2 = jnp.arange(1601)[None, :] < _lenS2[:, None]
        _causal = jnp.tril(jnp.ones((64, 64), dtype=bool))
        mask_BxSxS2_bk0 = jnp.logical_not(jnp.broadcast_to(_validS2[:, None, :], (32, 64, 1601)))
        return (x, ctx_1024, mask_BxSxS2_bk0)
    x, ctx_1024, mask_BxSxS2_bk0 = _rec_inputs()

    def _L0_xattn_setup():
        import jax, jax.numpy as jnp
        import numpy as np
        B, S, D_IN, D_H = (4, 512, 256, 256)
        key = jax.random.key(seed)
        k1, k2, k3, k4, k5, k6 = jax.random.split(key, 6)
        seq1 = jax.random.normal(k1, (B, S, D_IN), dtype=jnp.float32)
        seq2 = jax.random.normal(k2, (B, S, D_IN), dtype=jnp.float32)
        attn_mask = jax.random.randint(k3, (B, S, S), 0, 2).astype(jnp.bool_)
        scale = 1.0 / np.sqrt(D_IN)
        Wq = jax.random.uniform(k4, (D_H, D_IN), dtype=jnp.float32, minval=-scale, maxval=scale)
        Wk = jax.random.uniform(k5, (D_H, D_IN), dtype=jnp.float32, minval=-scale, maxval=scale)
        Wv = jax.random.uniform(k6, (D_H, D_IN), dtype=jnp.float32, minval=-scale, maxval=scale)
        return {'seq1': seq1, 'seq2': seq2, 'attn_mask': attn_mask, 'Wq': Wq, 'Wk': Wk, 'Wv': Wv}
    _L0_xattn_all = _L0_xattn_setup()
    _L0_xattn_in = {k: v for k, v in _L0_xattn_all.items() if k in ('Wq', 'Wk', 'Wv')}
    del _L0_xattn_all

    def _L0_attn_setup():
        import jax, jax.numpy as jnp
        import numpy as np
        B, L, D_MODEL = (2, 256, 256)
        D_STATE, D_CONV, EXPAND = (16, 4, 2)
        D_INNER = D_MODEL * EXPAND
        LN_EPS = 1e-05

        def _forward(x, in_proj_w, conv_w, conv_b, x_proj_w, A_log, D_param, dt_w, dt_b, out_w, ln_g, ln_b):
            Lq = x.shape[1]
            xz = jnp.einsum('bld,ed->ble', x, in_proj_w)
            xb, z = (xz[..., :D_INNER], xz[..., D_INNER:])
            xpad = jnp.pad(xb, ((0, 0), (D_CONV - 1, 0), (0, 0)))
            xc = conv_b
            for k in range(D_CONV):
                xc = xc + xpad[:, k:k + Lq, :] * conv_w[:, k]
            xb = jax.nn.silu(xc)
            proj = jnp.einsum('bld,ed->ble', xb, x_proj_w)
            dt_in = proj[..., :1]
            Bp = proj[..., 1:1 + D_STATE]
            Cp = proj[..., 1 + D_STATE:]
            dt = jax.nn.softplus(dt_in * dt_w[:, 0] + dt_b)
            A = -jnp.exp(A_log)
            dA = jnp.exp(dt[..., None] * A)
            x_scaled = (xb * dt)[..., None] * Bp[..., None, :]

            def comb(a, b):
                return (a[0] * b[0], b[0] * a[1] + b[1])
            _, h = jax.lax.associative_scan(comb, (dA, x_scaled), axis=1)
            y = jnp.einsum('bldn,bln->bld', h, Cp) + xb * D_param
            mu = jnp.mean(y, axis=-1, keepdims=True)
            var = jnp.var(y, axis=-1, keepdims=True)
            y = (y - mu) / jnp.sqrt(var + LN_EPS) * ln_g + ln_b
            y = y * jax.nn.silu(z)
            return jnp.einsum('bld,ed->ble', y, out_w)
        key = jax.random.key(seed)
        ks = jax.random.split(key, 6)
        g = lambda k, shape, scale: jax.random.normal(k, shape, jnp.float32) * scale
        x = jax.random.normal(ks[0], (B, L, D_MODEL), jnp.float32)
        in_proj_w = g(ks[1], (2 * D_INNER, D_MODEL), D_MODEL ** (-0.5))
        conv_w = g(ks[2], (D_INNER, D_CONV), D_CONV ** (-0.5))
        conv_b = jnp.zeros((D_INNER,), jnp.float32)
        x_proj_w = g(ks[3], (2 * D_STATE + 1, D_INNER), D_INNER ** (-0.5))
        A_log = jnp.tile(jnp.log(jnp.arange(1, D_STATE + 1, dtype=jnp.float32)), (D_INNER, 1))
        D_param = jnp.ones((D_INNER,), jnp.float32)
        dt_w = g(ks[4], (D_INNER, 1), 1.0)
        dt_b = jnp.full((D_INNER,), -4.0, jnp.float32)
        out_w = g(ks[5], (D_MODEL, D_INNER), D_INNER ** (-0.5))
        ln_g = jnp.ones((D_INNER,), jnp.float32)
        ln_b = jnp.zeros((D_INNER,), jnp.float32)
        return dict(x=x, in_proj_w=in_proj_w, conv_w=conv_w, conv_b=conv_b, x_proj_w=x_proj_w, A_log=A_log, D_param=D_param, dt_w=dt_w, dt_b=dt_b, out_w=out_w, ln_g=ln_g, ln_b=ln_b)
    _L0_attn_all = _L0_attn_setup()
    _L0_attn_in = {k: v for k, v in _L0_attn_all.items() if k in ('in_proj_w', 'conv_w', 'conv_b', 'x_proj_w', 'A_log', 'D_param', 'dt_w', 'dt_b', 'out_w', 'ln_g', 'ln_b')}
    del _L0_attn_all

    def _L0_ffn_setup():
        import jax, jax.numpy as jnp
        import numpy as np
        B, S, D = (4, 512, 256)
        E = 8
        TOPK = 2
        I = 938

        def _swiglu(x, gate_up, down):
            h = jnp.einsum('bsd,fd->bsf', x, gate_up)
            g, u = jnp.split(h, 2, axis=-1)
            return jnp.einsum('bsi,di->bsd', jax.nn.silu(g) * u, down)
        key = jax.random.key(seed)
        ks = jax.random.split(key, 6)
        scale = 1.0 / np.sqrt(D)
        return {'hidden_states': jax.random.normal(ks[0], (B, S, D), dtype=jnp.float32), 'gate_weight': jax.random.normal(ks[1], (E, D), dtype=jnp.float32) * scale, 'shared_gate_up': jax.random.normal(ks[2], (2 * I, D), dtype=jnp.float32) * scale, 'shared_down': jax.random.normal(ks[3], (D, I), dtype=jnp.float32) * (1.0 / np.sqrt(I)), 'experts_gate_up': jax.random.normal(ks[4], (E, 2 * I, D), dtype=jnp.float32) * scale, 'experts_down': jax.random.normal(ks[5], (E, D, I), dtype=jnp.float32) * (1.0 / np.sqrt(I))}
    _L0_ffn_all = _L0_ffn_setup()
    _L0_ffn_in = {k: v for k, v in _L0_ffn_all.items() if k in ('gate_weight', 'shared_gate_up', 'shared_down', 'experts_gate_up', 'experts_down')}
    del _L0_ffn_all
    return {'x': x, 'ctx_1024': ctx_1024, 'mask_BxSxS2_bk0': mask_BxSxS2_bk0, 'L0_xattn_Wq': _L0_xattn_in['Wq'], 'L0_xattn_Wk': _L0_xattn_in['Wk'], 'L0_xattn_Wv': _L0_xattn_in['Wv'], 'L0_attn_in_proj_w': _L0_attn_in['in_proj_w'], 'L0_attn_conv_w': _L0_attn_in['conv_w'], 'L0_attn_conv_b': _L0_attn_in['conv_b'], 'L0_attn_x_proj_w': _L0_attn_in['x_proj_w'], 'L0_attn_A_log': _L0_attn_in['A_log'], 'L0_attn_D_param': _L0_attn_in['D_param'], 'L0_attn_dt_w': _L0_attn_in['dt_w'], 'L0_attn_dt_b': _L0_attn_in['dt_b'], 'L0_attn_out_w': _L0_attn_in['out_w'], 'L0_attn_ln_g': _L0_attn_in['ln_g'], 'L0_attn_ln_b': _L0_attn_in['ln_b'], 'L0_ffn_gate_weight': _L0_ffn_in['gate_weight'], 'L0_ffn_shared_gate_up': _L0_ffn_in['shared_gate_up'], 'L0_ffn_shared_down': _L0_ffn_in['shared_down'], 'L0_ffn_experts_gate_up': _L0_ffn_in['experts_gate_up'], 'L0_ffn_experts_down': _L0_ffn_in['experts_down']}

def reference(x, ctx_1024, mask_BxSxS2_bk0, L0_xattn_Wq, L0_xattn_Wk, L0_xattn_Wv, L0_attn_in_proj_w, L0_attn_conv_w, L0_attn_conv_b, L0_attn_x_proj_w, L0_attn_A_log, L0_attn_D_param, L0_attn_dt_w, L0_attn_dt_b, L0_attn_out_w, L0_attn_ln_g, L0_attn_ln_b, L0_ffn_gate_weight, L0_ffn_shared_gate_up, L0_ffn_shared_down, L0_ffn_experts_gate_up, L0_ffn_experts_down):
    import jax
    import jax.numpy as jnp

    def _L0_xattn_ref(seq1, seq2, attn_mask, Wq, Wk, Wv):
        import jax, jax.numpy as jnp
        import numpy as np
        B, S, D_IN, D_H = (4, 512, 256, 256)
        q = jnp.einsum('bsd,hd->bsh', seq1, Wq)
        k = jnp.einsum('bsd,hd->bsh', seq2, Wk)
        v = jnp.einsum('bsd,hd->bsh', seq2, Wv)
        score = jnp.einsum('bqh,bkh->bqk', q, k) / jnp.sqrt(jnp.float32(q.shape[-1]))
        mask_score = jnp.where(attn_mask, jnp.float32(1e-09), score)
        score_matrix = jax.nn.softmax(mask_score, axis=1)
        out = jnp.einsum('bqk,bkh->bqh', score_matrix, v)
        return out

    def _L0_attn_ref(x, in_proj_w, conv_w, conv_b, x_proj_w, A_log, D_param, dt_w, dt_b, out_w, ln_g, ln_b):
        import jax, jax.numpy as jnp
        import numpy as np
        B, L, D_MODEL = (2, 256, 256)
        D_STATE, D_CONV, EXPAND = (16, 4, 2)
        D_INNER = D_MODEL * EXPAND
        LN_EPS = 1e-05

        def _forward(x, in_proj_w, conv_w, conv_b, x_proj_w, A_log, D_param, dt_w, dt_b, out_w, ln_g, ln_b):
            Lq = x.shape[1]
            xz = jnp.einsum('bld,ed->ble', x, in_proj_w)
            xb, z = (xz[..., :D_INNER], xz[..., D_INNER:])
            xpad = jnp.pad(xb, ((0, 0), (D_CONV - 1, 0), (0, 0)))
            xc = conv_b
            for k in range(D_CONV):
                xc = xc + xpad[:, k:k + Lq, :] * conv_w[:, k]
            xb = jax.nn.silu(xc)
            proj = jnp.einsum('bld,ed->ble', xb, x_proj_w)
            dt_in = proj[..., :1]
            Bp = proj[..., 1:1 + D_STATE]
            Cp = proj[..., 1 + D_STATE:]
            dt = jax.nn.softplus(dt_in * dt_w[:, 0] + dt_b)
            A = -jnp.exp(A_log)
            dA = jnp.exp(dt[..., None] * A)
            x_scaled = (xb * dt)[..., None] * Bp[..., None, :]

            def comb(a, b):
                return (a[0] * b[0], b[0] * a[1] + b[1])
            _, h = jax.lax.associative_scan(comb, (dA, x_scaled), axis=1)
            y = jnp.einsum('bldn,bln->bld', h, Cp) + xb * D_param
            mu = jnp.mean(y, axis=-1, keepdims=True)
            var = jnp.var(y, axis=-1, keepdims=True)
            y = (y - mu) / jnp.sqrt(var + LN_EPS) * ln_g + ln_b
            y = y * jax.nn.silu(z)
            return jnp.einsum('bld,ed->ble', y, out_w)
        return _forward(x, in_proj_w, conv_w, conv_b, x_proj_w, A_log, D_param, dt_w, dt_b, out_w, ln_g, ln_b)

    def _L0_ffn_ref(hidden_states, gate_weight, shared_gate_up, shared_down, experts_gate_up, experts_down):
        import jax, jax.numpy as jnp
        import numpy as np
        B, S, D = (4, 512, 256)
        E = 8
        TOPK = 2
        I = 938

        def _swiglu(x, gate_up, down):
            h = jnp.einsum('bsd,fd->bsf', x, gate_up)
            g, u = jnp.split(h, 2, axis=-1)
            return jnp.einsum('bsi,di->bsd', jax.nn.silu(g) * u, down)
        x = hidden_states
        out = _swiglu(x, shared_gate_up, shared_down)
        logits = jnp.einsum('bsd,ed->bse', x, gate_weight)
        probs = jax.nn.softmax(logits.astype(jnp.float32), axis=-1)
        top_p, sel = jax.lax.top_k(probs, TOPK)
        top_p = top_p / (jnp.sum(top_p, axis=-1, keepdims=True) + 1e-08)
        cw = jnp.sum(top_p[..., None] * jax.nn.one_hot(sel, E, dtype=top_p.dtype), axis=2)
        for e in range(E):
            y = _swiglu(x, experts_gate_up[e], experts_down[e])
            out = out + cw[..., e:e + 1] * y
        return out
    x = x + _L0_xattn_ref(_layernorm(x, axis=-1), ctx_1024, mask_BxSxS2_bk0, L0_xattn_Wq, L0_xattn_Wk, L0_xattn_Wv)
    x = x + _L0_attn_ref(_layernorm(x, axis=-1), L0_attn_in_proj_w, L0_attn_conv_w, L0_attn_conv_b, L0_attn_x_proj_w, L0_attn_A_log, L0_attn_D_param, L0_attn_dt_w, L0_attn_dt_b, L0_attn_out_w, L0_attn_ln_g, L0_attn_ln_b)
    x = x + _L0_ffn_ref(_layernorm(x, axis=-1), L0_ffn_gate_weight, L0_ffn_shared_gate_up, L0_ffn_shared_down, L0_ffn_experts_gate_up, L0_ffn_experts_down)
    return x

_drawn_inputs = setup_inputs


def setup_inputs(seed=0):
    import zlib

    import numpy as np

    out = dict(_drawn_inputs(seed))
    spreads = {'L0_attn_conv_b': (0.0, 0.8),
     'L0_attn_D_param': (1.0, 0.6),
     'L0_attn_dt_b': (-4.0, 0.6),
     'L0_attn_ln_g': (1.0, 0.6),
     'L0_attn_ln_b': (0.0, 0.8)}
    factors = {'L0_attn_A_log': 3.51, 'L0_attn_dt_w': 5.645}
    for name, (base, spread) in spreads.items():
        noise = np.random.default_rng([zlib.crc32(name.encode()), seed]).standard_normal(out[name].shape)
        drawn = base * np.exp(spread * noise) if base else spread * noise
        out[name] = jnp.asarray(drawn.astype(out[name].dtype))
    for name, factor in factors.items():
        out[name] = (out[name] * factor).astype(out[name].dtype)
    return out
```

```python
from contextlib import ExitStack

import numpy as np

import concourse.bass as bass
from concourse import mybir

F32 = mybir.dt.float32
BF16 = mybir.dt.bfloat16
U8 = mybir.dt.uint8
U32 = mybir.dt.uint32
ALU = mybir.AluOpType
ACT = mybir.ActivationFunctionType
AX = mybir.AxisListType

P = 128
BATCH, SEQ, DIM = 32, 64, 256
TOKENS = BATCH * SEQ
TILES = TOKENS // P
HALVES = DIM // P
CTX = 1601
KROWS = CTX // P
KREST = CTX - KROWS * P
KT = KROWS + 1
INNER, STATE, TAPS = 512, 16, 4
Q = INNER // P
CHUNK = 512
CHUNKS = TOKENS // CHUNK
CB = CHUNK // SEQ
PADDED = SEQ + TAPS - 1
EXPERTS, TOPK, FF = 8, 2, 938
FP = 118
FG = 8
EPS = 1e-5


class Count:

    def __init__(self, sem):
        self.sem, self.n = sem, 0

    def inc(self, instruction):
        self.n += 1
        instruction.then_inc(self.sem, 1)
        return self.n


def build(nc, x, ctx_rows, mask_t, wq, wk, wv_t, in_w_t, conv_w, conv_b, bc_w_t, dt_row_t, a_log,
          d_param, dt_w, dt_b, out_w_t, ln_g, ln_b, gate_w_t, gu_t, down_t, ident_in,
          sel_in, iota_in, out):
    sems = ExitStack()
    keep = ExitStack()

    def sem(name):
        return sems.enter_context(nc.semaphore(name))

    def sb(stack, name, shape, dt=F32):
        return stack.enter_context(nc.sbuf_tensor(name, shape, dt))

    with sems, keep:
        xres = sb(keep, "xres", [P, TILES, DIM])
        xnT = sb(keep, "xnT", [P, HALVES, TOKENS])
        ident = sb(keep, "ident", [P, P])
        stats = sb(keep, "stats", [P, TILES, 6])
        meanvar = sb(keep, "meanvar", [P, TILES, 2])
        rstd = sb(keep, "rstd", [P, TILES])
        epsc = sb(keep, "epsc", [P, 1])
        own_turn = sem("own_turn")
        banks = [keep.enter_context(nc.psum_tensor(f"bank{i}", [P, 512], F32)) for i in range(8)]

        def layernorm(tag, stack, before=None):
            xn = sb(stack, f"xn_{tag}", [P, TILES, DIM])
            stats_done, aggr_done = sem(f"stats_done_{tag}"), sem(f"aggr_done_{tag}")
            std_done, rstd_done = sem(f"std_done_{tag}"), sem(f"rstd_done_{tag}")
            xn_ready, turned, bank_free = sem(f"xn_ready_{tag}"), sem(f"turned_{tag}"), sem(f"turn_free_{tag}")

            def vector(dve):
                for i in range(TILES):
                    if before:
                        before(dve, i)
                    dve.bn_stats(stats[:, i, :], xres[:, i, :]).then_inc(stats_done, 1)
                for i in range(TILES):
                    dve.wait_ge(stats_done, i + 1)
                    dve.bn_aggr(meanvar[:, i, :], stats[:, i, :]).then_inc(aggr_done, 1)
                dve.wait_ge(std_done, 1)
                dve.reciprocal(rstd[:, :], rstd[:, :]).then_inc(rstd_done, 1)
                dve.wait_ge(rstd_done, 1)
                for i in range(TILES):
                    dve.tensor_scalar(xn[:, i, :], xres[:, i, :], meanvar[:, i, 0:1], rstd[:, i:i + 1],
                                      ALU.subtract, ALU.mult).then_inc(xn_ready, 1)

            def scalar(act):
                act.wait_ge(aggr_done, TILES)
                act.activation(rstd[:, :], meanvar[:, :, 1], ACT.Sqrt, bias=epsc[:, 0:1]).then_inc(std_done, 1)
                for g in range(TILES // 2):
                    act.wait_ge(turned, g + 1)
                    act.copy(xnT[:, :, g * 2 * P:(g + 1) * 2 * P],
                             banks[g % 2][:, :].rearrange("p (h t) -> p h t", h=HALVES)).then_inc(bank_free, 1)

            def tensor(pe):
                for g in range(TILES // 2):
                    pe.wait_ge(xn_ready, 2 * g + 2)
                    if g >= 2:
                        pe.wait_ge(bank_free, g - 1)
                    for h in range(HALVES):
                        for t in range(2):
                            at = (h * 2 + t) * P
                            last = pe.transpose(banks[g % 2][:, at:at + P],
                                                xn[:, 2 * g + t, h * P:(h + 1) * P], ident[:, :])
                    last.then_inc(turned, 1)

            return vector, scalar, tensor, bank_free

        att = ExitStack()
        with att:
            qkT = sb(att, "qkT", [P, HALVES, TOKENS])
            wv_sb = sb(att, "wv_sb", [P, HALVES, DIM])
            with ExitStack() as first:
                wq_sb = sb(first, "wq_sb", [P, HALVES, DIM])
                wk_sb = sb(first, "wk_sb", [P, HALVES, DIM])
                wqk = sb(first, "wqk", [P, HALVES, DIM])
                x_in = [sem(f"x_in{i}") for i in range(4)]
                ident_in_s, w_in, eps_set = sem("ident_loaded"), sem("attention_weights_loaded"), sem("eps_set")
                wqk_done, wqk_copied = sem("wqk_done"), sem("wqk_copied")
                qk_done, qk_copied = sem("qk_done"), sem("qk_copied")
                nx = TILES // 4
                vec, sca, ten, ln_copied = layernorm(
                    "a", first, lambda dve, i: dve.wait_ge(x_in[i // nx], 16) if i % nx == 0 else None)
                with nc.Block() as block:
                    @block.sync
                    def _(sp):
                        for c in range(4):
                            sp.dma_start(xres[:, c * nx:(c + 1) * nx, :],
                                         x[c * nx * P:(c + 1) * nx * P, :].rearrange("(i p) d -> p i d", p=P)
                                         ).then_inc(x_in[c], 16)
                        sp.dma_start(ident[:, :], ident_in).then_inc(ident_in_s, 16)
                        for dst, src in ((wq_sb, wq), (wk_sb, wk), (wv_sb, wv_t)):
                            sp.dma_start(dst[:, :, :], src.rearrange("(h p) d -> p h d", p=P)).then_inc(w_in, 16)
                        sp.wait_ge(w_in, 48)

                    @block.vector
                    def _(dve):
                        dve.memset(epsc[:, :], EPS).then_inc(eps_set, 1)
                        vec(dve)

                    @block.scalar
                    def _(act):
                        act.wait_ge(eps_set, 1)
                        sca(act)
                        for k in range(HALVES):
                            act.wait_ge(wqk_done, k + 1)
                            act.copy(wqk[:, k, :], banks[2 + k][:, 0:DIM]).then_inc(wqk_copied, 1)
                        for n in range(HALVES * CHUNKS):
                            h, c = n % HALVES, n // HALVES
                            act.wait_ge(qk_done, n + 1)
                            act.copy(qkT[:, h, c * CHUNK:(c + 1) * CHUNK], banks[4 + n % 4][:, :]).then_inc(qk_copied, 1)

                    @block.tensor
                    def _(pe):
                        pe.wait_ge(ident_in_s, 16)
                        pe.wait_ge(w_in, 48)
                        ten(pe)
                        for k in range(HALVES):
                            for h in range(HALVES):
                                mm = pe.matmul(banks[2 + k][:, 0:DIM], wq_sb[:, h, k * P:(k + 1) * P], wk_sb[:, h, :],
                                               start=(h == 0), stop=(h == HALVES - 1))
                            mm.then_inc(wqk_done, 1)
                        pe.wait_ge(wqk_copied, HALVES)
                        pe.wait_ge(ln_copied, TILES // 2)
                        for n in range(HALVES * CHUNKS):
                            h, c = n % HALVES, n // HALVES
                            if n >= 4:
                                pe.wait_ge(qk_copied, n - 3)
                            for k in range(HALVES):
                                mm = pe.matmul(banks[4 + n % 4][:, :], wqk[:, k, h * P:(h + 1) * P],
                                               xnT[:, k, c * CHUNK:(c + 1) * CHUNK],
                                               start=(k == 0), stop=(k == HALVES - 1))
                            mm.then_inc(qk_done, 1)

            with ExitStack() as st:
                ctx_sb = [sb(st, f"ctx{s}", [P, KT, DIM]) for s in range(2)]
                ctxT = [sb(st, f"ctxT{s}", [P, KT * HALVES, P]) for s in range(2)]
                mask_words = [sb(st, f"mask{s}", [P, KT, SEQ // 4], U32) for s in range(2)]
                mask_sb = [m[:, :, :].bitcast(U8) for m in mask_words]
                sc = [sb(st, f"scores{s}", [P, KT, SEQ]) for s in range(2)]
                rowmax = [sb(st, f"rowmax{s}", [P, KT]) for s in range(2)]
                rowsum = [sb(st, f"rowsum{s}", [P, KT]) for s in range(2)]
                rowinv = [sb(st, f"rowinv{s}", [P, KT]) for s in range(2)]
                fill = sb(st, "fill", [P, KT, SEQ])
                pcT = sb(st, "pcT", [P, HALVES, P])
                cleared, fill_set = sem("padding_cleared"), sem("fill_set")
                ctx_in = [sem(f"ctx_in{s}") for s in range(2)]
                turned = [sem(f"ctx_turned{b}") for b in range(2)]
                turn_free = [sem(f"turn_bank_free{b}") for b in range(2)]
                s_done = [sem(f"scores_done{s}") for s in range(2)]
                s_copied = [sem(f"scores_copied{s}") for s in range(2)]
                s_masked = [sem(f"scores_masked{s}") for s in range(2)]
                s_max = [sem(f"scores_max{s}") for s in range(2)]
                s_shift = [sem(f"scores_shifted{s}") for s in range(2)]
                s_exp = [sem(f"scores_exp{s}") for s in range(2)]
                s_sum = [sem(f"scores_sum{s}") for s in range(2)]
                s_inv = [sem(f"scores_inverse{s}") for s in range(2)]
                p_ready = [sem(f"probs_ready{s}") for s in range(2)]
                pv_done, pv_copied = sem("pv_done"), sem("pv_copied")
                o_done, o_added = sem("attention_out_done"), sem("attention_out_added")
                GROUPS = [list(range(g, min(g + 4, KT * HALVES))) for g in range(0, KT * HALVES, 4)]
                NG = len(GROUPS)
                PARTS = [(0, 7), (7, KT)]
                PAIRS = BATCH // 2

                with nc.Block() as block:
                    @block.sync
                    def _(sp):
                        sp.wait_ge(cleared, 4)

                        def load(i, s):
                            base = (2 * i + s) * CTX
                            rows, rest = bass.ds(base, KROWS * P), bass.ds(base + KROWS * P, KREST)
                            sp.dma_start(ctx_sb[s][:, 0:KROWS, :],
                                         ctx_rows[rows, :].rearrange("(p t) d -> p t d", t=KROWS)).then_inc(ctx_in[s], 16)
                            sp.dma_start(mask_words[s][:, 0:KROWS, :],
                                         mask_t[rows, :].rearrange("(p t) q -> p t q", t=KROWS)).then_inc(ctx_in[s], 16)
                            sp.dma_start(ctx_sb[s][0:KREST, KROWS, :], ctx_rows[rest, :]).then_inc(ctx_in[s], 16)
                            sp.dma_start(mask_words[s][0:KREST, KROWS, :], mask_t[rest, :]).then_inc(ctx_in[s], 16)

                        load(0, 0)
                        load(0, 1)
                        with sp.Fori(1, PAIRS) as i:
                            for s in range(2):
                                sp.wait_ge(pv_done, 2 * i + s - 1)
                                sp.wait_ge(s_masked[s], 2 * i)
                                load(i, s)

                    @block.vector
                    def _(dve):
                        for s in range(2):
                            dve.memset(ctx_sb[s][:, KROWS, :], 0.0).then_inc(cleared, 1)
                            dve.memset(mask_words[s][:, KROWS, :], 0).then_inc(cleared, 1)
                        dve.memset(fill[:, :, :], 1e-9).then_inc(fill_set, 1)
                        dve.wait_ge(fill_set, 1)

                        def softmax(i, s):
                            for n, (a, b) in enumerate(PARTS):
                                k = 2 * i + n + 1
                                view = sc[s][:, a:b, :]
                                if n == 0:
                                    dve.wait_ge(ctx_in[s], 64 * i + 64)
                                dve.wait_ge(s_copied[s], k)
                                dve.sem_inc(own_turn, 1)
                                dve.copy_predicated(view, mask_sb[s][:, a:b, :], fill[:, a:b, :]).then_inc(s_masked[s], 1)
                                dve.wait_ge(s_masked[s], k)
                                dve.tensor_reduce(rowmax[s][:, a:b], view, AX.X, ALU.max).then_inc(s_max[s], 1)
                            for n, (a, b) in enumerate(PARTS):
                                k = 2 * i + n + 1
                                view = sc[s][:, a:b, :]
                                dve.wait_ge(s_exp[s], k)
                                dve.tensor_reduce(rowsum[s][:, a:b], view, AX.X, ALU.add).then_inc(s_sum[s], 1)
                                dve.wait_ge(s_sum[s], k)
                                dve.reciprocal(rowinv[s][:, a:b], rowsum[s][:, a:b]).then_inc(s_inv[s], 1)
                                dve.wait_ge(s_inv[s], k)
                                dve.tensor_tensor(view, view, rowinv[s][:, a:b].unsqueeze(2).broadcast_to([P, b - a, SEQ]),
                                                  ALU.mult).then_inc(p_ready[s], 1)

                        def add_out(i):
                            dve.wait_ge(o_done, i + 1)
                            dve.tensor_tensor(xres[:, bass.ds(i, 1), :].rearrange("p o d -> p (o d)"),
                                              xres[:, bass.ds(i, 1), :].rearrange("p o d -> p (o d)"),
                                              banks[7][:, 0:DIM], ALU.add).then_inc(o_added, 1)

                        softmax(0, 0)
                        with dve.Fori(0, PAIRS - 1) as i:
                            softmax(i, 1)
                            softmax(i + 1, 0)
                            add_out(i)
                        softmax(PAIRS - 1, 1)
                        add_out(PAIRS - 1)

                    @block.gpsimd
                    def _(pool):
                        def shift(i, s):
                            for n, (a, b) in enumerate(PARTS):
                                k = 2 * i + n + 1
                                view = sc[s][:, a:b, :]
                                pool.wait_ge(s_max[s], k)
                                pool.tensor_tensor(view, view, rowmax[s][:, a:b].unsqueeze(2).broadcast_to([P, b - a, SEQ]),
                                                   ALU.subtract).then_inc(s_shift[s], 1)

                        with pool.Fori(0, PAIRS) as i:
                            shift(i, 0)
                            shift(i, 1)

                    @block.scalar
                    def _(act):
                        def turn_out(i, s):
                            for g, blocks in enumerate(GROUPS):
                                n = s * NG + g
                                act.wait_ge(turned[n % 2], NG * i + n // 2 + 1)
                                act.copy(ctxT[s][:, blocks[0]:blocks[-1] + 1, :],
                                         banks[n % 2][:, 0:len(blocks) * P].rearrange("p (b k) -> p b k", k=P)
                                         ).then_inc(turn_free[n % 2], 1)

                        def copy_scores(i, s, first=False):
                            for n, (a, b) in enumerate(PARTS):
                                k = 2 * i + n + 1
                                act.wait_ge(s_done[s], k)
                                if n == 0 and not first:
                                    act.wait_ge(pv_done, 2 * i + s - 1)
                                act.mul(sc[s][:, a:b, :], banks[2 + 2 * s + n][:, 0:(b - a) * SEQ]
                                        .rearrange("p (t q) -> p t q", q=SEQ), DIM ** -0.5).then_inc(s_copied[s], 1)

                        def exps(i, s):
                            for n, (a, b) in enumerate(PARTS):
                                k = 2 * i + n + 1
                                view = sc[s][:, a:b, :]
                                act.wait_ge(s_shift[s], k)
                                act.activation(view, view, ACT.Exp).then_inc(s_exp[s], 1)

                        def pv_out(i, s, first=False):
                            act.wait_ge(pv_done, 2 * i + s + 1)
                            if s == 0 and not first:
                                act.wait_ge(o_done, i)
                            act.copy(pcT[:, :, s * SEQ:(s + 1) * SEQ],
                                     banks[6][:, 0:HALVES * SEQ].rearrange("p (h q) -> p h q", q=SEQ)
                                     ).then_inc(pv_copied, 1)

                        def pair(i, first=False, last=False):
                            exps(i, 0)
                            turn_out(i, 1)
                            copy_scores(i, 1, first)
                            pv_out(i, 0, first)
                            exps(i, 1)
                            if not last:
                                turn_out(i + 1, 0)
                                copy_scores(i + 1, 0)
                            pv_out(i, 1)

                        turn_out(0, 0)
                        copy_scores(0, 0, first=True)
                        pair(0, first=True)
                        with act.Fori(1, PAIRS - 1) as i:
                            pair(i)
                        pair(PAIRS - 1, last=True)

                    @block.tensor
                    def _(pe):
                        def turn(i, s, first=False):
                            pe.wait_ge(ctx_in[s], 64 * i + 64)
                            for g, blocks in enumerate(GROUPS):
                                n = s * NG + g
                                if not (first and n < 2):
                                    pe.wait_ge(turn_free[n % 2], NG * i + n // 2)
                                for at, blk in enumerate(blocks):
                                    t, h = blk // HALVES, blk % HALVES
                                    mm = pe.transpose(banks[n % 2][:, at * P:(at + 1) * P],
                                                      ctx_sb[s][:, t, h * P:(h + 1) * P], ident[:, :])
                                mm.then_inc(turned[n % 2], 1)

                        def scores(i, s, first=False):
                            for n in (s * NG + NG - 1, s * NG + NG - 2):
                                pe.wait_ge(turn_free[n % 2], NG * i + n // 2 + 1)
                            if not first:
                                pe.wait_ge(s_copied[s], 2 * i)
                            for n, (a, b) in enumerate(PARTS):
                                for t in range(a, b):
                                    for h in range(HALVES):
                                        mm = pe.matmul(banks[2 + 2 * s + n][:, (t - a) * SEQ:(t - a + 1) * SEQ],
                                                       ctxT[s][:, t * HALVES + h, :],
                                                       qkT[:, h, bass.ds((2 * i + s) * SEQ, SEQ)],
                                                       start=(h == 0), stop=(h == HALVES - 1))
                                mm.then_inc(s_done[s], 1)

                        def weigh(i, s, first=False):
                            pe.wait_ge(p_ready[s], 2 * i + 2)
                            if not (first and s == 0):
                                pe.wait_ge(pv_copied, 2 * i + s)
                            for h in range(HALVES):
                                for t in range(KT):
                                    mm = pe.matmul(banks[6][:, h * SEQ:(h + 1) * SEQ], ctx_sb[s][:, t, h * P:(h + 1) * P],
                                                   sc[s][:, t, :], start=(t == 0), stop=(t == KT - 1))
                            mm.then_inc(pv_done, 1)

                        def project(i, first=False):
                            pe.wait_ge(pv_copied, 2 * i + 2)
                            if not first:
                                pe.wait_ge(o_added, i)
                            for h in range(HALVES):
                                mm = pe.matmul(banks[7][:, 0:DIM], pcT[:, h, :], wv_sb[:, h, :],
                                               start=(h == 0), stop=(h == HALVES - 1))
                            mm.then_inc(o_done, 1)

                        def pair(i, first=False, last=False):
                            turn(i, 1, first)
                            scores(i, 1, first)
                            weigh(i, 0, first)
                            if not last:
                                turn(i + 1, 0)
                                scores(i + 1, 0)
                            weigh(i, 1)
                            project(i, first)

                        pe.wait_ge(fill_set, 1)
                        turn(0, 0, first=True)
                        scores(0, 0, first=True)
                        pair(0, first=True)
                        with pe.Fori(1, PAIRS - 1) as i:
                            pair(i)
                        pair(PAIRS - 1, last=True)


        with ExitStack() as st:
            in_w = sb(st, "in_w", [P, HALVES, 2 * INNER])
            cw = sb(st, "cw", [P, Q, TAPS])
            cb = sb(st, "cb", [P, Q])
            bc_w = sb(st, "bc_w", [P, Q, 2 * STATE])
            dt_row = sb(st, "dt_row", [P, Q, P])
            a_neg = sb(st, "a_neg", [P, Q, STATE])
            dpar = sb(st, "dpar", [P, Q])
            dtw = sb(st, "dtw", [P, Q])
            dtb = sb(st, "dtb", [P, Q])
            out_w = sb(st, "out_w", [P, Q, DIM])
            lng = sb(st, "lng", [P, Q])
            lnb = sb(st, "lnb", [P, Q])
            d_diag = sb(st, "d_diag", [P, Q, P])
            mean_w = sb(st, "mean_w", [P, P])
            sel = sb(st, "sel", [6 * STATE, 2 * STATE, P // 2], U32)
            weights_in, small_set, a_exp, a_done = sem("mamba_weights_in"), sem("small_set"), sem("a_exp"), sem("a_done")
            ln_st = ExitStack()
            vec, sca, ten, _ = layernorm("b", ln_st)
            loads = [(in_w, in_w_t.rearrange("(h p) e -> p h e", p=P)),
                     (cw, conv_w.rearrange("(q p) k -> p q k", p=P)), (cb, conv_b.rearrange("(q p) -> p q", p=P)),
                     (bc_w, bc_w_t.rearrange("(q p) n -> p q n", p=P)),
                     (dt_row, dt_row_t.rearrange("(q p) n -> p q n", p=P)),
                     (a_neg, a_log.rearrange("(q p) n -> p q n", p=P)), (dpar, d_param.rearrange("(q p) -> p q", p=P)),
                     (dtw, dt_w.rearrange("(q p) o -> p (q o)", p=P)), (dtb, dt_b.rearrange("(q p) -> p q", p=P)),
                     (out_w, out_w_t.rearrange("(q p) d -> p q d", p=P)),
                     (lng, ln_g.rearrange("(q p) -> p q", p=P)), (lnb, ln_b.rearrange("(q p) -> p q", p=P)),
                     (sel, sel_in)]
            with nc.Block() as block:
                @block.sync
                def _(sp):
                    for dst, src in loads:
                        with nc.allow_non_contiguous_dma("a few small vectors"):
                            sp.dma_start(dst[tuple([slice(None)] * len(dst.shape))], src).then_inc(weights_in, 16)
                    sp.wait_ge(weights_in, 16 * len(loads))

                @block.vector
                def _(dve):
                    vec(dve)
                    dve.memset(mean_w[:, :], 1.0 / INNER).then_inc(small_set, 1)
                    dve.wait_ge(weights_in, 16 * len(loads))
                    for q in range(Q):
                        dve.tensor_scalar(d_diag[:, q, :], ident[:, :], dpar[:, q:q + 1], None, ALU.mult).then_inc(small_set, 1)

                @block.scalar
                def _(act):
                    sca(act)
                    act.wait_ge(weights_in, 16 * len(loads))
                    act.activation(a_neg[:, :, :], a_neg[:, :, :], ACT.Exp).then_inc(a_exp, 1)
                    act.wait_ge(a_exp, 1)
                    act.mul(a_neg[:, :, :], a_neg[:, :, :], -1.0).then_inc(a_done, 1)

                @block.tensor
                def _(pe):
                    ten(pe)
            ln_st.close()

            xpad = sb(st, "xpad", [P, Q, CB, PADDED])
            xb = sb(st, "xb", [P, Q, CHUNK])
            sz = sb(st, "sz", [P, Q, CHUNK])
            dt = sb(st, "dt", [P, Q, CHUNK])
            xdt = sb(st, "xdt", [P, Q, CHUNK])
            tmp = sb(st, "tmp", [P, Q, CHUNK])
            tmp2 = sb(st, "tmp2", [P, Q, CHUNK])
            tmp3 = sb(st, "tmp3", [P, Q, CHUNK])
            small = sb(st, "small", [P, Q, CHUNK], U8)
            bc_parts = sb(st, "bc_parts", [6 * STATE, CHUNK], BF16)
            bc_mid = sb(st, "bc_mid", [2 * STATE, CHUNK], BF16)
            bc_rest = sb(st, "bc_rest", [2 * STATE, CHUNK])
            b_sb = [sb(st, f"b_sb{s}", [P, CHUNK]) for s in range(2)]
            dA = [sb(st, f"dA{s}", [P, Q, CB, SEQ]) for s in range(2)]
            u = [sb(st, f"u{s}", [P, Q, CHUNK]) for s in range(2)]
            sel16 = sel[:, :, :].bitcast(BF16)
            yc, sq = tmp, tmp2
            BB, CC, YY = banks[0:2], banks[2:4], banks[4:8]

            padded = sem("padding_zeroed")
            in_done = [sem(f"in_proj_done{b}") for b in range(4)]
            in_copied = [sem(f"in_proj_copied{b}") for b in range(4)]
            conv_part, conv_done = sem("conv_part"), sem("conv_done")
            xb_ready = sem("xb_ready")
            dt_done, bc_done = sem("dt_product_done"), sem("bc_product_done")
            dt_abs, dt_z, dt_log, dt_relu = sem("dt_abs"), sem("dt_z"), sem("dt_log"), sem("dt_relu")
            dt_step, dt_ready, xdt_ready = sem("dt_step"), sem("dt_ready"), sem("xdt_ready")
            part_step, parts_ready = sem("bc_part_step"), sem("bc_parts_ready")
            b_done = [sem(f"b_spread{s}") for s in range(2)]
            c_done = [sem(f"c_spread{s}") for s in range(2)]
            b_copied = [sem(f"b_copied{s}") for s in range(2)]
            dA_ready = [sem(f"dA_ready{s}") for s in range(2)]
            xs_ready = [sem(f"xs_ready{s}") for s in range(2)]
            h_ready = [sem(f"h_ready{s}") for s in range(2)]
            hc_ready = [sem(f"hc_ready{s}") for s in range(2)]
            hc_used = [sem(f"hc_used{s}") for s in range(2)]
            y_copied = sem("y_copied")
            mean_done, yc_ready, sq_ready, var_done = sem("mean_done"), sem("yc_ready"), sem("sq_ready"), sem("var_done")
            ystd, yrstd, ynorm, yaff, yfin = sem("y_std"), sem("y_rstd"), sem("y_norm"), sem("y_affine"), sem("y_final")
            op_done, op_added = sem("out_proj_done"), sem("out_proj_added")
            PAIRN = STATE // 2

            with nc.Block() as block:
                @block.tensor
                def _(pe):
                    def spread(c, j, s, first_chunk=False):
                        k = c * PAIRN + j
                        free = not (first_chunk and isinstance(j, int) and j == 0)
                        if free:
                            pe.wait_ge(hc_ready[s], Q * k)
                            pe.wait_ge(b_copied[s], k)
                        n = 2 * j + s
                        pe.matmul(BB[s][:, :], sel16[:, bass.ds(n, 1), :].rearrange("k o p -> k (o p)"), bc_parts[:, :],
                                  start=True, stop=True).then_inc(b_done[s], 1)
                        pe.matmul(CC[s][:, :], sel16[:, bass.ds(n + STATE, 1), :].rearrange("k o p -> k (o p)"),
                                  bc_parts[:, :], start=True, stop=True).then_inc(c_done[s], 1)

                    def gather(c, j, s, last=False):
                        k = c * PAIRN + j
                        for q in range(Q):
                            pe.wait_ge(hc_ready[s], Q * k + q + 1)
                            pe.matmul(YY[q][:, :], ident[:, :], u[s][:, q, :], start=False, stop=last,
                                      skip_group_check=True).then_inc(hc_used[s], 1)

                    def chunk(c, first=False):
                        for k in range(2 * Q):
                            b = k % 4
                            if k >= 4:
                                pe.wait_ge(in_copied[b], 2 * c + 1)
                            elif not first:
                                if k == 0:
                                    pe.wait_ge(op_added, 4 * c)
                                    pe.wait_ge(yrstd, c)
                            for h in range(HALVES):
                                mm = pe.matmul(banks[b][:, :], in_w[:, h, k * P:(k + 1) * P],
                                               xnT[:, h, bass.ds(c * CHUNK, CHUNK)], start=(h == 0), stop=(h == HALVES - 1))
                            mm.then_inc(in_done[b], 1)
                        pe.wait_ge(in_copied[0], 2 * c + 2)
                        pe.wait_ge(in_copied[1], 2 * c + 2)
                        for q in range(Q):
                            pe.wait_ge(xb_ready, Q * c + q + 1)
                            mm = pe.matmul(banks[0][:, :], dt_row[:, q, :], xb[:, q, :], start=(q == 0), stop=(q == Q - 1))
                        mm.then_inc(dt_done, 1)
                        for q in range(Q):
                            mm = pe.matmul(banks[1][0:2 * STATE, :], bc_w[:, q, :], xb[:, q, :], start=(q == 0), stop=(q == Q - 1))
                        mm.then_inc(bc_done, 1)
                        if not first:
                            pe.wait_ge(y_copied, Q * c)
                        for q in range(Q):
                            pe.matmul(YY[q][:, :], d_diag[:, q, :], xb[:, q, :], start=True, stop=False,
                                      skip_group_check=True)
                        pe.wait_ge(parts_ready, c + 1)
                        pe.wait_ge(dt_relu, Q * c + Q)
                        pe.wait_ge(in_copied[2], 2 * c + 2)
                        pe.wait_ge(in_copied[3], 2 * c + 2)
                        spread(c, 0, 0, first)
                        spread(c, 0, 1, first)
                        with pe.Fori(0, PAIRN - 1) as j:
                            gather(c, j, 0)
                            spread(c, j + 1, 0)
                            gather(c, j, 1)
                            spread(c, j + 1, 1)
                        gather(c, PAIRN - 1, 0)
                        gather(c, PAIRN - 1, 1, last=True)
                        for q in range(Q):
                            pe.wait_ge(y_copied, Q * c + q + 1)
                            mm = pe.matmul(banks[0][:, :], mean_w[:, :], yc[:, q, :], start=(q == 0), stop=(q == Q - 1))
                        mm.then_inc(mean_done, 1)
                        for q in range(Q):
                            pe.wait_ge(sq_ready, Q * c + q + 1)
                            mm = pe.matmul(banks[1][:, :], mean_w[:, :], sq[:, q, :], start=(q == 0), stop=(q == Q - 1))
                        mm.then_inc(var_done, 1)
                        pe.wait_ge(yfin, Q * c + Q)
                        for t in range(CHUNK // P):
                            if t >= 2:
                                pe.wait_ge(op_added, 4 * c + t - 1)
                            for q in range(Q):
                                mm = pe.matmul(banks[2 + t % 2][:, 0:DIM], yc[:, q, t * P:(t + 1) * P], out_w[:, q, :],
                                               start=(q == 0), stop=(q == Q - 1))
                            mm.then_inc(op_done, 1)

                    pe.wait_ge(small_set, 1 + Q)
                    chunk(0, first=True)
                    with pe.Fori(1, CHUNKS) as c:
                        chunk(c)

                @block.scalar
                def _(act):
                    def states(c, j, s, first=False):
                        k = c * PAIRN + j
                        n = 2 * j + s
                        act.wait_ge(b_done[s], k + 1)
                        if not first:
                            act.wait_ge(xs_ready[s], Q * k)
                        act.copy(b_sb[s][:, :], BB[s][:, :]).then_inc(b_copied[s], 1)
                        for q in range(Q):
                            if q == 0 and not first:
                                act.wait_ge(h_ready[s], Q * k)
                            act.activation(dA[s][:, q, :, 1:SEQ], dt[:, q, :].rearrange("p (b l) -> p b l", l=SEQ)[:, :, 1:SEQ],
                                           ACT.Exp, scale=a_neg[:, q, bass.ds(n, 1)]).then_inc(dA_ready[s], 1)

                    def chunk(c, first=False):
                        for k in range(2 * Q):
                            b, q = k % 4, k % Q
                            act.wait_ge(in_done[b], 2 * c + k // 4 + 1)
                            if k < Q:
                                if k == 0 and not first:
                                    act.wait_ge(conv_done, Q * c)
                                act.copy(xpad[:, q, :, TAPS - 1:PADDED],
                                         banks[b][:, :].rearrange("p (b l) -> p b l", l=SEQ)).then_inc(in_copied[b], 1)
                            else:
                                if q == 0 and not first:
                                    act.wait_ge(yfin, Q * c)
                                act.activation(sz[:, q, :], banks[b][:, :], ACT.Silu).then_inc(in_copied[b], 1)
                        for q in range(Q):
                            act.wait_ge(conv_done, Q * c + q + 1)
                            act.activation(xb[:, q, :], xb[:, q, :], ACT.Silu).then_inc(xb_ready, 1)
                        act.wait_ge(dt_done, c + 1)
                        if not first:
                            act.wait_ge(op_done, 4 * c)
                            act.wait_ge(var_done, c)
                        for q in range(Q):
                            act.activation(tmp[:, q, :], banks[0][:, :], ACT.Abs, bias=dtb[:, q:q + 1],
                                           scale=dtw[:, q:q + 1]).then_inc(dt_abs, 1)
                            act.activation(dt[:, q, :], banks[0][:, :], ACT.Relu, bias=dtb[:, q:q + 1],
                                           scale=dtw[:, q:q + 1]).then_inc(dt_relu, 1)
                        act.wait_ge(dt_abs, Q * c + Q)
                        act.activation(tmp[:, :, :], tmp[:, :, :], ACT.Exp, scale=-1.0).then_inc(dt_z, 1)
                        act.wait_ge(dt_z, c + 1)
                        act.activation(tmp2[:, :, :], tmp[:, :, :], ACT.Ln, bias=1.0).then_inc(dt_log, 1)
                        act.wait_ge(dt_ready, c + 1)
                        states(c, 0, 0, first)
                        states(c, 0, 1, first)
                        with act.Fori(1, PAIRN) as j:
                            states(c, j, 0)
                            states(c, j, 1)
                        for q in range(Q):
                            act.wait_ge(hc_used[1], Q * PAIRN * c + Q * (PAIRN - 1) + q + 1)
                            act.copy(yc[:, q, :], YY[q][:, :]).then_inc(y_copied, 1)
                        for q in range(Q):
                            act.wait_ge(yc_ready, Q * c + q + 1)
                            act.activation(sq[:, q, :], yc[:, q, :], ACT.Square).then_inc(sq_ready, 1)
                        act.wait_ge(var_done, c + 1)
                        act.activation(tmp3[:, 0, :], banks[1][:, :], ACT.Sqrt, bias=epsc[:, 0:1]).then_inc(ystd, 1)
                        for q in range(Q):
                            act.wait_ge(ynorm, Q * c + q + 1)
                            act.activation(yc[:, q, :], yc[:, q, :], ACT.Identity, bias=lnb[:, q:q + 1],
                                           scale=lng[:, q:q + 1]).then_inc(yaff, 1)

                    act.wait_ge(padded, 3)
                    chunk(0, first=True)
                    with act.Fori(1, CHUNKS) as c:
                        chunk(c)

                @block.vector
                def _(dve):
                    dve.memset(xpad[:, :, :, 0:TAPS - 1], 0.0).then_inc(padded, 1)
                    for s in range(2):
                        dve.memset(dA[s][:, :, :, 0:1], 0.0).then_inc(padded, 1)

                    def states(c, j, s):
                        k = c * PAIRN + j
                        for q in range(Q):
                            dve.wait_ge(dA_ready[s], Q * k + q + 1)
                            dve.wait_ge(xs_ready[s], Q * k + q + 1)
                            dve.tensor_tensor_scan(u[s][:, q, :], dA[s][:, q, :, :].rearrange("p b l -> p (b l)"),
                                                   u[s][:, q, :], 0.0, ALU.mult, ALU.add).then_inc(h_ready[s], 1)
                        dve.wait_ge(c_done[s], k + 1)
                        for q in range(Q):
                            dve.wait_ge(h_ready[s], Q * k + q + 1)
                            dve.tensor_tensor(u[s][:, q, :], u[s][:, q, :], CC[s][:, :], ALU.mult).then_inc(hc_ready[s], 1)

                    def chunk(c, first=False):
                        for q in range(Q):
                            dve.wait_ge(in_copied[q], 2 * c + 1)
                            row = xb[:, q, :].rearrange("p (b l) -> p b l", l=SEQ)
                            if q == 0 and not first:
                                dve.wait_ge(hc_used[1], Q * PAIRN * c)
                            dve.tensor_scalar(row, xpad[:, q, :, 0:SEQ], cw[:, q, 0:1], cb[:, q:q + 1],
                                              ALU.mult, ALU.add).then_inc(conv_part, 1)
                            for k in range(1, TAPS):
                                dve.wait_ge(conv_part, (Q * c + q) * (TAPS - 1) + k)
                                dve.scalar_tensor_tensor(row, xpad[:, q, :, k:k + SEQ], cw[:, q, k:k + 1], row,
                                                         ALU.mult, ALU.add).then_inc(conv_part if k < TAPS - 1 else conv_done, 1)
                        dve.wait_ge(bc_done, c + 1)
                        bank = banks[1][0:2 * STATE, :]
                        hi, mid, lo = (bc_parts[2 * STATE * k:2 * STATE * (k + 1), :] for k in range(3))
                        base = 5 * c
                        dve.tensor_copy(hi, bank).then_inc(part_step, 1)
                        dve.wait_ge(part_step, base + 1)
                        dve.tensor_tensor(bc_rest[:, :], bank, hi, ALU.subtract).then_inc(part_step, 1)
                        dve.wait_ge(part_step, base + 2)
                        dve.tensor_copy(bc_mid[:, :], bc_rest[:, :]).then_inc(part_step, 1)
                        dve.wait_ge(part_step, base + 3)
                        dve.tensor_copy(mid, bc_mid[:, :]).then_inc(part_step, 1)
                        dve.tensor_tensor(bc_rest[:, :], bc_rest[:, :], bc_mid[:, :], ALU.subtract).then_inc(part_step, 1)
                        dve.wait_ge(part_step, base + 5)
                        dve.tensor_copy(lo, bc_rest[:, :]).then_inc(parts_ready, 1)
                        dve.wait_ge(dt_log, c + 1)
                        z, t3 = tmp[:, :, :], tmp3[:, :, :]
                        steps = 7 * c
                        dve.tensor_scalar(small[:, :, :], z, 1.0 / 32, None, ALU.is_lt).then_inc(dt_step, 1)
                        dve.tensor_scalar(t3, z, 0.2, -0.25, ALU.mult, ALU.add).then_inc(dt_step, 1)
                        dve.wait_ge(dt_step, steps + 2)
                        dve.tensor_tensor(t3, t3, z, ALU.mult).then_inc(dt_step, 1)
                        for n, coefficient in enumerate((1.0 / 3, -0.5, 1.0)):
                            dve.wait_ge(dt_step, steps + 3 + n)
                            dve.scalar_tensor_tensor(t3, t3, coefficient, z, ALU.add, ALU.mult).then_inc(dt_step, 1)
                        dve.wait_ge(dt_step, steps + 6)
                        dve.sem_inc(own_turn, 1)
                        dve.copy_predicated(tmp2[:, :, :], small[:, :, :], t3).then_inc(dt_step, 1)
                        dve.wait_ge(dt_step, steps + 7)
                        dve.wait_ge(dt_relu, Q * c + Q)
                        dve.tensor_tensor(dt[:, :, :], dt[:, :, :], tmp2[:, :, :], ALU.add).then_inc(dt_ready, 1)
                        dve.wait_ge(dt_ready, c + 1)
                        dve.tensor_tensor(xdt[:, :, :], xb[:, :, :], dt[:, :, :], ALU.mult).then_inc(xdt_ready, 1)
                        with dve.Fori(0, PAIRN) as j:
                            states(c, j, 0)
                            states(c, j, 1)
                        dve.wait_ge(mean_done, c + 1)
                        for q in range(Q):
                            dve.tensor_tensor(yc[:, q, :], yc[:, q, :], banks[0][:, :], ALU.subtract).then_inc(yc_ready, 1)
                        dve.wait_ge(ystd, c + 1)
                        dve.reciprocal(tmp3[:, 0, :], tmp3[:, 0, :]).then_inc(yrstd, 1)
                        dve.wait_ge(yrstd, c + 1)
                        dve.wait_ge(sq_ready, Q * c + Q)
                        for q in range(Q):
                            dve.tensor_tensor(yc[:, q, :], yc[:, q, :], tmp3[:, 0, :], ALU.mult).then_inc(ynorm, 1)
                        for q in range(Q):
                            dve.wait_ge(yaff, Q * c + q + 1)
                            dve.tensor_tensor(yc[:, q, :], yc[:, q, :], sz[:, q, :], ALU.mult).then_inc(yfin, 1)
                        for t in range(CHUNK // P):
                            dve.wait_ge(op_done, 4 * c + t + 1)
                            rows = xres[:, bass.ds(4 * c + t, 1), :].rearrange("p o d -> p (o d)")
                            dve.tensor_tensor(rows, rows, banks[2 + t % 2][:, 0:DIM], ALU.add).then_inc(op_added, 1)

                    chunk(0, first=True)
                    with dve.Fori(1, CHUNKS) as c:
                        chunk(c)

                @block.gpsimd
                def _(pool):
                    def states(c, j, s, first=False):
                        k = c * PAIRN + j
                        pool.wait_ge(b_copied[s], k + 1)
                        for q in range(Q):
                            if not first:
                                pool.wait_ge(hc_used[s], Q * (k - 1) + q + 1)
                            pool.tensor_tensor(u[s][:, q, :], xdt[:, q, :], b_sb[s][:, :], ALU.mult).then_inc(xs_ready[s], 1)

                    def chunk(c, first=False):
                        pool.wait_ge(xdt_ready, c + 1)
                        states(c, 0, 0, first)
                        states(c, 0, 1, first)
                        with pool.Fori(1, PAIRN) as j:
                            states(c, j, 0)
                            states(c, j, 1)

                    chunk(0, first=True)
                    with pool.Fori(1, CHUNKS) as c:
                        chunk(c)

        with ExitStack() as st:
            cwt = sb(st, "combine", [P, TILES, EXPERTS + 1])
            gate_w = sb(st, "gate_w", [P, HALVES, EXPERTS])
            gu = [sb(st, f"gu{s}", [P, HALVES, 2 * FG * FP]) for s in range(2)]
            down = [sb(st, f"down{s}", [FP, FG, DIM]) for s in range(2)]
            gu_in = [sem(f"expert_in{s}") for s in range(2)]
            gate_in = sem("gate_in")
            iota_f = sb(st, "iota_f", [P, EXPERTS])
            ln_st = ExitStack()
            vec, sca, ten, ln_copied = layernorm("c", ln_st)
            probs = sb(ln_st, "probs", [P, TILES, EXPERTS])
            lmax = sb(ln_st, "lmax", [P, TILES])
            top = sb(ln_st, "top", [P, TILES, 8])
            topi = sb(ln_st, "topi", [P, TILES, 8], U32)
            topf = sb(ln_st, "topf", [P, TILES, 8])
            one = sb(ln_st, "one", [P, TILES, EXPERTS])
            two = sb(ln_st, "two", [P, TILES, EXPERTS])
            logits_done, rstep, expd = sem("logits_done"), sem("router_step"), sem("router_exp")

            def load_expert(sp, e, s):
                sp.dma_start(gu[s][:, :, :], gu_t[bass.ds(e * HALVES * P, HALVES * P), :].rearrange("(h p) f -> p h f", p=P)
                             ).then_inc(gu_in[s], 16)
                sp.dma_start(down[s][:, :, :], down_t[bass.ds(e * FP * FG, FP * FG), :].rearrange("(g p) d -> p g d", p=FP)
                             ).then_inc(gu_in[s], 16)

            with nc.Block() as block:
                @block.sync
                def _(sp):
                    sp.dma_start(gate_w[:, :, :], gate_w_t.rearrange("(h p) e -> p h e", p=P)).then_inc(gate_in, 16)
                    sp.dma_start(iota_f[:, :], iota_in).then_inc(gate_in, 16)
                    load_expert(sp, 0, 0)
                    load_expert(sp, 1, 1)
                    sp.wait_ge(gate_in, 32)
                    for s in range(2):
                        sp.wait_ge(gu_in[s], 32)

                @block.tensor
                def _(pe):
                    ten(pe)
                    pe.wait_ge(gate_in, 32)
                    pe.wait_ge(ln_copied, TILES // 2)
                    for t in range(TILES):
                        for h in range(HALVES):
                            mm = pe.matmul(banks[2][:, t * EXPERTS:(t + 1) * EXPERTS], xnT[:, h, t * P:(t + 1) * P],
                                           gate_w[:, h, :], start=(h == 0), stop=(h == HALVES - 1))
                    mm.then_inc(logits_done, 1)

                @block.scalar
                def _(act):
                    sca(act)
                    act.wait_ge(rstep, 3)
                    act.activation(probs[:, :, :], probs[:, :, :], ACT.Exp).then_inc(expd, 1)

                @block.vector
                def _(dve):
                    vec(dve)
                    step = Count(rstep)

                    def do(instruction):
                        dve.wait_ge(rstep, step.inc(instruction))

                    def wide(a):
                        return a.unsqueeze(2).broadcast_to([P, TILES, EXPERTS])

                    logits = banks[2][:, 0:TILES * EXPERTS].rearrange("p (t e) -> p t e", e=EXPERTS)
                    dve.wait_ge(logits_done, 1)
                    do(dve.tensor_reduce(lmax[:, :], logits, AX.X, ALU.max))
                    do(dve.tensor_tensor(probs[:, :, :], logits, wide(lmax[:, :]), ALU.subtract))
                    do(dve.memset(cwt[:, :, 0:1], 1.0))
                    dve.wait_ge(expd, 1)
                    do(dve.tensor_reduce(lmax[:, :], probs[:, :, :], AX.X, ALU.add))
                    do(dve.reciprocal(lmax[:, :], lmax[:, :]))
                    do(dve.tensor_tensor(probs[:, :, :], probs[:, :, :], wide(lmax[:, :]), ALU.mult))
                    for t in range(TILES):
                        do(dve.max(top[:, t, :], probs[:, t, :]))
                        do(dve.max_index(topi[:, t, :], top[:, t, :], probs[:, t, :]))
                    do(dve.tensor_copy(topf[:, :, :], topi[:, :, :]))
                    do(dve.tensor_tensor(lmax[:, :], top[:, :, 0], top[:, :, 1], ALU.add))
                    do(dve.tensor_scalar(lmax[:, :], lmax[:, :], 1e-8, None, ALU.add))
                    do(dve.reciprocal(lmax[:, :], lmax[:, :]))
                    nums = iota_f[:, :].unsqueeze(1).broadcast_to([P, TILES, EXPERTS])
                    do(dve.tensor_tensor(one[:, :, :], nums, wide(topf[:, :, 0]), ALU.is_equal))
                    do(dve.tensor_tensor(one[:, :, :], one[:, :, :], wide(top[:, :, 0]), ALU.mult))
                    do(dve.tensor_tensor(two[:, :, :], nums, wide(topf[:, :, 1]), ALU.is_equal))
                    do(dve.tensor_tensor(two[:, :, :], two[:, :, :], wide(top[:, :, 1]), ALU.mult))
                    do(dve.tensor_tensor(one[:, :, :], one[:, :, :], two[:, :, :], ALU.add))
                    do(dve.tensor_tensor(cwt[:, :, 1:EXPERTS + 1], one[:, :, :], wide(lmax[:, :]), ALU.mult))
            ln_st.close()

            h_sb = [sb(st, f"h{s}", [FP, FG, CHUNK]) for s in range(2)]
            silu_g = [sb(st, f"silu_g{s}", [FP, CHUNK]) for s in range(2)]
            g_done = [sem(f"gate_done{s}") for s in range(2)]
            g_copied = [sem(f"gate_silu{s}") for s in range(2)]
            h_ready = [sem(f"hidden_ready{s}") for s in range(2)]
            d_done = [sem(f"down_done{s}") for s in range(2)]
            d_added = [sem(f"down_added{s}") for s in range(2)]
            stored = sem("stored")
            GB, UB, DB = banks[0:2], banks[2:4], banks[4:6]
            HG, HT = FG // 2, CHUNK // P // 2

            with nc.Block() as block:
                @block.sync
                def _(sp):
                    with sp.Fori(1, EXPERTS // 2) as k:
                        for s in range(2):
                            sp.wait_ge(d_done[1], HT * CHUNKS * (2 * k - 1 + s))
                            load_expert(sp, 2 * k + s, s)
                    sp.wait_ge(d_done[1], HT * CHUNKS * (EXPERTS - 1))
                    load_expert(sp, EXPERTS, 0)
                    sp.wait_ge(d_added[1], HT * CHUNKS * (EXPERTS + 1))
                    sp.wait_ge(d_added[0], HT * CHUNKS * (EXPERTS + 1))
                    sp.dma_start(out.rearrange("(i p) d -> p i d", p=P), xres[:, :, :]).then_inc(stored, 16)
                    sp.wait_ge(stored, 16)

                def each_expert(engine, run):
                    run(0, 0, first=True)
                    with engine.Fori(0, EXPERTS // 2) as k:
                        run(2 * k + 1, 1)
                        run(2 * k + 2, 0)

                @block.tensor
                def _(pe):
                    def hidden(e, s, c, first):
                        n = e * CHUNKS + c
                        for g in range(FG):
                            b = g % 2
                            if not (first and c == 0 and g < 2):
                                pe.wait_ge(h_ready[b], HG * n + g // 2)
                            for bank, off in ((GB[b], 0), (UB[b], FG * FP)):
                                for h in range(HALVES):
                                    mm = pe.matmul(bank[0:FP, :], gu[s][:, h, off + g * FP:off + (g + 1) * FP],
                                                   xnT[:, h, c * CHUNK:(c + 1) * CHUNK], start=(h == 0), stop=(h == HALVES - 1))
                            mm.then_inc(g_done[b], 1)

                    def project(e, s, c, first):
                        n = e * CHUNKS + c
                        for b in range(2):
                            pe.wait_ge(h_ready[b], HG * n + HG)
                        for t in range(CHUNK // P):
                            b = t % 2
                            if not (first and c == 0 and t < 2):
                                pe.wait_ge(d_added[b], HT * n + t // 2)
                            for g in range(FG):
                                mm = pe.matmul(DB[b][:, 0:DIM], h_sb[c % 2][:, g, t * P:(t + 1) * P], down[s][:, g, :],
                                               start=(g == 0), stop=(g == FG - 1))
                            mm.then_inc(d_done[b], 1)

                    def run(e, s, first=False):
                        pe.wait_ge(gu_in[s], 32 if first else 16 * (e + 2 - s) )
                        for c in range(CHUNKS):
                            hidden(e, s, c, first)
                            if c:
                                project(e, s, c - 1, first)
                        project(e, s, CHUNKS - 1, first)

                    each_expert(pe, run)

                @block.scalar
                def _(act):
                    def run(e, s, first=False):
                        for c in range(CHUNKS):
                            n = e * CHUNKS + c
                            for g in range(FG):
                                b = g % 2
                                act.wait_ge(g_done[b], HG * n + g // 2 + 1)
                                if not (first and c == 0 and g < 2):
                                    act.wait_ge(h_ready[b], HG * n + g // 2)
                                act.activation(silu_g[b][:, :], GB[b][0:FP, :], ACT.Silu).then_inc(g_copied[b], 1)

                    each_expert(act, run)

                @block.vector
                def _(dve):
                    def add(e, s, c):
                        n = e * CHUNKS + c
                        for t in range(CHUNK // P):
                            b = t % 2
                            dve.wait_ge(d_done[b], HT * n + t // 2 + 1)
                            rows = xres[:, c * (CHUNK // P) + t, :]
                            dve.scalar_tensor_tensor(rows, DB[b][:, 0:DIM], cwt[:, c * (CHUNK // P) + t, bass.ds(e, 1)], rows,
                                                     ALU.mult, ALU.add).then_inc(d_added[b], 1)

                    def run(e, s, first=False):
                        for c in range(CHUNKS):
                            n = e * CHUNKS + c
                            for g in range(FG):
                                b = g % 2
                                dve.wait_ge(g_copied[b], HG * n + g // 2 + 1)
                                if g == 0 and not (first and c < 2):
                                    dve.wait_ge(d_done[1], HT * (n - 1))
                                dve.tensor_tensor(h_sb[c % 2][:, g, :], silu_g[b][:, :], UB[b][0:FP, :],
                                                  ALU.mult).then_inc(h_ready[b], 1)
                            if c:
                                add(e, s, c - 1)
                        add(e, s, CHUNKS - 1)

                    each_expert(dve, run)


def kernel(**inputs):
    import concourse.bacc as bacc
    from concourse.bass_utils import run_bass_kernel_spmd

    a = {k: np.asarray(v) for k, v in inputs.items()}
    gate_up = np.concatenate([a["L0_ffn_shared_gate_up"][None], a["L0_ffn_experts_gate_up"]])
    down = np.concatenate([a["L0_ffn_shared_down"][None], a["L0_ffn_experts_down"]])
    gu_t = np.zeros((EXPERTS + 1, DIM, 2, FG * FP), np.float32)
    gu_t[:, :, :, 0:FF] = gate_up.reshape(EXPERTS + 1, 2, FF, DIM).transpose(0, 3, 1, 2)
    down_t = np.zeros((EXPERTS + 1, FG * FP, DIM), np.float32)
    down_t[:, 0:FF, :] = down.transpose(0, 2, 1)
    xp = a["L0_attn_x_proj_w"]
    sel = np.zeros((3, 2 * STATE, 2 * STATE, P // 2), np.uint32)
    for n in range(2 * STATE):
        sel[:, n, n, :] = 0x3F803F80
    laid = {
        "x": a["x"].reshape(TOKENS, DIM),
        "ctx_rows": a["ctx_1024"].reshape(BATCH * CTX, DIM),
        "mask_t": a["mask_BxSxS2_bk0"].transpose(0, 2, 1).reshape(BATCH * CTX, SEQ).view(np.uint32),
        "wq": a["L0_xattn_Wq"], "wk": a["L0_xattn_Wk"], "wv_t": a["L0_xattn_Wv"].T,
        "in_w_t": a["L0_attn_in_proj_w"].T, "conv_w": a["L0_attn_conv_w"], "conv_b": a["L0_attn_conv_b"],
        "bc_w_t": xp[1:].T, "dt_row_t": np.repeat(xp[0:1].T, P, axis=1),
        "a_log": a["L0_attn_A_log"], "d_param": a["L0_attn_D_param"], "dt_w": a["L0_attn_dt_w"], "dt_b": a["L0_attn_dt_b"],
        "out_w_t": a["L0_attn_out_w"].T, "ln_g": a["L0_attn_ln_g"], "ln_b": a["L0_attn_ln_b"],
        "gate_w_t": a["L0_ffn_gate_weight"].T,
        "gu_t": gu_t.reshape((EXPERTS + 1) * DIM, 2 * FG * FP), "down_t": down_t.reshape((EXPERTS + 1) * FG * FP, DIM),
        "ident_in": np.eye(P, dtype=np.float32),
        "sel_in": sel.reshape(6 * STATE, 2 * STATE, P // 2),
        "iota_in": np.tile(np.arange(EXPERTS, dtype=np.float32), (P, 1)),
    }
    nc = bacc.Bacc("TRN2", target_bir_lowering=False, num_devices=1)
    arrays, args = {}, []
    for name, array in laid.items():
        arrays[name] = np.ascontiguousarray(array)
        args.append(nc.dram_tensor(name, array.shape, mybir.dt.from_np(array.dtype), kind="ExternalInput").ap())
    out = nc.dram_tensor("out", (TOKENS, DIM), F32, kind="ExternalOutput").ap()
    build(nc, *args, out)
    result = run_bass_kernel_spmd(nc, [arrays], core_ids=[0])
    return result.results[0]["out"].reshape(BATCH, SEQ, DIM)
```

```python
from contextlib import ExitStack

import numpy as np

import concourse.bass as bass
from concourse import mybir

F32 = mybir.dt.float32
BF16 = mybir.dt.bfloat16
F16 = mybir.dt.float16
U8 = mybir.dt.uint8
U32 = mybir.dt.uint32
ALU = mybir.AluOpType
ACT = mybir.ActivationFunctionType
AX = mybir.AxisListType

P = 128
BATCH, SEQ, DIM = 32, 64, 256
TOKENS = BATCH * SEQ
TILES = TOKENS // P
HALVES = DIM // P
CTX = 1601
KROWS = CTX // P
KREST = CTX - KROWS * P
KT = KROWS + 1
INNER, STATE, TAPS = 512, 16, 4
Q = INNER // P
CHUNK = 512
CHUNKS = TOKENS // CHUNK
CB = CHUNK // SEQ
PADDED = SEQ + TAPS - 1
EXPERTS, TOPK, FF = 8, 2, 938
FP = 118
FG = 8
SLOTS = 256
SLOT_TILES = TOKENS * TOPK // SLOTS + EXPERTS - 1
GU_SCALE, DOWN_SCALE = 16.0, 64.0
EPS = 1e-5


class Count:

    def __init__(self, sem):
        self.sem, self.n = sem, 0

    def inc(self, instruction):
        self.n += 1
        instruction.then_inc(self.sem, 1)
        return self.n


def build(nc, x, ctx_rows, mask_t, wq, wk, wv_t, in_w_t, conv_w, conv_b, bc_w_t, dt_row_t, a_log,
          d_param, dt_w, dt_b, out_w_t, ln_g, ln_b, gate_w_t, gu_t, down_t, ident_in,
          sel_in, consts_t, tri_in, out):
    keep = ExitStack()
    stage_sems = []

    def sem(name):
        stage_sems.append(nc.alloc_semaphore(name=name))
        return stage_sems[-1]

    def end_of_stage():
        nc.clear_and_free_semaphores(stage_sems)
        nc.all_engine_barrier()
        stage_sems.clear()

    def sb(stack, name, shape, dt=F32):
        return stack.enter_context(nc.sbuf_tensor(name, shape, dt))

    with keep:
        xres = sb(keep, "xres", [P, TILES, DIM])
        xnT = sb(keep, "xnT", [P, HALVES, TOKENS])
        ident = sb(keep, "ident", [P, P])
        stats = sb(keep, "stats", [P, TILES, 6])
        meanvar = sb(keep, "meanvar", [P, TILES, 2])
        rstd = sb(keep, "rstd", [P, TILES])
        epsc = sb(keep, "epsc", [P, 1])
        banks = [keep.enter_context(nc.psum_tensor(f"bank{i}", [P, 512], F32)) for i in range(8)]

        ten_rows = [None]
        xs_rows = nc.dram_tensor("xs_rows", (SLOT_TILES * SLOTS, DIM), F32, kind="Internal").ap()
        ys_rows = nc.dram_tensor("ys_rows", (SLOT_TILES * SLOTS, DIM), F32, kind="Internal").ap()

        def layernorm(tag, stack, before=None):
            xn = sb(stack, f"xn_{tag}", [P, TILES, DIM])
            ten_rows[0] = xn
            stats_done, aggr_done = sem(f"stats_done_{tag}"), sem(f"aggr_done_{tag}")
            std_done, rstd_done = sem(f"std_done_{tag}"), sem(f"rstd_done_{tag}")
            xn_ready, turned, bank_free = sem(f"xn_ready_{tag}"), sem(f"turned_{tag}"), sem(f"turn_free_{tag}")

            def vector(dve):
                for i in range(TILES):
                    if before:
                        before(dve, i)
                    dve.bn_stats(stats[:, i, :], xres[:, i, :]).then_inc(stats_done, 1)
                for i in range(TILES):
                    dve.wait_ge(stats_done, i + 1)
                    dve.bn_aggr(meanvar[:, i, :], stats[:, i, :]).then_inc(aggr_done, 1)
                dve.wait_ge(std_done, 1)
                dve.reciprocal(rstd[:, :], rstd[:, :]).then_inc(rstd_done, 1)
                dve.wait_ge(rstd_done, 1)
                for i in range(TILES):
                    dve.tensor_scalar(xn[:, i, :], xres[:, i, :], meanvar[:, i, 0:1], rstd[:, i:i + 1],
                                      ALU.subtract, ALU.mult).then_inc(xn_ready, 1)

            def scalar(act):
                act.wait_ge(aggr_done, TILES)
                act.activation(rstd[:, :], meanvar[:, :, 1], ACT.Sqrt, bias=epsc[:, 0:1]).then_inc(std_done, 1)
                for g in range(TILES // 2):
                    act.wait_ge(turned, g + 1)
                    act.copy(xnT[:, :, g * 2 * P:(g + 1) * 2 * P],
                             banks[g % 2][:, :].rearrange("p (h t) -> p h t", h=HALVES)).then_inc(bank_free, 1)

            def tensor(pe):
                for g in range(TILES // 2):
                    pe.wait_ge(xn_ready, 2 * g + 2)
                    if g >= 2:
                        pe.wait_ge(bank_free, g - 1)
                    for h in range(HALVES):
                        for t in range(2):
                            at = (h * 2 + t) * P
                            last = pe.transpose(banks[g % 2][:, at:at + P],
                                                xn[:, 2 * g + t, h * P:(h + 1) * P], ident[:, :])
                    last.then_inc(turned, 1)

            return vector, scalar, tensor, bank_free

        att = ExitStack()
        with att:
            qkT = sb(att, "qkT", [P, HALVES, TOKENS])
            wv_sb = sb(att, "wv_sb", [P, HALVES, DIM])
            with ExitStack() as first:
                wq_sb = sb(first, "wq_sb", [P, HALVES, DIM])
                wk_sb = sb(first, "wk_sb", [P, HALVES, DIM])
                wqk = sb(first, "wqk", [P, HALVES, DIM])
                x_in = [sem(f"x_in{i}") for i in range(4)]
                zero = sb(first, "zero", [P, DIM])
                zero_set, xs_zeroed = sem("zero_set"), sem("xs_zeroed")
                ident_in_s, w_in, eps_set = sem("ident_loaded"), sem("attention_weights_loaded"), sem("eps_set")
                wqk_done, wqk_copied = sem("wqk_done"), sem("wqk_copied")
                qk_done, qk_copied = sem("qk_done"), sem("qk_copied")
                nx = TILES // 4
                vec, sca, ten, ln_copied = layernorm(
                    "a", first, lambda dve, i: dve.wait_ge(x_in[i // nx], 16) if i % nx == 0 else None)
                with nc.Block() as block:
                    @block.sync
                    def _(sp):
                        for c in range(4):
                            sp.dma_start(xres[:, c * nx:(c + 1) * nx, :],
                                         x[c * nx * P:(c + 1) * nx * P, :].rearrange("(i p) d -> p i d", p=P)
                                         ).then_inc(x_in[c], 16)
                        sp.dma_start(ident[:, :], ident_in).then_inc(ident_in_s, 16)
                        for dst, src in ((wq_sb, wq), (wk_sb, wk), (wv_sb, wv_t)):
                            sp.dma_start(dst[:, :, :], src.rearrange("(h p) d -> p h d", p=P)).then_inc(w_in, 16)
                        sp.wait_ge(zero_set, 1)
                        sp.dma_start(xs_rows.rearrange("(p r) d -> p r d", p=P),
                                     zero[:, :].unsqueeze(1).broadcast_to([P, SLOT_TILES * SLOTS // P, DIM])).then_inc(xs_zeroed, 16)
                        sp.wait_ge(w_in, 48)
                        sp.wait_ge(xs_zeroed, 16)

                    @block.vector
                    def _(dve):
                        dve.memset(epsc[:, :], EPS).then_inc(eps_set, 1)
                        dve.memset(zero[:, :], 0.0).then_inc(zero_set, 1)
                        vec(dve)

                    @block.scalar
                    def _(act):
                        act.wait_ge(eps_set, 1)
                        sca(act)
                        for k in range(HALVES):
                            act.wait_ge(wqk_done, k + 1)
                            act.copy(wqk[:, k, :], banks[2 + k][:, 0:DIM]).then_inc(wqk_copied, 1)
                        for n in range(HALVES * CHUNKS):
                            h, c = n % HALVES, n // HALVES
                            act.wait_ge(qk_done, n + 1)
                            act.copy(qkT[:, h, c * CHUNK:(c + 1) * CHUNK], banks[4 + n % 4][:, :]).then_inc(qk_copied, 1)

                    @block.tensor
                    def _(pe):
                        pe.wait_ge(ident_in_s, 16)
                        pe.wait_ge(w_in, 48)
                        ten(pe)
                        for k in range(HALVES):
                            for h in range(HALVES):
                                mm = pe.matmul(banks[2 + k][:, 0:DIM], wq_sb[:, h, k * P:(k + 1) * P], wk_sb[:, h, :],
                                               start=(h == 0), stop=(h == HALVES - 1))
                            mm.then_inc(wqk_done, 1)
                        pe.wait_ge(wqk_copied, HALVES)
                        pe.wait_ge(ln_copied, TILES // 2)
                        for n in range(HALVES * CHUNKS):
                            h, c = n % HALVES, n // HALVES
                            if n >= 4:
                                pe.wait_ge(qk_copied, n - 3)
                            for k in range(HALVES):
                                mm = pe.matmul(banks[4 + n % 4][:, :], wqk[:, k, h * P:(h + 1) * P],
                                               xnT[:, k, c * CHUNK:(c + 1) * CHUNK],
                                               start=(k == 0), stop=(k == HALVES - 1))
                            mm.then_inc(qk_done, 1)

            with ExitStack() as st:
                ctx_sb = [sb(st, f"ctx{s}", [P, KT, DIM]) for s in range(2)]
                ctxT = [sb(st, f"ctxT{s}", [P, KT * HALVES, P]) for s in range(2)]
                mask_words = [sb(st, f"mask{s}", [P, KT, SEQ // 4], U32) for s in range(2)]
                mask_sb = [m[:, :, :].bitcast(U8) for m in mask_words]
                sc = [sb(st, f"scores{s}", [P, KT, SEQ]) for s in range(2)]
                rowmax = [sb(st, f"rowmax{s}", [P, KT]) for s in range(2)]
                rowsum = [sb(st, f"rowsum{s}", [P, KT]) for s in range(2)]
                rowinv = [sb(st, f"rowinv{s}", [P, KT]) for s in range(2)]
                fill = sb(st, "fill", [P, KT, SEQ])
                pcT = sb(st, "pcT", [P, HALVES, P])
                own_turn = sem("own_turn")
                cleared, fill_set = sem("padding_cleared"), sem("fill_set")
                ctx_in = [sem(f"ctx_in{s}") for s in range(2)]
                turned = [sem(f"ctx_turned{b}") for b in range(2)]
                turn_free = [sem(f"turn_bank_free{b}") for b in range(2)]
                s_done = [sem(f"scores_done{s}") for s in range(2)]
                s_copied = [sem(f"scores_copied{s}") for s in range(2)]
                s_masked = [sem(f"scores_masked{s}") for s in range(2)]
                s_max = [sem(f"scores_max{s}") for s in range(2)]
                s_shift = [sem(f"scores_shifted{s}") for s in range(2)]
                s_exp = [sem(f"scores_exp{s}") for s in range(2)]
                s_sum = [sem(f"scores_sum{s}") for s in range(2)]
                s_inv = [sem(f"scores_inverse{s}") for s in range(2)]
                p_ready = [sem(f"probs_ready{s}") for s in range(2)]
                pv_done, pv_copied = sem("pv_done"), sem("pv_copied")
                o_done, o_added = sem("attention_out_done"), sem("attention_out_added")
                GROUPS = [list(range(g, min(g + 4, KT * HALVES))) for g in range(0, KT * HALVES, 4)]
                NG = len(GROUPS)
                PARTS = [(0, 7), (7, KT)]
                PAIRS = BATCH // 2

                with nc.Block() as block:
                    @block.sync
                    def _(sp):
                        sp.wait_ge(cleared, 4)

                        def load(i, s):
                            base = (2 * i + s) * CTX
                            rows, rest = bass.ds(base, KROWS * P), bass.ds(base + KROWS * P, KREST)
                            sp.dma_start(ctx_sb[s][:, 0:KROWS, :],
                                         ctx_rows[rows, :].rearrange("(p t) d -> p t d", t=KROWS)).then_inc(ctx_in[s], 16)
                            sp.dma_start(mask_words[s][:, 0:KROWS, :],
                                         mask_t[rows, :].rearrange("(p t) q -> p t q", t=KROWS)).then_inc(ctx_in[s], 16)
                            sp.dma_start(ctx_sb[s][0:KREST, KROWS, :], ctx_rows[rest, :]).then_inc(ctx_in[s], 16)
                            sp.dma_start(mask_words[s][0:KREST, KROWS, :], mask_t[rest, :]).then_inc(ctx_in[s], 16)

                        load(0, 0)
                        load(0, 1)
                        with sp.Fori(1, PAIRS) as i:
                            for s in range(2):
                                sp.wait_ge(pv_done, 2 * i + s - 1)
                                sp.wait_ge(s_masked[s], 2 * i)
                                load(i, s)

                    @block.vector
                    def _(dve):
                        for s in range(2):
                            dve.memset(ctx_sb[s][:, KROWS, :], 0.0).then_inc(cleared, 1)
                            dve.memset(mask_words[s][:, KROWS, :], 0).then_inc(cleared, 1)
                        dve.memset(fill[:, :, :], 1e-9).then_inc(fill_set, 1)
                        dve.wait_ge(fill_set, 1)

                        def softmax(i, s):
                            for n, (a, b) in enumerate(PARTS):
                                k = 2 * i + n + 1
                                view = sc[s][:, a:b, :]
                                if n == 0:
                                    dve.wait_ge(ctx_in[s], 64 * i + 64)
                                dve.wait_ge(s_copied[s], k)
                                dve.sem_inc(own_turn, 1)
                                dve.copy_predicated(view, mask_sb[s][:, a:b, :], fill[:, a:b, :]).then_inc(s_masked[s], 1)
                                dve.wait_ge(s_masked[s], k)
                                dve.tensor_reduce(rowmax[s][:, a:b], view, AX.X, ALU.max).then_inc(s_max[s], 1)
                            for n, (a, b) in enumerate(PARTS):
                                k = 2 * i + n + 1
                                view = sc[s][:, a:b, :]
                                dve.wait_ge(s_exp[s], k)
                                dve.tensor_reduce(rowsum[s][:, a:b], view, AX.X, ALU.add).then_inc(s_sum[s], 1)
                                dve.wait_ge(s_sum[s], k)
                                dve.reciprocal(rowinv[s][:, a:b], rowsum[s][:, a:b]).then_inc(s_inv[s], 1)
                                dve.wait_ge(s_inv[s], k)
                                dve.tensor_tensor(view, view, rowinv[s][:, a:b].unsqueeze(2).broadcast_to([P, b - a, SEQ]),
                                                  ALU.mult).then_inc(p_ready[s], 1)

                        def add_out(i):
                            dve.wait_ge(o_done, i + 1)
                            dve.tensor_tensor(xres[:, bass.ds(i, 1), :].rearrange("p o d -> p (o d)"),
                                              xres[:, bass.ds(i, 1), :].rearrange("p o d -> p (o d)"),
                                              banks[7][:, 0:DIM], ALU.add).then_inc(o_added, 1)

                        softmax(0, 0)
                        with dve.Fori(0, PAIRS - 1) as i:
                            softmax(i, 1)
                            softmax(i + 1, 0)
                            add_out(i)
                        softmax(PAIRS - 1, 1)
                        add_out(PAIRS - 1)

                    @block.gpsimd
                    def _(pool):
                        def shift(i, s):
                            for n, (a, b) in enumerate(PARTS):
                                k = 2 * i + n + 1
                                view = sc[s][:, a:b, :]
                                pool.wait_ge(s_max[s], k)
                                pool.tensor_tensor(view, view, rowmax[s][:, a:b].unsqueeze(2).broadcast_to([P, b - a, SEQ]),
                                                   ALU.subtract).then_inc(s_shift[s], 1)

                        with pool.Fori(0, PAIRS) as i:
                            shift(i, 0)
                            shift(i, 1)

                    @block.scalar
                    def _(act):
                        def turn_out(i, s):
                            for g, blocks in enumerate(GROUPS):
                                n = s * NG + g
                                act.wait_ge(turned[n % 2], NG * i + n // 2 + 1)
                                act.copy(ctxT[s][:, blocks[0]:blocks[-1] + 1, :],
                                         banks[n % 2][:, 0:len(blocks) * P].rearrange("p (b k) -> p b k", k=P)
                                         ).then_inc(turn_free[n % 2], 1)

                        def copy_scores(i, s, first=False):
                            for n, (a, b) in enumerate(PARTS):
                                k = 2 * i + n + 1
                                act.wait_ge(s_done[s], k)
                                if n == 0 and not first:
                                    act.wait_ge(pv_done, 2 * i + s - 1)
                                act.mul(sc[s][:, a:b, :], banks[2 + 2 * s + n][:, 0:(b - a) * SEQ]
                                        .rearrange("p (t q) -> p t q", q=SEQ), DIM ** -0.5).then_inc(s_copied[s], 1)

                        def exps(i, s):
                            for n, (a, b) in enumerate(PARTS):
                                k = 2 * i + n + 1
                                view = sc[s][:, a:b, :]
                                act.wait_ge(s_shift[s], k)
                                act.activation(view, view, ACT.Exp).then_inc(s_exp[s], 1)

                        def pv_out(i, s, first=False):
                            act.wait_ge(pv_done, 2 * i + s + 1)
                            if s == 0 and not first:
                                act.wait_ge(o_done, i)
                            act.copy(pcT[:, :, s * SEQ:(s + 1) * SEQ],
                                     banks[6][:, 0:HALVES * SEQ].rearrange("p (h q) -> p h q", q=SEQ)
                                     ).then_inc(pv_copied, 1)

                        def pair(i, first=False, last=False):
                            exps(i, 0)
                            turn_out(i, 1)
                            copy_scores(i, 1, first)
                            pv_out(i, 0, first)
                            exps(i, 1)
                            if not last:
                                turn_out(i + 1, 0)
                                copy_scores(i + 1, 0)
                            pv_out(i, 1)

                        turn_out(0, 0)
                        copy_scores(0, 0, first=True)
                        pair(0, first=True)
                        with act.Fori(1, PAIRS - 1) as i:
                            pair(i)
                        pair(PAIRS - 1, last=True)

                    @block.tensor
                    def _(pe):
                        def turn(i, s, first=False):
                            pe.wait_ge(ctx_in[s], 64 * i + 64)
                            for g, blocks in enumerate(GROUPS):
                                n = s * NG + g
                                if not (first and n < 2):
                                    pe.wait_ge(turn_free[n % 2], NG * i + n // 2)
                                for at, blk in enumerate(blocks):
                                    t, h = blk // HALVES, blk % HALVES
                                    mm = pe.transpose(banks[n % 2][:, at * P:(at + 1) * P],
                                                      ctx_sb[s][:, t, h * P:(h + 1) * P], ident[:, :])
                                mm.then_inc(turned[n % 2], 1)

                        def scores(i, s, first=False):
                            for n in (s * NG + NG - 1, s * NG + NG - 2):
                                pe.wait_ge(turn_free[n % 2], NG * i + n // 2 + 1)
                            if not first:
                                pe.wait_ge(s_copied[s], 2 * i)
                            for n, (a, b) in enumerate(PARTS):
                                for t in range(a, b):
                                    for h in range(HALVES):
                                        mm = pe.matmul(banks[2 + 2 * s + n][:, (t - a) * SEQ:(t - a + 1) * SEQ],
                                                       ctxT[s][:, t * HALVES + h, :],
                                                       qkT[:, h, bass.ds((2 * i + s) * SEQ, SEQ)],
                                                       start=(h == 0), stop=(h == HALVES - 1))
                                mm.then_inc(s_done[s], 1)

                        def weigh(i, s, first=False):
                            pe.wait_ge(p_ready[s], 2 * i + 2)
                            if not (first and s == 0):
                                pe.wait_ge(pv_copied, 2 * i + s)
                            for h in range(HALVES):
                                for t in range(KT):
                                    mm = pe.matmul(banks[6][:, h * SEQ:(h + 1) * SEQ], ctx_sb[s][:, t, h * P:(h + 1) * P],
                                                   sc[s][:, t, :], start=(t == 0), stop=(t == KT - 1))
                            mm.then_inc(pv_done, 1)

                        def project(i, first=False):
                            pe.wait_ge(pv_copied, 2 * i + 2)
                            if not first:
                                pe.wait_ge(o_added, i)
                            for h in range(HALVES):
                                mm = pe.matmul(banks[7][:, 0:DIM], pcT[:, h, :], wv_sb[:, h, :],
                                               start=(h == 0), stop=(h == HALVES - 1))
                            mm.then_inc(o_done, 1)

                        def pair(i, first=False, last=False):
                            turn(i, 1, first)
                            scores(i, 1, first)
                            weigh(i, 0, first)
                            if not last:
                                turn(i + 1, 0)
                                scores(i + 1, 0)
                            weigh(i, 1)
                            project(i, first)

                        pe.wait_ge(fill_set, 1)
                        turn(0, 0, first=True)
                        scores(0, 0, first=True)
                        pair(0, first=True)
                        with pe.Fori(1, PAIRS - 1) as i:
                            pair(i)
                        pair(PAIRS - 1, last=True)


        end_of_stage()

        with ExitStack() as st:
            in_w = sb(st, "in_w", [P, HALVES, 2 * INNER])
            cw = sb(st, "cw", [P, Q, TAPS])
            cb = sb(st, "cb", [P, Q])
            bc_w = sb(st, "bc_w", [P, Q, 2 * STATE])
            dt_row = sb(st, "dt_row", [P, Q, P])
            a_neg = sb(st, "a_neg", [P, Q, STATE])
            dpar = sb(st, "dpar", [P, Q])
            dtw = sb(st, "dtw", [P, Q])
            dtb = sb(st, "dtb", [P, Q])
            out_w = sb(st, "out_w", [P, Q, DIM])
            lng = sb(st, "lng", [P, Q])
            lnb = sb(st, "lnb", [P, Q])
            d_diag = sb(st, "d_diag", [P, Q, P])
            mean_w = sb(st, "mean_w", [P, P])
            sel = sb(st, "sel", [6 * STATE, 2 * STATE, P // 2], U32)
            weights_in, small_set, a_exp, a_done = sem("mamba_weights_in"), sem("small_set"), sem("a_exp"), sem("a_done")
            ln_st = ExitStack()
            vec, sca, ten, _ = layernorm("b", ln_st)
            loads = [(in_w, in_w_t.rearrange("(h p) e -> p h e", p=P)),
                     (cw, conv_w.rearrange("(q p) k -> p q k", p=P)), (cb, conv_b.rearrange("(q p) -> p q", p=P)),
                     (bc_w, bc_w_t.rearrange("(q p) n -> p q n", p=P)),
                     (dt_row, dt_row_t.rearrange("(q p) n -> p q n", p=P)),
                     (a_neg, a_log.rearrange("(q p) n -> p q n", p=P)), (dpar, d_param.rearrange("(q p) -> p q", p=P)),
                     (dtw, dt_w.rearrange("(q p) o -> p (q o)", p=P)), (dtb, dt_b.rearrange("(q p) -> p q", p=P)),
                     (out_w, out_w_t.rearrange("(q p) d -> p q d", p=P)),
                     (lng, ln_g.rearrange("(q p) -> p q", p=P)), (lnb, ln_b.rearrange("(q p) -> p q", p=P)),
                     (sel, sel_in)]
            with nc.Block() as block:
                @block.sync
                def _(sp):
                    for dst, src in loads:
                        with nc.allow_non_contiguous_dma("a few small vectors"):
                            sp.dma_start(dst[tuple([slice(None)] * len(dst.shape))], src).then_inc(weights_in, 16)
                    sp.wait_ge(weights_in, 16 * len(loads))

                @block.vector
                def _(dve):
                    vec(dve)
                    dve.memset(mean_w[:, :], 1.0 / INNER).then_inc(small_set, 1)
                    dve.wait_ge(weights_in, 16 * len(loads))
                    for q in range(Q):
                        dve.tensor_scalar(d_diag[:, q, :], ident[:, :], dpar[:, q:q + 1], None, ALU.mult).then_inc(small_set, 1)

                @block.scalar
                def _(act):
                    sca(act)
                    act.wait_ge(weights_in, 16 * len(loads))
                    act.activation(a_neg[:, :, :], a_neg[:, :, :], ACT.Exp).then_inc(a_exp, 1)
                    act.wait_ge(a_exp, 1)
                    act.mul(a_neg[:, :, :], a_neg[:, :, :], -1.0).then_inc(a_done, 1)

                @block.tensor
                def _(pe):
                    ten(pe)
            ln_st.close()

            xpad = sb(st, "xpad", [P, Q, CB, PADDED])
            xb = sb(st, "xb", [P, Q, CHUNK])
            sz = sb(st, "sz", [P, Q, CHUNK])
            dt = sb(st, "dt", [P, Q, CHUNK])
            xdt = sb(st, "xdt", [P, Q, CHUNK])
            tmp = sb(st, "tmp", [P, Q, CHUNK])
            tmp2 = sb(st, "tmp2", [P, Q, CHUNK])
            tmp3 = sb(st, "tmp3", [P, Q, CHUNK])
            small = sb(st, "small", [P, Q, CHUNK], U8)
            bc_parts = sb(st, "bc_parts", [6 * STATE, CHUNK], BF16)
            bc_mid = sb(st, "bc_mid", [2 * STATE, CHUNK], BF16)
            bc_rest = sb(st, "bc_rest", [2 * STATE, CHUNK])
            b_sb = [sb(st, f"b_sb{s}", [P, CHUNK]) for s in range(2)]
            dA = [sb(st, f"dA{s}", [P, Q, CB, SEQ]) for s in range(2)]
            u = [sb(st, f"u{s}", [P, Q, CHUNK]) for s in range(2)]
            sel16 = sel[:, :, :].bitcast(BF16)
            yc, sq = tmp, tmp2
            BB, CC, YY = banks[0:2], banks[2:4], banks[4:8]

            dt_turn = sem("dt_turn")
            padded = sem("padding_zeroed")
            in_done = [sem(f"in_proj_done{b}") for b in range(4)]
            in_copied = [sem(f"in_proj_copied{b}") for b in range(4)]
            conv_part, conv_done = sem("conv_part"), sem("conv_done")
            xb_ready = sem("xb_ready")
            dt_done, bc_done = sem("dt_product_done"), sem("bc_product_done")
            dt_abs, dt_z, dt_log, dt_relu = sem("dt_abs"), sem("dt_z"), sem("dt_log"), sem("dt_relu")
            dt_step, dt_ready, xdt_ready = sem("dt_step"), sem("dt_ready"), sem("xdt_ready")
            part_step, parts_ready = sem("bc_part_step"), sem("bc_parts_ready")
            b_done = [sem(f"b_spread{s}") for s in range(2)]
            c_done = [sem(f"c_spread{s}") for s in range(2)]
            b_copied = [sem(f"b_copied{s}") for s in range(2)]
            dA_ready = [sem(f"dA_ready{s}") for s in range(2)]
            xs_ready = [sem(f"xs_ready{s}") for s in range(2)]
            h_ready = [sem(f"h_ready{s}") for s in range(2)]
            hc_ready = [sem(f"hc_ready{s}") for s in range(2)]
            hc_used = [sem(f"hc_used{s}") for s in range(2)]
            y_copied = sem("y_copied")
            mean_done, yc_ready, sq_ready, var_done = sem("mean_done"), sem("yc_ready"), sem("sq_ready"), sem("var_done")
            ystd, yrstd, ynorm, yaff, yfin = sem("y_std"), sem("y_rstd"), sem("y_norm"), sem("y_affine"), sem("y_final")
            op_done, op_added = sem("out_proj_done"), sem("out_proj_added")
            PAIRN = STATE // 2

            with nc.Block() as block:
                @block.tensor
                def _(pe):
                    def spread(c, j, s, first_chunk=False):
                        k = c * PAIRN + j
                        free = not (first_chunk and isinstance(j, int) and j == 0)
                        if free:
                            pe.wait_ge(hc_ready[s], Q * k)
                            pe.wait_ge(b_copied[s], k)
                        n = 2 * j + s
                        pe.matmul(BB[s][:, :], sel16[:, bass.ds(n, 1), :].rearrange("k o p -> k (o p)"), bc_parts[:, :],
                                  start=True, stop=True).then_inc(b_done[s], 1)
                        pe.matmul(CC[s][:, :], sel16[:, bass.ds(n + STATE, 1), :].rearrange("k o p -> k (o p)"),
                                  bc_parts[:, :], start=True, stop=True).then_inc(c_done[s], 1)

                    def gather(c, j, s, last=False):
                        k = c * PAIRN + j
                        for q in range(Q):
                            pe.wait_ge(hc_ready[s], Q * k + q + 1)
                            pe.matmul(YY[q][:, :], ident[:, :], u[s][:, q, :], start=False, stop=last,
                                      skip_group_check=True).then_inc(hc_used[s], 1)

                    def chunk(c, first=False):
                        for k in range(2 * Q):
                            b = k % 4
                            if k >= 4:
                                pe.wait_ge(in_copied[b], 2 * c + 1)
                            elif not first:
                                if k == 0:
                                    pe.wait_ge(op_added, 4 * c)
                                    pe.wait_ge(yrstd, c)
                            for h in range(HALVES):
                                mm = pe.matmul(banks[b][:, :], in_w[:, h, k * P:(k + 1) * P],
                                               xnT[:, h, bass.ds(c * CHUNK, CHUNK)], start=(h == 0), stop=(h == HALVES - 1))
                            mm.then_inc(in_done[b], 1)
                        pe.wait_ge(in_copied[0], 2 * c + 2)
                        pe.wait_ge(in_copied[1], 2 * c + 2)
                        for q in range(Q):
                            pe.wait_ge(xb_ready, Q * c + q + 1)
                            mm = pe.matmul(banks[0][:, :], dt_row[:, q, :], xb[:, q, :], start=(q == 0), stop=(q == Q - 1))
                        mm.then_inc(dt_done, 1)
                        for q in range(Q):
                            mm = pe.matmul(banks[1][0:2 * STATE, :], bc_w[:, q, :], xb[:, q, :], start=(q == 0), stop=(q == Q - 1))
                        mm.then_inc(bc_done, 1)
                        if not first:
                            pe.wait_ge(y_copied, Q * c)
                        for q in range(Q):
                            pe.matmul(YY[q][:, :], d_diag[:, q, :], xb[:, q, :], start=True, stop=False,
                                      skip_group_check=True)
                        pe.wait_ge(parts_ready, c + 1)
                        pe.wait_ge(dt_relu, Q * c + Q)
                        pe.wait_ge(in_copied[2], 2 * c + 2)
                        pe.wait_ge(in_copied[3], 2 * c + 2)
                        spread(c, 0, 0, first)
                        spread(c, 0, 1, first)
                        with pe.Fori(0, PAIRN - 1) as j:
                            gather(c, j, 0)
                            spread(c, j + 1, 0)
                            gather(c, j, 1)
                            spread(c, j + 1, 1)
                        gather(c, PAIRN - 1, 0)
                        gather(c, PAIRN - 1, 1, last=True)
                        for q in range(Q):
                            pe.wait_ge(y_copied, Q * c + q + 1)
                            mm = pe.matmul(banks[0][:, :], mean_w[:, :], yc[:, q, :], start=(q == 0), stop=(q == Q - 1))
                        mm.then_inc(mean_done, 1)
                        for q in range(Q):
                            pe.wait_ge(sq_ready, Q * c + q + 1)
                            mm = pe.matmul(banks[1][:, :], mean_w[:, :], sq[:, q, :], start=(q == 0), stop=(q == Q - 1))
                        mm.then_inc(var_done, 1)
                        pe.wait_ge(yfin, Q * c + Q)
                        for t in range(CHUNK // P):
                            if t >= 2:
                                pe.wait_ge(op_added, 4 * c + t - 1)
                            for q in range(Q):
                                mm = pe.matmul(banks[2 + t % 2][:, 0:DIM], yc[:, q, t * P:(t + 1) * P], out_w[:, q, :],
                                               start=(q == 0), stop=(q == Q - 1))
                            mm.then_inc(op_done, 1)

                    pe.wait_ge(small_set, 1 + Q)
                    chunk(0, first=True)
                    with pe.Fori(1, CHUNKS) as c:
                        chunk(c)

                @block.scalar
                def _(act):
                    def states(c, j, s, first=False):
                        k = c * PAIRN + j
                        n = 2 * j + s
                        act.wait_ge(b_done[s], k + 1)
                        if not first:
                            act.wait_ge(xs_ready[s], Q * k)
                        act.copy(b_sb[s][:, :], BB[s][:, :]).then_inc(b_copied[s], 1)
                        for q in range(Q):
                            if q == 0 and not first:
                                act.wait_ge(h_ready[s], Q * k)
                            act.activation(dA[s][:, q, :, 1:SEQ], dt[:, q, :].rearrange("p (b l) -> p b l", l=SEQ)[:, :, 1:SEQ],
                                           ACT.Exp, scale=a_neg[:, q, bass.ds(n, 1)]).then_inc(dA_ready[s], 1)

                    def chunk(c, first=False):
                        for k in range(2 * Q):
                            b, q = k % 4, k % Q
                            act.wait_ge(in_done[b], 2 * c + k // 4 + 1)
                            if k < Q:
                                if k == 0 and not first:
                                    act.wait_ge(conv_done, Q * c)
                                act.copy(xpad[:, q, :, TAPS - 1:PADDED],
                                         banks[b][:, :].rearrange("p (b l) -> p b l", l=SEQ)).then_inc(in_copied[b], 1)
                            else:
                                if q == 0 and not first:
                                    act.wait_ge(yfin, Q * c)
                                act.activation(sz[:, q, :], banks[b][:, :], ACT.Silu).then_inc(in_copied[b], 1)
                        for q in range(Q):
                            act.wait_ge(conv_done, Q * c + q + 1)
                            act.activation(xb[:, q, :], xb[:, q, :], ACT.Silu).then_inc(xb_ready, 1)
                        act.wait_ge(dt_done, c + 1)
                        if not first:
                            act.wait_ge(op_done, 4 * c)
                            act.wait_ge(var_done, c)
                        for q in range(Q):
                            act.activation(tmp[:, q, :], banks[0][:, :], ACT.Abs, bias=dtb[:, q:q + 1],
                                           scale=dtw[:, q:q + 1]).then_inc(dt_abs, 1)
                            act.activation(dt[:, q, :], banks[0][:, :], ACT.Relu, bias=dtb[:, q:q + 1],
                                           scale=dtw[:, q:q + 1]).then_inc(dt_relu, 1)
                        act.wait_ge(dt_abs, Q * c + Q)
                        act.activation(tmp[:, :, :], tmp[:, :, :], ACT.Exp, scale=-1.0).then_inc(dt_z, 1)
                        act.wait_ge(dt_z, c + 1)
                        act.activation(tmp2[:, :, :], tmp[:, :, :], ACT.Ln, bias=1.0).then_inc(dt_log, 1)
                        act.wait_ge(dt_ready, c + 1)
                        states(c, 0, 0, first)
                        states(c, 0, 1, first)
                        with act.Fori(1, PAIRN) as j:
                            states(c, j, 0)
                            states(c, j, 1)
                        for q in range(Q):
                            act.wait_ge(hc_used[1], Q * PAIRN * c + Q * (PAIRN - 1) + q + 1)
                            act.copy(yc[:, q, :], YY[q][:, :]).then_inc(y_copied, 1)
                        for q in range(Q):
                            act.wait_ge(yc_ready, Q * c + q + 1)
                            act.activation(sq[:, q, :], yc[:, q, :], ACT.Square).then_inc(sq_ready, 1)
                        act.wait_ge(var_done, c + 1)
                        act.activation(tmp3[:, 0, :], banks[1][:, :], ACT.Sqrt, bias=epsc[:, 0:1]).then_inc(ystd, 1)
                        for q in range(Q):
                            act.wait_ge(ynorm, Q * c + q + 1)
                            act.activation(yc[:, q, :], yc[:, q, :], ACT.Identity, bias=lnb[:, q:q + 1],
                                           scale=lng[:, q:q + 1]).then_inc(yaff, 1)

                    act.wait_ge(padded, 3)
                    chunk(0, first=True)
                    with act.Fori(1, CHUNKS) as c:
                        chunk(c)

                @block.vector
                def _(dve):
                    dve.memset(xpad[:, :, :, 0:TAPS - 1], 0.0).then_inc(padded, 1)
                    for s in range(2):
                        dve.memset(dA[s][:, :, :, 0:1], 0.0).then_inc(padded, 1)

                    def states(c, j, s):
                        k = c * PAIRN + j
                        for q in range(Q):
                            dve.wait_ge(dA_ready[s], Q * k + q + 1)
                            dve.wait_ge(xs_ready[s], Q * k + q + 1)
                            dve.tensor_tensor_scan(u[s][:, q, :], dA[s][:, q, :, :].rearrange("p b l -> p (b l)"),
                                                   u[s][:, q, :], 0.0, ALU.mult, ALU.add).then_inc(h_ready[s], 1)
                        dve.wait_ge(c_done[s], k + 1)
                        for q in range(Q):
                            dve.wait_ge(h_ready[s], Q * k + q + 1)
                            dve.tensor_tensor(u[s][:, q, :], u[s][:, q, :], CC[s][:, :], ALU.mult).then_inc(hc_ready[s], 1)

                    def chunk(c, first=False):
                        for q in range(Q):
                            dve.wait_ge(in_copied[q], 2 * c + 1)
                            row = xb[:, q, :].rearrange("p (b l) -> p b l", l=SEQ)
                            if q == 0 and not first:
                                dve.wait_ge(hc_used[1], Q * PAIRN * c)
                            dve.tensor_scalar(row, xpad[:, q, :, 0:SEQ], cw[:, q, 0:1], cb[:, q:q + 1],
                                              ALU.mult, ALU.add).then_inc(conv_part, 1)
                            for k in range(1, TAPS):
                                dve.wait_ge(conv_part, (Q * c + q) * (TAPS - 1) + k)
                                dve.scalar_tensor_tensor(row, xpad[:, q, :, k:k + SEQ], cw[:, q, k:k + 1], row,
                                                         ALU.mult, ALU.add).then_inc(conv_part if k < TAPS - 1 else conv_done, 1)
                        dve.wait_ge(bc_done, c + 1)
                        bank = banks[1][0:2 * STATE, :]
                        hi, mid, lo = (bc_parts[2 * STATE * k:2 * STATE * (k + 1), :] for k in range(3))
                        base = 5 * c
                        dve.tensor_copy(hi, bank).then_inc(part_step, 1)
                        dve.wait_ge(part_step, base + 1)
                        dve.tensor_tensor(bc_rest[:, :], bank, hi, ALU.subtract).then_inc(part_step, 1)
                        dve.wait_ge(part_step, base + 2)
                        dve.tensor_copy(bc_mid[:, :], bc_rest[:, :]).then_inc(part_step, 1)
                        dve.wait_ge(part_step, base + 3)
                        dve.tensor_copy(mid, bc_mid[:, :]).then_inc(part_step, 1)
                        dve.tensor_tensor(bc_rest[:, :], bc_rest[:, :], bc_mid[:, :], ALU.subtract).then_inc(part_step, 1)
                        dve.wait_ge(part_step, base + 5)
                        dve.tensor_copy(lo, bc_rest[:, :]).then_inc(parts_ready, 1)
                        dve.wait_ge(dt_log, c + 1)
                        z, t3 = tmp[:, :, :], tmp3[:, :, :]
                        steps = 7 * c
                        dve.tensor_scalar(small[:, :, :], z, 1.0 / 32, None, ALU.is_lt).then_inc(dt_step, 1)
                        dve.tensor_scalar(t3, z, 0.2, -0.25, ALU.mult, ALU.add).then_inc(dt_step, 1)
                        dve.wait_ge(dt_step, steps + 2)
                        dve.tensor_tensor(t3, t3, z, ALU.mult).then_inc(dt_step, 1)
                        for n, coefficient in enumerate((1.0 / 3, -0.5, 1.0)):
                            dve.wait_ge(dt_step, steps + 3 + n)
                            dve.scalar_tensor_tensor(t3, t3, coefficient, z, ALU.add, ALU.mult).then_inc(dt_step, 1)
                        dve.wait_ge(dt_step, steps + 6)
                        dve.sem_inc(dt_turn, 1)
                        dve.copy_predicated(tmp2[:, :, :], small[:, :, :], t3).then_inc(dt_step, 1)
                        dve.wait_ge(dt_step, steps + 7)
                        dve.wait_ge(dt_relu, Q * c + Q)
                        dve.tensor_tensor(dt[:, :, :], dt[:, :, :], tmp2[:, :, :], ALU.add).then_inc(dt_ready, 1)
                        dve.wait_ge(dt_ready, c + 1)
                        dve.tensor_tensor(xdt[:, :, :], xb[:, :, :], dt[:, :, :], ALU.mult).then_inc(xdt_ready, 1)
                        with dve.Fori(0, PAIRN) as j:
                            states(c, j, 0)
                            states(c, j, 1)
                        dve.wait_ge(mean_done, c + 1)
                        for q in range(Q):
                            dve.tensor_tensor(yc[:, q, :], yc[:, q, :], banks[0][:, :], ALU.subtract).then_inc(yc_ready, 1)
                        dve.wait_ge(ystd, c + 1)
                        dve.reciprocal(tmp3[:, 0, :], tmp3[:, 0, :]).then_inc(yrstd, 1)
                        dve.wait_ge(yrstd, c + 1)
                        dve.wait_ge(sq_ready, Q * c + Q)
                        for q in range(Q):
                            dve.tensor_tensor(yc[:, q, :], yc[:, q, :], tmp3[:, 0, :], ALU.mult).then_inc(ynorm, 1)
                        for q in range(Q):
                            dve.wait_ge(yaff, Q * c + q + 1)
                            dve.tensor_tensor(yc[:, q, :], yc[:, q, :], sz[:, q, :], ALU.mult).then_inc(yfin, 1)
                        for t in range(CHUNK // P):
                            dve.wait_ge(op_done, 4 * c + t + 1)
                            rows = xres[:, bass.ds(4 * c + t, 1), :].rearrange("p o d -> p (o d)")
                            dve.tensor_tensor(rows, rows, banks[2 + t % 2][:, 0:DIM], ALU.add).then_inc(op_added, 1)

                    chunk(0, first=True)
                    with dve.Fori(1, CHUNKS) as c:
                        chunk(c)

                @block.gpsimd
                def _(pool):
                    def states(c, j, s, first=False):
                        k = c * PAIRN + j
                        pool.wait_ge(b_copied[s], k + 1)
                        for q in range(Q):
                            if not first:
                                pool.wait_ge(hc_used[s], Q * (k - 1) + q + 1)
                            pool.tensor_tensor(u[s][:, q, :], xdt[:, q, :], b_sb[s][:, :], ALU.mult).then_inc(xs_ready[s], 1)

                    def chunk(c, first=False):
                        pool.wait_ge(xdt_ready, c + 1)
                        states(c, 0, 0, first)
                        states(c, 0, 1, first)
                        with pool.Fori(1, PAIRN) as j:
                            states(c, j, 0)
                            states(c, j, 1)

                    chunk(0, first=True)
                    with pool.Fori(1, CHUNKS) as c:
                        chunk(c)

        end_of_stage()

        with ExitStack() as st:
            X = EXPERTS
            gate_w = sb(st, "gate_w", [P, HALVES, X])
            consts = sb(st, "consts", [P, 2 * SLOT_TILES + X])
            tri = sb(st, "tri", [P, P])
            ones = sb(st, "ones", [P, P])
            pos_u = [sb(st, f"pos{k}", [P, TILES], U32) for k in range(TOPK)]
            share = [sb(st, f"share{k}", [P, TILES]) for k in range(TOPK)]
            eid_u = sb(st, "eid_u", [P, SLOT_TILES], U32)
            xh = [sb(st, f"xn_{n}", [P, HALVES, TOKENS], F16) for n in ("hi", "lo")]
            raw = [sb(st, f"raw_gu{h}", [P, 2 * FG * FP]) for h in range(HALVES)] + [sb(st, "raw_down", [FP, FG, DIM])]
            gu = [[sb(st, f"gu_{n}{w}", [P, HALVES, 2 * FG * FP], F16) for n in ("hi", "lo")] for w in range(2)]
            down = [[sb(st, f"down_{n}{w}", [FP, FG, DIM], F16) for n in ("hi", "lo")] for w in range(2)]
            consts_in, xsplit = sem("router_constants_in"), sem("xn_split")
            positions, eids_ready, one_set = sem("slots_known"), sem("slot_experts_known"), sem("ones_set")
            raw_in = [sem(f"raw_in{k}") for k in range(3)]
            w_hi = [sem(f"weights_hi{k}") for k in range(3)]
            w_lo = [sem(f"weights_lo{k}") for k in range(3)]
            scattered = sem("rows_scattered")
            small_st = ExitStack()
            vec, sca, ten, ln_copied = layernorm("c", small_st)
            xn = ten_rows[0]
            wide_ = [P, TILES, X]
            probs = sb(small_st, "probs", wide_)
            hot = [sb(small_st, f"hot{k}", wide_) for k in range(TOPK)]
            work = sb(small_st, "work", wide_)
            chosen = sb(small_st, "chosen", wide_)
            slot_of = sb(small_st, "slot_of", wide_)
            lmax = sb(small_st, "lmax", [P, TILES])
            top = sb(small_st, "top", [P, TILES, 8])
            topi = sb(small_st, "topi", [P, TILES, 8], U32)
            topf = sb(small_st, "topf", [P, TILES, 8])
            shifted = sb(small_st, "shifted", [P, X, TILES])
            carry = sb(small_st, "carry", [P, X, TILES])
            before = sb(small_st, "before", [P, X, TILES])
            count = sb(small_st, "count", [P, X])
            cmp = sb(small_st, "cmp", [P, SLOT_TILES, X])
            tiles_of = sb(small_st, "tiles_of", [P, X])
            tiles_sh = sb(small_st, "tiles_sh", [P, X])
            first_tile = sb(small_st, "first_tile", [P, X])
            end_tile = sb(small_st, "end_tile", [P, X])
            eid = sb(small_st, "eid", [P, SLOT_TILES])
            ones_x = sb(small_st, "ones_x", [P, X])
            logits_done, rstep, expd = sem("logits_done"), sem("router_step"), sem("router_exp")
            chosen_ready, ranks_done = sem("chosen_ready"), sem("ranks_done")
            BIG = 2 * FG * FP

            def load_raw(sp, k, row):
                if k < HALVES:
                    sp.dma_start(raw[k][:, :], gu_t[bass.ds(row * DIM + k * P, P), :]).then_inc(raw_in[k], 16)
                else:
                    sp.dma_start(raw[2][:, :, :], down_t[bass.ds(row * FG * FP, FG * FP), :]
                                 .rearrange("(g p) d -> p g d", p=FP)).then_inc(raw_in[2], 16)

            with nc.Block() as block:
                @block.sync
                def _(sp):
                    sp.dma_start(gate_w[:, :, :], gate_w_t.rearrange("(h p) e -> p h e", p=P)).then_inc(consts_in, 16)
                    sp.dma_start(consts[:, :], consts_t).then_inc(consts_in, 16)
                    sp.dma_start(tri[:, :], tri_in).then_inc(consts_in, 16)
                    for k in range(3):
                        load_raw(sp, k, 0)
                    for k in range(3):
                        sp.wait_ge(raw_in[k], 16)
                    sp.wait_ge(consts_in, 48)

                @block.gpsimd
                def _(pool):
                    pool.wait_ge(positions, 1)
                    for t in range(TILES):
                        for k in range(TOPK):
                            pool.indirect_dma_start(out=xs_rows, out_offset=bass.IndirectOffsetOnAxis(ap=pos_u[k][:, t:t + 1], axis=0),
                                                    in_=xn[:, t, :], in_offset=None).then_inc(scattered, 16)
                    pool.wait_ge(scattered, 16 * TILES * TOPK)

                @block.tensor
                def _(pe):
                    ten(pe)
                    pe.wait_ge(consts_in, 48)
                    pe.wait_ge(ln_copied, TILES // 2)
                    for t in range(TILES):
                        for h in range(HALVES):
                            mm = pe.matmul(banks[2][:, t * X:(t + 1) * X], xnT[:, h, t * P:(t + 1) * P],
                                           gate_w[:, h, :], start=(h == 0), stop=(h == HALVES - 1))
                    mm.then_inc(logits_done, 1)
                    pe.wait_ge(chosen_ready, 1)
                    pe.wait_ge(one_set, 1)
                    flat = chosen[:, :, :].rearrange("p t e -> p (t e)")
                    pe.matmul(banks[3][:, 0:TILES * X], tri[:, :], flat, start=True, stop=True)
                    pe.matmul(banks[4][:, 0:TILES * X], ones[:, :], flat, start=True, stop=True).then_inc(ranks_done, 1)

                @block.scalar
                def _(act):
                    sca(act)
                    act.wait_ge(rstep, 2)
                    act.activation(probs[:, :, :], probs[:, :, :], ACT.Exp).then_inc(expd, 1)
                    for k in range(HALVES):
                        act.wait_ge(raw_in[k], 16)
                        act.mul(gu[0][0][:, k, :], raw[k][:, :], GU_SCALE).then_inc(w_hi[k], 1)

                @block.vector
                def _(dve):
                    dve.memset(ones[:, :], 1.0).then_inc(one_set, 1)
                    vec(dve)
                    step = Count(rstep)

                    def do(instruction):
                        dve.wait_ge(rstep, step.inc(instruction))

                    def wide(a):
                        return a.unsqueeze(2).broadcast_to(wide_)

                    logits = banks[2][:, 0:TILES * X].rearrange("p (t e) -> p t e", e=X)
                    dve.wait_ge(logits_done, 1)
                    do(dve.tensor_reduce(lmax[:, :], logits, AX.X, ALU.max))
                    do(dve.tensor_tensor(probs[:, :, :], logits, wide(lmax[:, :]), ALU.subtract))
                    dve.wait_ge(ln_copied, TILES // 2)
                    dve.tensor_copy(xh[0][:, :, :], xnT[:, :, :]).then_inc(xsplit, 1)
                    dve.wait_ge(xsplit, 1)
                    dve.tensor_tensor(xh[1][:, :, :], xnT[:, :, :], xh[0][:, :, :], ALU.subtract).then_inc(xsplit, 1)
                    dve.wait_ge(expd, 1)
                    do(dve.tensor_reduce(lmax[:, :], probs[:, :, :], AX.X, ALU.add))
                    do(dve.reciprocal(lmax[:, :], lmax[:, :]))
                    do(dve.tensor_tensor(probs[:, :, :], probs[:, :, :], wide(lmax[:, :]), ALU.mult))
                    for t in range(TILES):
                        step.inc(dve.max(top[:, t, :], probs[:, t, :]))
                    dve.wait_ge(rstep, step.n)
                    for t in range(TILES):
                        step.inc(dve.max_index(topi[:, t, :], top[:, t, :], probs[:, t, :]))
                    dve.wait_ge(rstep, step.n)
                    do(dve.tensor_copy(topf[:, :, :], topi[:, :, :]))
                    do(dve.tensor_tensor(lmax[:, :], top[:, :, 0], top[:, :, 1], ALU.add))
                    do(dve.tensor_scalar(lmax[:, :], lmax[:, :], 1e-8, None, ALU.add))
                    do(dve.reciprocal(lmax[:, :], lmax[:, :]))
                    nums = consts[:, 0:X].unsqueeze(1).broadcast_to(wide_)
                    for k in range(TOPK):
                        do(dve.tensor_tensor(share[k][:, :], top[:, :, k], lmax[:, :], ALU.mult))
                        do(dve.tensor_tensor(hot[k][:, :, :], nums, wide(topf[:, :, k]), ALU.is_equal))
                    dve.tensor_tensor(chosen[:, :, :], hot[0][:, :, :], hot[1][:, :, :], ALU.add).then_inc(chosen_ready, 1)
                    ranks = banks[3][:, 0:TILES * X].rearrange("p (t e) -> p t e", e=X)
                    totals = banks[4][:, 0:TILES * X].rearrange("p (t e) -> p e t", e=X)
                    do(dve.memset(shifted[:, :, 0:1], 0.0))
                    do(dve.memset(carry[:, :, 1:TILES], 1.0))
                    do(dve.memset(carry[:, :, 0:1], 0.0))
                    do(dve.memset(ones_x[:, :], 1.0))
                    do(dve.memset(tiles_sh[:, :], 0.0))
                    dve.wait_ge(ranks_done, 1)
                    do(dve.tensor_copy(shifted[:, :, 1:TILES], totals[:, :, 0:TILES - 1]))
                    do(dve.tensor_tensor_scan(before[:, :, :].rearrange("p e t -> p (e t)"),
                                              carry[:, :, :].rearrange("p e t -> p (e t)"),
                                              shifted[:, :, :].rearrange("p e t -> p (e t)"), 0.0, ALU.mult, ALU.add))
                    do(dve.tensor_tensor(count[:, :], before[:, :, TILES - 1], totals[:, :, TILES - 1], ALU.add))
                    do(dve.tensor_tensor(cmp[:, 0:X, :], count[:, :].unsqueeze(2).broadcast_to([P, X, X]),
                                         consts[:, 2 * SLOT_TILES:].unsqueeze(1).broadcast_to([P, X, X]), ALU.is_gt))
                    do(dve.tensor_reduce(tiles_of[:, :], cmp[:, 0:X, :], AX.X, ALU.add))
                    do(dve.tensor_copy(tiles_sh[:, 1:X], tiles_of[:, 0:X - 1]))
                    do(dve.tensor_tensor_scan(first_tile[:, :], ones_x[:, :], tiles_sh[:, :], 0.0, ALU.mult, ALU.add))
                    do(dve.tensor_tensor(end_tile[:, :], first_tile[:, :], tiles_of[:, :], ALU.add))
                    do(dve.tensor_tensor(slot_of[:, :, :], ranks, before[:, :, :].rearrange("p e t -> p t e"), ALU.add))
                    do(dve.tensor_scalar(first_tile[:, :], first_tile[:, :], float(SLOTS), None, ALU.mult))
                    do(dve.tensor_tensor(slot_of[:, :, :], slot_of[:, :, :], first_tile[:, :].unsqueeze(1).broadcast_to(wide_), ALU.add))
                    for k in range(TOPK):
                        do(dve.tensor_tensor(work[:, :, :], slot_of[:, :, :], hot[k][:, :, :], ALU.mult))
                        do(dve.tensor_reduce(lmax[:, :], work[:, :, :], AX.X, ALU.add))
                        do(dve.tensor_copy(pos_u[k][:, :], lmax[:, :]))
                    dve.sem_inc(positions, 1)
                    both = [P, SLOT_TILES, X]
                    do(dve.tensor_tensor(cmp[:, :, :], end_tile[:, :].unsqueeze(1).broadcast_to(both),
                                         consts[:, 0:SLOT_TILES].unsqueeze(2).broadcast_to(both), ALU.is_le))
                    do(dve.tensor_reduce(eid[:, :], cmp[:, :, :], AX.X, ALU.add))
                    do(dve.tensor_scalar(eid[:, :], eid[:, :], float(X - 1), 1.0, ALU.min, ALU.add))
                    dve.tensor_copy(eid_u[:, :], eid[:, :]).then_inc(eids_ready, 1)
                    dve.wait_ge(eids_ready, 1)
                    for k in range(HALVES):
                        dve.wait_ge(w_hi[k], 1)
                        dve.scalar_tensor_tensor(gu[0][1][:, k, :], raw[k][:, :], GU_SCALE, gu[0][0][:, k, :],
                                                 ALU.mult, ALU.subtract).then_inc(w_lo[k], 1)
            small_st.close()

            xs_in_sb = [sb(st, f"xs_in{p}", [P, 2, DIM]) for p in range(2)]
            xsT = [[sb(st, f"xsT_{n}{p}", [P, HALVES, SLOTS], F16) for n in ("hi", "lo")] for p in range(2)]
            sg = [sb(st, f"sg{b}", [FP, 2, SLOTS]) for b in range(2)]
            h32 = [sb(st, f"h32_{b}", [FP, 2, SLOTS]) for b in range(2)]
            hh = [[sb(st, f"h_{n}{p}", [FP, FG, SLOTS], F16) for n in ("hi", "lo")] for p in range(2)]
            ysb = [sb(st, f"ysb{p}", [P, 2, DIM]) for p in range(2)]
            yg = [sb(st, f"yg{b}", [P, DIM]) for b in range(4)]
            xs_in = [sem(f"xs_in{p}") for p in range(2)]
            xs_turned = [sem(f"xs_turned{p}") for p in range(2)]
            xs_hi = [sem(f"xs_hi{p}") for p in range(2)]
            xs_lo = [sem(f"xs_lo{p}") for p in range(2)]
            g_done = [sem(f"gate_up_done{b}") for b in range(2)]
            sg_ready = [sem(f"gate_silu{b}") for b in range(2)]
            h32_ready = [sem(f"hidden{b}") for b in range(2)]
            h_hi = [sem(f"hidden_hi{b}") for b in range(2)]
            h_lo = [sem(f"hidden_lo{b}") for b in range(2)]
            d_done = [sem(f"down_done{t}") for t in range(2)]
            d_taken = [sem(f"down_taken{t}") for t in range(2)]
            ys_out = [sem(f"ys_out{p}") for p in range(2)]
            y_in = [sem(f"y_gathered{b}") for b in range(4)]
            y_added, stored = sem("y_added"), sem("stored")
            GB, UB, DB, TB = banks[0:2], banks[2:4], banks[4:6], banks[6:8]
            PASSES = ((0, 0), (0, 1), (1, 0))
            PAIRS_F = FG // 2
            SH = TOKENS // SLOTS // 2
            E0, E1 = SH, SH + SLOT_TILES
            LAST = E1 + SH
            COMBINE = {E1 + 1: (0, 8), E1 + 2: (8, 20), E1 + 3: (20, TILES * TOPK)}

            def place(m):
                unit = 0 if m < E0 else min(m, E1) - SH + 1
                return m % 2, unit, unit % 2

            def slot_tiles_to(half, p):
                return half - (E0 if E0 % 2 == p else E0 + 1) // 2

            def windows(window):
                def kind(m):
                    return "slot" if E0 <= m < E1 else "shared"

                def one(m):
                    p, u, w = place(m)
                    window(m, m // 2, p, u, w, kind(m), kind(m - 1) if m else None, kind(m + 1) if m + 1 < LAST else None,
                           m in (0, E1) or kind(m) == "slot", m)
                for m in range(E0 + 1):
                    one(m)
                pairs = (E1 - 1 - (E0 + 1)) // 2
                return one, pairs

            def run_windows(engine, window):
                one, pairs = windows(window)
                with engine.Fori(0, pairs) as k:
                    for s in range(2):
                        m0 = E0 + 1 + s
                        m = 2 * k + m0
                        window(m, k + m0 // 2, m0 % 2, m - SH + 1, (m0 - SH + 1) % 2, "slot", "slot", "slot", True, None)
                for m in range(E0 + 1 + 2 * pairs, LAST):
                    one(m)

            with nc.Block() as block:
                @block.sync
                def _(sp):
                    def load_rows(j, p):
                        sp.dma_start(xs_in_sb[p][:, :, :], xs_rows[bass.ds(j * SLOTS, SLOTS), :]
                                     .rearrange("(t p) d -> p t d", p=P)).then_inc(xs_in[p], 16)

                    def window(m, half, p, u, w, kind, prev, nxt, opens, static):
                        def expert(unit):
                            return sp.value_load(eid_u[0:1, bass.ds(unit - 1, 1)], min_val=1, max_val=EXPERTS)

                        if opens:
                            own = 0 if static in (0, E1) else expert(u)
                            nxt_own = 0 if static in (E1 - 1, E1) else expert(u + 1)
                            if static != 0:
                                sp.wait_ge(w_lo[2], u)
                                load_raw(sp, 2, own)
                            if static != E1:
                                for h in range(HALVES):
                                    sp.wait_ge(w_lo[h], u + 1)
                                    load_raw(sp, h, nxt_own)
                        if static is None or E0 <= static + 2 < E1:
                            if static is None or static + 2 >= E0 + 2:
                                sp.wait_ge(xs_turned[p], slot_tiles_to(half, p) + 1)
                            load_rows(m + 2 - SH, p)

                    run_windows(sp, window)
                    for c in range(2):
                        half = TILES // 2
                        sp.wait_ge(y_added, half * TOPK * (c + 1))
                        if c:
                            for t in range(2):
                                sp.wait_ge(d_taken[t], LAST)
                        sp.dma_start(out[c * half * P:(c + 1) * half * P, :].rearrange("(i p) d -> p i d", p=P),
                                     xres[:, c * half:(c + 1) * half, :]).then_inc(stored, 16)
                    sp.wait_ge(stored, 32)

                @block.tensor
                def _(pe):
                    def wait(semaphore, n):
                        if not (isinstance(n, int) and n <= 0):
                            pe.wait_ge(semaphore, n)

                    def turn(c, p):
                        pe.wait_ge(xs_in[p], 16 * c + 16)
                        wait(xs_lo[p], c)
                        for h in range(HALVES):
                            for t in range(2):
                                at = (h * 2 + t) * P
                                mm = pe.transpose(TB[p][:, at:at + P], xs_in_sb[p][:, t, h * P:(h + 1) * P], ident[:, :])
                        mm.then_inc(xs_turned[p], 1)

                    def hidden(m, half, p, u, w, kind, opens):
                        if opens:
                            for k in range(HALVES):
                                pe.wait_ge(w_lo[k], u + 1)
                        if kind == "slot":
                            pe.wait_ge(xs_lo[p], slot_tiles_to(half, p) + 1)
                            rows = [x[:, :, :] for x in xsT[p]]
                        else:
                            at = (m if m < E0 else m - SLOT_TILES) * SLOTS
                            rows = [x[:, :, at:at + SLOTS] for x in xh]
                        for g in range(PAIRS_F):
                            b = g % 2
                            wait(h32_ready[b], 2 * m + g // 2)
                            for bank, off in ((GB[b], 0), (UB[b], FG * FP)):
                                for f in range(2):
                                    col = off + (2 * g + f) * FP
                                    n = 0
                                    for h in range(HALVES):
                                        for wp, xp in PASSES:
                                            mm = pe.matmul(bank[0:FP, f * SLOTS:(f + 1) * SLOTS], gu[w][wp][:, h, col:col + FP],
                                                           rows[xp][:, h, :], start=(n == 0), stop=(n == 3 * HALVES - 1))
                                            n += 1
                            mm.then_inc(g_done[b], 1)

                    def project(m, p, u, w):
                        pe.wait_ge(w_lo[2], u + 1)
                        for b in range(2):
                            pe.wait_ge(h_lo[b], 2 * m + 2)
                        for t in range(2):
                            wait(d_taken[t], m)
                            n = 0
                            for g in range(FG):
                                for wp, hp in PASSES:
                                    mm = pe.matmul(DB[t][:, 0:DIM], hh[p][hp][:, g, t * P:(t + 1) * P], down[w][wp][:, g, :],
                                                   start=(n == 0), stop=(n == 3 * FG - 1))
                                    n += 1
                            mm.then_inc(d_done[t], 1)

                    def window(m, half, p, u, w, kind, prev, nxt, opens, static):
                        if nxt == "slot":
                            turn(slot_tiles_to(half + p, 1 - p), 1 - p)
                        hidden(m, half, p, u, w, kind, opens)
                        if prev:
                            pp, pu, pw = place(m - 1) if static is not None else (1 - p, u - 1, 1 - w)
                            project(m - 1, pp, pu, pw)

                    run_windows(pe, window)
                    project(LAST - 1, *place(LAST - 1))

                @block.scalar
                def _(act):
                    def wait(semaphore, n):
                        if not (isinstance(n, int) and n <= 0):
                            act.wait_ge(semaphore, n)

                    def split_hi(k, u, w):
                        act.wait_ge(raw_in[k], 16 * u + 16)
                        if k < HALVES:
                            act.mul(gu[w][0][:, k, :], raw[k][:, :], GU_SCALE).then_inc(w_hi[k], 1)
                        else:
                            act.mul(down[w][0][:, :, :], raw[2][:, :, :], DOWN_SCALE).then_inc(w_hi[2], 1)

                    def take(m, half, p):
                        for t in range(2):
                            act.wait_ge(d_done[t], m + 1)
                            if t == 0:
                                wait(ys_out[p], 16 * slot_tiles_to(half, p))
                            act.mul(ysb[p][:, t, :], DB[t][:, 0:DIM], 1.0 / (GU_SCALE * DOWN_SCALE)).then_inc(d_taken[t], 1)

                    def window(m, half, p, u, w, kind, prev, nxt, opens, static):
                        if nxt == "slot":
                            c = slot_tiles_to(half + p, 1 - p)
                            act.wait_ge(xs_turned[1 - p], c + 1)
                            act.copy(xsT[1 - p][0][:, :, :], TB[1 - p][:, :].rearrange("p (h t) -> p h t", h=HALVES)
                                     ).then_inc(xs_hi[1 - p], 1)
                        for g in range(PAIRS_F):
                            b = g % 2
                            n = 2 * m + g // 2
                            act.wait_ge(g_done[b], n + 1)
                            wait(h32_ready[b], n)
                            act.activation(sg[b][:, :, :], GB[b][0:FP, :].rearrange("p (f s) -> p f s", f=2), ACT.Silu,
                                           scale=1.0 / GU_SCALE).then_inc(sg_ready[b], 1)
                            if opens:
                                if g == 0:
                                    wait(d_done[1], 0 if static in (0, E0) else m - 1)
                                    split_hi(2, u, w)
                                elif g <= HALVES and static != E1:
                                    split_hi(g - 1, u + 1, 1 - w)
                            act.wait_ge(h32_ready[b], n + 1)
                            if g == 0:
                                wait(d_done[1], m - 1)
                            act.copy(hh[p][0][:, 2 * g:2 * g + 2, :], h32[b][:, :, :]).then_inc(h_hi[b], 1)
                        if prev == "slot":
                            take(m - 1, half - 1 + p, 1 - p)

                    run_windows(act, window)

                @block.vector
                def _(dve):
                    def wait(semaphore, n):
                        if not (isinstance(n, int) and n <= 0):
                            dve.wait_ge(semaphore, n)

                    def split_lo(k, u, w):
                        dve.wait_ge(w_hi[k], u + 1)
                        if k < HALVES:
                            dve.scalar_tensor_tensor(gu[w][1][:, k, :], raw[k][:, :], GU_SCALE, gu[w][0][:, k, :],
                                                     ALU.mult, ALU.subtract).then_inc(w_lo[k], 1)
                        else:
                            dve.scalar_tensor_tensor(down[w][1][:, :, :], raw[2][:, :, :], DOWN_SCALE, down[w][0][:, :, :],
                                                     ALU.mult, ALU.subtract).then_inc(w_lo[2], 1)

                    def add_shared(m):
                        tile = 2 * (m if m < E0 else m - SLOT_TILES)
                        for t in range(2):
                            dve.wait_ge(d_done[t], m + 1)
                            dve.scalar_tensor_tensor(xres[:, tile + t, :], DB[t][:, 0:DIM], 1.0 / (GU_SCALE * DOWN_SCALE),
                                                     xres[:, tile + t, :], ALU.mult, ALU.add).then_inc(d_taken[t], 1)

                    def window(m, half, p, u, w, kind, prev, nxt, opens, static):
                        if nxt == "slot":
                            c = slot_tiles_to(half + p, 1 - p)
                            dve.wait_ge(xs_hi[1 - p], c + 1)
                            dve.tensor_tensor(xsT[1 - p][1][:, :, :], TB[1 - p][:, :].rearrange("p (h t) -> p h t", h=HALVES),
                                              xsT[1 - p][0][:, :, :], ALU.subtract).then_inc(xs_lo[1 - p], 1)
                        for g in range(PAIRS_F):
                            b = g % 2
                            n = 2 * m + g // 2
                            dve.wait_ge(sg_ready[b], n + 1)
                            dve.tensor_tensor(h32[b][:, :, :], sg[b][:, :, :], UB[b][0:FP, :].rearrange("p (f s) -> p f s", f=2),
                                              ALU.mult).then_inc(h32_ready[b], 1)
                            if opens:
                                if g == 0:
                                    split_lo(2, u, w)
                                elif g <= HALVES and static != E1:
                                    split_lo(g - 1, u + 1, 1 - w)
                            dve.wait_ge(h_hi[b], n + 1)
                            dve.tensor_tensor(hh[p][1][:, 2 * g:2 * g + 2, :], h32[b][:, :, :], hh[p][0][:, 2 * g:2 * g + 2, :],
                                              ALU.subtract).then_inc(h_lo[b], 1)
                        if prev == "shared":
                            add_shared(m - 1)
                        for n in range(*COMBINE.get(static, (0, 0))):
                            t, k = n // TOPK, n % TOPK
                            wait(y_added, n)
                            wait(d_taken[t % 2], m if k == 0 else 0)
                            dve.wait_ge(y_in[n % 4], 16 * (n // 4 + 1))
                            dve.scalar_tensor_tensor(xres[:, t, :], yg[n % 4][:, :], share[k][:, t:t + 1], xres[:, t, :],
                                                     ALU.mult, ALU.add).then_inc(y_added, 1)

                    run_windows(dve, window)
                    dve.wait_ge(y_added, TILES * TOPK)
                    add_shared(LAST - 1)

                @block.gpsimd
                def _(pool):
                    def store(m, p):
                        for t in range(2):
                            pool.wait_ge(d_taken[t], m + 1)
                        pool.dma_start(ys_rows[bass.ds((m - SH) * SLOTS, SLOTS), :].rearrange("(t p) d -> p t d", p=P),
                                       ysb[p][:, :, :]).then_inc(ys_out[p], 16)

                    store(E0, E0 % 2)
                    with pool.Fori(0, (SLOT_TILES - 1) // 2) as k:
                        for s in range(2):
                            store(2 * k + E0 + 1 + s, (E0 + 1 + s) % 2)
                    pool.wait_ge(ys_out[E0 % 2], 16 * ((SLOT_TILES + 1) // 2))
                    pool.wait_ge(ys_out[1 - E0 % 2], 16 * (SLOT_TILES // 2))
                    for n in range(TILES * TOPK):
                        t, k = n // TOPK, n % TOPK
                        if n >= 4:
                            pool.wait_ge(y_added, n - 3)
                        pool.indirect_dma_start(out=yg[n % 4][:, :], out_offset=None, in_=ys_rows,
                                                in_offset=bass.IndirectOffsetOnAxis(ap=pos_u[k][:, t:t + 1], axis=0)
                                                ).then_inc(y_in[n % 4], 16)


def kernel(**inputs):
    import concourse.bacc as bacc
    from concourse.bass_utils import run_bass_kernel_spmd

    a = {k: np.asarray(v) for k, v in inputs.items()}
    gate_up = np.concatenate([a["L0_ffn_shared_gate_up"][None], a["L0_ffn_experts_gate_up"]])
    down = np.concatenate([a["L0_ffn_shared_down"][None], a["L0_ffn_experts_down"]])
    gu_t = np.zeros((EXPERTS + 1, DIM, 2, FG * FP), np.float32)
    gu_t[:, :, :, 0:FF] = gate_up.reshape(EXPERTS + 1, 2, FF, DIM).transpose(0, 3, 1, 2)
    down_t = np.zeros((EXPERTS + 1, FG * FP, DIM), np.float32)
    down_t[:, 0:FF, :] = down.transpose(0, 2, 1)
    xp = a["L0_attn_x_proj_w"]
    sel = np.zeros((3, 2 * STATE, 2 * STATE, P // 2), np.uint32)
    for n in range(2 * STATE):
        sel[:, n, n, :] = 0x3F803F80
    laid = {
        "x": a["x"].reshape(TOKENS, DIM),
        "ctx_rows": a["ctx_1024"].reshape(BATCH * CTX, DIM),
        "mask_t": a["mask_BxSxS2_bk0"].transpose(0, 2, 1).reshape(BATCH * CTX, SEQ).view(np.uint32),
        "wq": a["L0_xattn_Wq"], "wk": a["L0_xattn_Wk"], "wv_t": a["L0_xattn_Wv"].T,
        "in_w_t": a["L0_attn_in_proj_w"].T, "conv_w": a["L0_attn_conv_w"], "conv_b": a["L0_attn_conv_b"],
        "bc_w_t": xp[1:].T, "dt_row_t": np.repeat(xp[0:1].T, P, axis=1),
        "a_log": a["L0_attn_A_log"], "d_param": a["L0_attn_D_param"], "dt_w": a["L0_attn_dt_w"], "dt_b": a["L0_attn_dt_b"],
        "out_w_t": a["L0_attn_out_w"].T, "ln_g": a["L0_attn_ln_g"], "ln_b": a["L0_attn_ln_b"],
        "gate_w_t": a["L0_ffn_gate_weight"].T,
        "gu_t": gu_t.reshape((EXPERTS + 1) * DIM, 2 * FG * FP), "down_t": down_t.reshape((EXPERTS + 1) * FG * FP, DIM),
        "ident_in": np.eye(P, dtype=np.float32),
        "sel_in": sel.reshape(6 * STATE, 2 * STATE, P // 2),
        "consts_t": np.tile(np.concatenate([np.arange(2 * SLOT_TILES), SLOTS * np.arange(EXPERTS)]).astype(np.float32), (P, 1)),
        "tri_in": np.triu(np.ones((P, P), np.float32), 1),
    }
    nc = bacc.Bacc("TRN2", target_bir_lowering=False, num_devices=1)
    arrays, args = {}, []
    for name, array in laid.items():
        arrays[name] = np.ascontiguousarray(array)
        args.append(nc.dram_tensor(name, array.shape, mybir.dt.from_np(array.dtype), kind="ExternalInput").ap())
    out = nc.dram_tensor("out", (TOKENS, DIM), F32, kind="ExternalOutput").ap()
    build(nc, *args, out)
    result = run_bass_kernel_spmd(nc, [arrays], core_ids=[0])
    return result.results[0]["out"].reshape(BATCH, SEQ, DIM)
```

```python
from contextlib import ExitStack

import numpy as np

import concourse.bass as bass
from concourse import mybir

F32 = mybir.dt.float32
BF16 = mybir.dt.bfloat16
F16 = mybir.dt.float16
U8 = mybir.dt.uint8
U32 = mybir.dt.uint32
ALU = mybir.AluOpType
ACT = mybir.ActivationFunctionType
AX = mybir.AxisListType

P = 128
BATCH, SEQ, DIM = 32, 64, 256
TOKENS = BATCH * SEQ
TILES = TOKENS // P
HALVES = DIM // P
CTX = 1601
KROWS = CTX // P
KREST = CTX - KROWS * P
KT = KROWS + 1
INNER, STATE, TAPS = 512, 16, 4
Q = INNER // P
CHUNK = 512
CHUNKS = TOKENS // CHUNK
CB = CHUNK // SEQ
PADDED = SEQ + TAPS - 1
EXPERTS, TOPK, FF = 8, 2, 938
FP = 118
FG = 8
SLOTS = 256
SLOT_TILES = TOKENS * TOPK // SLOTS + EXPERTS - 1
GU_SCALE, DOWN_SCALE = 16.0, 64.0
EPS = 1e-5


class Count:

    def __init__(self, sem):
        self.sem, self.n = sem, 0

    def inc(self, instruction):
        self.n += 1
        instruction.then_inc(self.sem, 1)
        return self.n


def build(nc, x, ctx_rows, mask_t, wq, wk, wv_t, in_w_t, conv_w, conv_b, bc_w_t, dt_row_t, a_log,
          d_param, dt_w, dt_b, out_w_t, ln_g, ln_b, gate_w_t, gu_t, down_t, ident_in,
          sel_in, consts_t, tri_in, out):
    keep = ExitStack()
    stage_sems = []

    def sem(name):
        stage_sems.append(nc.alloc_semaphore(name=name))
        return stage_sems[-1]

    def end_of_stage():
        nc.clear_and_free_semaphores(stage_sems)
        nc.all_engine_barrier()
        stage_sems.clear()

    def sb(stack, name, shape, dt=F32):
        return stack.enter_context(nc.sbuf_tensor(name, shape, dt))

    with keep:
        xres = sb(keep, "xres", [P, TILES, DIM])
        xnT = sb(keep, "xnT", [P, HALVES, TOKENS])
        ident = sb(keep, "ident", [P, P])
        stats = sb(keep, "stats", [P, TILES, 6])
        meanvar = sb(keep, "meanvar", [P, TILES, 2])
        rstd = sb(keep, "rstd", [P, TILES])
        epsc = sb(keep, "epsc", [P, 1])
        banks = [keep.enter_context(nc.psum_tensor(f"bank{i}", [P, 512], F32)) for i in range(8)]

        ten_rows = [None]
        xs_rows = nc.dram_tensor("xs_rows", (SLOT_TILES * SLOTS, DIM), F32, kind="Internal").ap()
        ys_rows = nc.dram_tensor("ys_rows", (SLOT_TILES * SLOTS, DIM), F32, kind="Internal").ap()

        def layernorm(tag, stack, before=None):
            xn = sb(stack, f"xn_{tag}", [P, TILES, DIM])
            ten_rows[0] = xn
            stats_done, aggr_done = sem(f"stats_done_{tag}"), sem(f"aggr_done_{tag}")
            std_done, rstd_done = sem(f"std_done_{tag}"), sem(f"rstd_done_{tag}")
            xn_ready, turned, bank_free = sem(f"xn_ready_{tag}"), sem(f"turned_{tag}"), sem(f"turn_free_{tag}")

            def vector(dve):
                for i in range(TILES):
                    if before:
                        before(dve, i)
                    dve.bn_stats(stats[:, i, :], xres[:, i, :]).then_inc(stats_done, 1)
                for i in range(TILES):
                    dve.wait_ge(stats_done, i + 1)
                    dve.bn_aggr(meanvar[:, i, :], stats[:, i, :]).then_inc(aggr_done, 1)
                dve.wait_ge(std_done, 1)
                dve.reciprocal(rstd[:, :], rstd[:, :]).then_inc(rstd_done, 1)
                dve.wait_ge(rstd_done, 1)
                for i in range(TILES):
                    dve.tensor_scalar(xn[:, i, :], xres[:, i, :], meanvar[:, i, 0:1], rstd[:, i:i + 1],
                                      ALU.subtract, ALU.mult).then_inc(xn_ready, 1)

            def scalar(act):
                act.wait_ge(aggr_done, TILES)
                act.activation(rstd[:, :], meanvar[:, :, 1], ACT.Sqrt, bias=epsc[:, 0:1]).then_inc(std_done, 1)
                for g in range(TILES // 2):
                    act.wait_ge(turned, g + 1)
                    act.copy(xnT[:, :, g * 2 * P:(g + 1) * 2 * P],
                             banks[g % 2][:, :].rearrange("p (h t) -> p h t", h=HALVES)).then_inc(bank_free, 1)

            def tensor(pe):
                for g in range(TILES // 2):
                    pe.wait_ge(xn_ready, 2 * g + 2)
                    if g >= 2:
                        pe.wait_ge(bank_free, g - 1)
                    for h in range(HALVES):
                        for t in range(2):
                            at = (h * 2 + t) * P
                            last = pe.transpose(banks[g % 2][:, at:at + P],
                                                xn[:, 2 * g + t, h * P:(h + 1) * P], ident[:, :])
                    last.then_inc(turned, 1)

            return vector, scalar, tensor, bank_free

        att = ExitStack()
        with att:
            qk = [sb(att, f"qk_{n}", [P, HALVES, TOKENS], F16) for n in ("hi", "lo")]
            wv_sb = sb(att, "wv_sb", [P, HALVES, DIM])
            RAW, NAT, TWO = 2, 4, 2
            raw = [sb(att, f"ctx_raw{n}", [P, KT, DIM]) for n in range(RAW)]
            mask_words = [sb(att, f"mask{n}", [P, KT, SEQ // 4], U32) for n in range(NAT)]
            cleared = sem("padding_cleared")
            ctx_in = [sem(f"ctx_in{n}") for n in range(RAW)]

            def load_batch(sp, first, n, m):
                rows, rest = bass.ds(first, KROWS * P), bass.ds(first + KROWS * P, KREST)
                sp.dma_start(raw[n][:, 0:KROWS, :],
                             ctx_rows[rows, :].rearrange("(p t) d -> p t d", t=KROWS)).then_inc(ctx_in[n], 16)
                sp.dma_start(mask_words[m][:, 0:KROWS, :],
                             mask_t[rows, :].rearrange("(p t) q -> p t q", t=KROWS)).then_inc(ctx_in[n], 16)
                sp.dma_start(raw[n][0:KREST, KROWS, :], ctx_rows[rest, :]).then_inc(ctx_in[n], 16)
                sp.dma_start(mask_words[m][0:KREST, KROWS, :], mask_t[rest, :]).then_inc(ctx_in[n], 16)

            with ExitStack() as first:
                wq_sb = sb(first, "wq_sb", [P, HALVES, DIM])
                wk_sb = sb(first, "wk_sb", [P, HALVES, DIM])
                wqk = sb(first, "wqk", [P, HALVES, DIM])
                x_in = [sem(f"x_in{i}") for i in range(4)]
                ident_in_s, w_in, eps_set = sem("ident_loaded"), sem("attention_weights_loaded"), sem("eps_set")
                wqk_done, wqk_copied = sem("wqk_done"), sem("wqk_copied")
                qk_done, qk_hi, qk_lo = sem("qk_done"), sem("qk_hi"), sem("qk_lo")
                nx = TILES // 4
                vec, sca, ten, ln_copied = layernorm(
                    "a", first, lambda dve, i: dve.wait_ge(x_in[i // nx], 16) if i % nx == 0 else None)
                with nc.Block() as block:
                    @block.sync
                    def _(sp):
                        for c in range(4):
                            sp.dma_start(xres[:, c * nx:(c + 1) * nx, :],
                                         x[c * nx * P:(c + 1) * nx * P, :].rearrange("(i p) d -> p i d", p=P)
                                         ).then_inc(x_in[c], 16)
                        sp.dma_start(ident[:, :], ident_in).then_inc(ident_in_s, 16)
                        for dst, src in ((wq_sb, wq), (wk_sb, wk), (wv_sb, wv_t)):
                            sp.dma_start(dst[:, :, :], src.rearrange("(h p) d -> p h d", p=P)).then_inc(w_in, 16)
                        sp.wait_ge(cleared, RAW + NAT)
                        for b in range(RAW):
                            load_batch(sp, b * CTX, b, b)
                        sp.wait_ge(w_in, 48)

                    @block.vector
                    def _(dve):
                        dve.memset(epsc[:, :], EPS).then_inc(eps_set, 1)
                        for n in range(RAW):
                            dve.memset(raw[n][:, KROWS, :], 0.0).then_inc(cleared, 1)
                        for n in range(NAT):
                            dve.memset(mask_words[n][:, KROWS, :], 0).then_inc(cleared, 1)
                        vec(dve)
                        for n in range(HALVES * CHUNKS):
                            h, c = n % HALVES, n // HALVES
                            dve.wait_ge(qk_hi, n + 1)
                            dve.tensor_tensor(qk[1][:, h, c * CHUNK:(c + 1) * CHUNK], banks[4 + n % 4][:, :],
                                              qk[0][:, h, c * CHUNK:(c + 1) * CHUNK], ALU.subtract).then_inc(qk_lo, 1)

                    @block.scalar
                    def _(act):
                        act.wait_ge(eps_set, 1)
                        sca(act)
                        for k in range(HALVES):
                            act.wait_ge(wqk_done, k + 1)
                            act.copy(wqk[:, k, :], banks[2 + k][:, 0:DIM]).then_inc(wqk_copied, 1)
                        for n in range(HALVES * CHUNKS):
                            h, c = n % HALVES, n // HALVES
                            act.wait_ge(qk_done, n + 1)
                            act.copy(qk[0][:, h, c * CHUNK:(c + 1) * CHUNK], banks[4 + n % 4][:, :]).then_inc(qk_hi, 1)

                    @block.tensor
                    def _(pe):
                        pe.wait_ge(ident_in_s, 16)
                        pe.wait_ge(w_in, 48)
                        ten(pe)
                        for k in range(HALVES):
                            for h in range(HALVES):
                                mm = pe.matmul(banks[2 + k][:, 0:DIM], wq_sb[:, h, k * P:(k + 1) * P], wk_sb[:, h, :],
                                               start=(h == 0), stop=(h == HALVES - 1))
                            mm.then_inc(wqk_done, 1)
                        pe.wait_ge(wqk_copied, HALVES)
                        pe.wait_ge(ln_copied, TILES // 2)
                        for n in range(HALVES * CHUNKS):
                            h, c = n % HALVES, n // HALVES
                            if n >= 4:
                                pe.wait_ge(qk_lo, n - 3)
                            for k in range(HALVES):
                                mm = pe.matmul(banks[4 + n % 4][:, :], wqk[:, k, h * P:(h + 1) * P],
                                               xnT[:, k, c * CHUNK:(c + 1) * CHUNK],
                                               start=(k == 0), stop=(k == HALVES - 1))
                            mm.then_inc(qk_done, 1)

            with ExitStack() as st:
                nat = [[sb(st, f"ctx_{x}{n}", [P, KT, DIM], F16) for x in ("hi", "lo")] for n in range(NAT)]
                ctxT = [sb(st, f"ctxT{n}", [P, KT * HALVES, 2, P], F16) for n in range(TWO)]
                mask_sb = [m[:, :, :].bitcast(U8) for m in mask_words]
                sc = [sb(st, f"scores{n}", [P, KT, SEQ]) for n in range(TWO)]
                pr = [[sb(st, f"probs_{x}{n}", [P, KT, SEQ], F16) for x in ("hi", "lo")] for n in range(TWO)]
                rowmax = [sb(st, f"rowmax{n}", [P, KT]) for n in range(TWO)]
                rowsum = [sb(st, f"rowsum{n}", [P, KT]) for n in range(TWO)]
                rowinv = [sb(st, f"rowinv{n}", [P, KT]) for n in range(TWO)]
                fill = sb(st, "fill", [P, KT, SEQ])
                ident16 = sb(st, "ident16", [P, P], F16)
                pcT = [sb(st, f"pcT{n}", [P, HALVES, P]) for n in range(TWO)]
                SB, TB, PB, OB = banks[0:2], banks[2:6], banks[6], banks[7]
                TB16 = [t[:, :].bitcast(F16) for t in TB]
                ident16_set = sem("ident16_set")
                own_turn = sem("own_turn")
                fill_set = sem("fill_set")
                nat_hi_b, nat_hi_a = sem("ctx_hi_b"), sem("ctx_hi_a")
                nat_lo_b, nat_lo_a = sem("ctx_lo_b"), sem("ctx_lo_a")
                turned = sem("ctx_turned")
                ev_act, ev_dve = sem("turned_copied_act"), sem("turned_copied_dve")
                s_done, s_copied, s_masked = sem("scores_done"), sem("scores_copied"), sem("scores_masked")
                s_max, s_shift, s_exp = sem("scores_max"), sem("scores_shifted"), sem("scores_exp")
                s_sum, s_inv, p_full = sem("scores_sum"), sem("scores_inverse"), sem("probs_full")
                p_hi, p_lo = sem("probs_hi"), sem("probs_lo")
                pv_done, pv_copied = sem("pv_done"), sem("pv_copied")
                o_done, o_added = sem("attention_out_done"), sem("attention_out_added")
                BLOCKS = KT * HALVES * 2
                PER = 8
                GROUPS = [(g, min(g + PER, BLOCKS)) for g in range(0, BLOCKS, PER)]
                NG = len(GROUPS)
                BY_ACT = (2, 5)
                BY_DVE = tuple(g for g in range(NG) if g not in BY_ACT)
                PARTS = [(0, 7), (7, KT)]
                A, B = (0, 7), (7, KT)
                P_SCALE = 4096.0

                def wait(engine, semaphore, n):
                    if not (isinstance(n, int) and n <= 0):
                        engine.wait_ge(semaphore, n)

                def steps(engine, step):
                    head, tail = 4, BATCH - 4
                    for k in range(-2, head):
                        step(0, 0, k)
                    with engine.Fori(0, (tail - head) // NAT) as j:
                        for c in range(NAT):
                            step(NAT * j, NAT // 2 * j, head + c)
                    for k in range(tail, BATCH + 1):
                        step(0, 0, k)

                def exists(base, c):
                    return not isinstance(base, int) or 0 <= c < BATCH

                def copied(engine, base, c, g):
                    while g < 0:
                        g, c = g + NG, c - 1
                    by, s_ = (BY_ACT, ev_act) if g in BY_ACT else (BY_DVE, ev_dve)
                    wait(engine, s_, base * len(by) + c * len(by) + by.index(g) + 1 if exists(base, c) else 0)

                with nc.Block() as block:
                    @block.sync
                    def _(sp):
                        def load(base, c):
                            n, m = c % RAW, c % NAT
                            wait(sp, nat_lo_a, base + c - 1)
                            wait(sp, nat_lo_b, base + c - 1)
                            load_batch(sp, (base + c) * CTX, n, m)

                        for b in range(RAW, NAT):
                            load(0, b)
                        with sp.Fori(0, BATCH // NAT - 1) as j:
                            for c in range(NAT):
                                load(NAT * j, NAT + c)

                    @block.vector
                    def _(dve):
                        dve.memset(fill[:, :, :], 1e-9).then_inc(fill_set, 1)
                        dve.tensor_copy(ident16[:, :], ident[:, :]).then_inc(ident16_set, 1)
                        dve.wait_ge(fill_set, 1)

                        def mask_max(base, c, n):
                            a, b = PARTS[n]
                            k = 2 * base + 2 * c + n + 1
                            view = sc[c % TWO][:, a:b, :]
                            dve.wait_ge(s_copied, k)
                            dve.sem_inc(own_turn, 1)
                            dve.copy_predicated(view, mask_sb[c % NAT][:, a:b, :], fill[:, a:b, :]).then_inc(s_masked, 1)
                            dve.wait_ge(s_masked, k)
                            dve.tensor_reduce(rowmax[c % TWO][:, a:b], view, AX.X, ALU.max).then_inc(s_max, 1)

                        def sums(base, c, n):
                            a, b = PARTS[n]
                            k = 2 * base + 2 * c + n + 1
                            dve.wait_ge(s_exp, k)
                            dve.tensor_reduce(rowsum[c % TWO][:, a:b], sc[c % TWO][:, a:b, :], AX.X, ALU.add).then_inc(s_sum, 1)
                            dve.wait_ge(s_sum, k)
                            dve.reciprocal(rowinv[c % TWO][:, a:b], rowsum[c % TWO][:, a:b]).then_inc(s_inv, 1)

                        def low(base, c, n):
                            a, b = PARTS[n]
                            dve.wait_ge(p_hi, 2 * base + 2 * c + n + 1)
                            dve.scalar_tensor_tensor(pr[c % TWO][1][:, a:b, :], sc[c % TWO][:, a:b, :], P_SCALE,
                                                     pr[c % TWO][0][:, a:b, :], ALU.mult, ALU.subtract).then_inc(p_lo, 1)

                        def turned_out(base, c, groups):
                            for g in groups:
                                a, b = GROUPS[g]
                                if g == 0:
                                    wait(dve, s_done, 2 * base + 2 * c - 2)
                                dve.wait_ge(turned, NG * base + NG * c + g + 1)
                                dve.tensor_copy(ctxT[c % TWO][:, a // 2:b // 2, :, :],
                                                TB16[(NG * c + g) % 4][:, 0:(b - a) * P]
                                                .rearrange("p (b x k) -> p b x k", x=2, k=P)).then_inc(ev_dve, 1)

                        def step(base, half, c):
                            if exists(base, c):
                                dve.wait_ge(ctx_in[c % RAW], 64 * half + 64 * (c // 2) + 64)
                                mask_max(base, c, 0)
                                mask_max(base, c, 1)
                            if exists(base, c + 1):
                                turned_out(base, c + 1, (0, 1))
                            if exists(base, c):
                                sums(base, c, 0)
                            if exists(base, c + 1):
                                turned_out(base, c + 1, (3,))
                            if exists(base, c):
                                sums(base, c, 1)
                            if exists(base, c + 1):
                                turned_out(base, c + 1, (4, 6))
                            if exists(base, c + 2):
                                d = c + 2
                                a, b = B
                                dve.wait_ge(nat_hi_b, base + d + 1)
                                dve.tensor_tensor(nat[d % NAT][1][:, a:b, :], raw[d % RAW][:, a:b, :], nat[d % NAT][0][:, a:b, :],
                                                  ALU.subtract).then_inc(nat_lo_b, 1)
                            if exists(base, c):
                                low(base, c, 0)
                                low(base, c, 1)
                            if c % 2 == 1 and exists(base, c - 3):
                                i = half + c // 2 - 1
                                dve.wait_ge(o_done, i + 1)
                                rows = xres[:, bass.ds(i, 1), :].rearrange("p o d -> p (o d)")
                                dve.tensor_tensor(rows, rows, OB[:, 0:DIM], ALU.add).then_inc(o_added, 1)

                        steps(dve, step)
                        i = BATCH // 2 - 1
                        dve.wait_ge(o_done, i + 1)
                        dve.tensor_tensor(xres[:, i, :], xres[:, i, :], OB[:, 0:DIM], ALU.add).then_inc(o_added, 1)

                    @block.gpsimd
                    def _(pool):
                        def shift(base, c, n):
                            a, b = PARTS[n]
                            view = sc[c % TWO][:, a:b, :]
                            pool.wait_ge(s_max, 2 * base + 2 * c + n + 1)
                            pool.tensor_tensor(view, view, rowmax[c % TWO][:, a:b].unsqueeze(2).broadcast_to([P, b - a, SEQ]),
                                               ALU.subtract).then_inc(s_shift, 1)

                        def normalize(base, c, n):
                            a, b = PARTS[n]
                            view = sc[c % TWO][:, a:b, :]
                            pool.wait_ge(s_inv, 2 * base + 2 * c + n + 1)
                            pool.tensor_tensor(view, view, rowinv[c % TWO][:, a:b].unsqueeze(2).broadcast_to([P, b - a, SEQ]),
                                               ALU.mult).then_inc(p_full, 1)

                        def step(base, half, c):
                            if exists(base, c):
                                shift(base, c, 0)
                                shift(base, c, 1)
                                normalize(base, c, 0)
                                normalize(base, c, 1)
                            if exists(base, c + 2):
                                d = c + 2
                                a, b = A
                                pool.wait_ge(nat_hi_a, base + d + 1)
                                pool.tensor_tensor(nat[d % NAT][1][:, a:b, :], raw[d % RAW][:, a:b, :], nat[d % NAT][0][:, a:b, :],
                                                   ALU.subtract).then_inc(nat_lo_a, 1)

                        steps(pool, step)

                    @block.scalar
                    def _(act):
                        def copy_scores(base, c, n):
                            a, b = PARTS[n]
                            act.wait_ge(s_done, 2 * base + 2 * c + n + 1)
                            wait(act, p_lo, 2 * base + 2 * c - 2)
                            act.mul(sc[c % TWO][:, a:b, :], SB[n][:, 0:(b - a) * SEQ]
                                    .rearrange("p (t q) -> p t q", q=SEQ), DIM ** -0.5).then_inc(s_copied, 1)

                        def exps(base, c, n):
                            a, b = PARTS[n]
                            view = sc[c % TWO][:, a:b, :]
                            act.wait_ge(s_shift, 2 * base + 2 * c + n + 1)
                            act.activation(view, view, ACT.Exp).then_inc(s_exp, 1)

                        def high(base, c, n):
                            a, b = PARTS[n]
                            act.wait_ge(p_full, 2 * base + 2 * c + n + 1)
                            wait(act, pv_done, base + c - 1)
                            act.mul(pr[c % TWO][0][:, a:b, :], sc[c % TWO][:, a:b, :], P_SCALE).then_inc(p_hi, 1)

                        def rows_hi(base, half, c, tiles, done):
                            a, b = tiles
                            act.wait_ge(ctx_in[c % RAW], 64 * half + 64 * (c // 2) + 64)
                            wait(act, pv_done, base + c - 3)
                            act.copy(nat[c % NAT][0][:, a:b, :], raw[c % RAW][:, a:b, :]).then_inc(done, 1)

                        def turned_out(base, c, g):
                            a, b = GROUPS[g]
                            act.wait_ge(turned, NG * base + NG * c + g + 1)
                            act.copy(ctxT[c % TWO][:, a // 2:b // 2, :, :], TB16[(NG * c + g) % 4][:, 0:(b - a) * P]
                                     .rearrange("p (b x k) -> p b x k", x=2, k=P)).then_inc(ev_act, 1)

                        def step(base, half, c):
                            if exists(base, c):
                                copy_scores(base, c, 0)
                                copy_scores(base, c, 1)
                            if exists(base, c + 2):
                                rows_hi(base, half, c + 2, B, nat_hi_b)
                            if exists(base, c):
                                exps(base, c, 0)
                            if exists(base, c + 1):
                                turned_out(base, c + 1, 2)
                            if exists(base, c):
                                exps(base, c, 1)
                            if exists(base, c + 1):
                                turned_out(base, c + 1, 5)
                            if exists(base, c + 2):
                                rows_hi(base, half, c + 2, A, nat_hi_a)
                            if exists(base, c):
                                high(base, c, 0)
                                high(base, c, 1)
                            if exists(base, c - 1):
                                d = c - 1
                                pair = half + d // 2
                                act.wait_ge(pv_done, base + d + 1)
                                if d % 2 == 0:
                                    wait(act, o_done, pair - 1)
                                act.mul(pcT[d // 2 % TWO][:, :, d % 2 * SEQ:(d % 2 + 1) * SEQ],
                                        PB[:, 0:HALVES * SEQ].rearrange("p (h q) -> p h q", q=SEQ),
                                        1.0 / P_SCALE).then_inc(pv_copied, 1)

                        steps(act, step)

                    @block.tensor
                    def _(pe):
                        PASSES = ((0, 0), (0, 1), (1, 0))

                        def scores(base, c):
                            copied(pe, base, c, NG - 1)
                            copied(pe, base, c, BY_ACT[-1])
                            wait(pe, s_copied, 2 * base + 2 * c)
                            for n, (a, b) in enumerate(PARTS):
                                for t in range(a, b):
                                    i = 0
                                    for h in range(HALVES):
                                        for cp, qp in PASSES:
                                            mm = pe.matmul(SB[n][:, (t - a) * SEQ:(t - a + 1) * SEQ],
                                                           ctxT[c % TWO][:, t * HALVES + h, cp, :],
                                                           qk[qp][:, h, bass.ds((base + c) * SEQ, SEQ)],
                                                           start=(i == 0), stop=(i == 3 * HALVES - 1))
                                            i += 1
                                mm.then_inc(s_done, 1)

                        def turn(base, c):
                            pe.wait_ge(nat_lo_a, base + c + 1)
                            for g, (a, b) in enumerate(GROUPS):
                                if a // 4 >= B[0] or b // 4 >= B[0]:
                                    pe.wait_ge(nat_lo_b, base + c + 1)
                                copied(pe, base, c, g - 4)
                                for i in range(a, b):
                                    t, h, x = i // 4, i // 2 % 2, i % 2
                                    mm = pe.transpose(TB16[(NG * c + g) % 4][:, (i - a) * P:(i - a + 1) * P],
                                                      nat[c % NAT][x][:, t, h * P:(h + 1) * P], ident16[:, :])
                                mm.then_inc(turned, 1)

                        def weigh(base, c):
                            pe.wait_ge(p_lo, 2 * base + 2 * c + 2)
                            wait(pe, pv_copied, base + c)
                            for h in range(HALVES):
                                i = 0
                                for t in range(KT):
                                    for cp, pp in PASSES:
                                        mm = pe.matmul(PB[:, h * SEQ:(h + 1) * SEQ], nat[c % NAT][cp][:, t, h * P:(h + 1) * P],
                                                       pr[c % TWO][pp][:, t, :], start=(i == 0), stop=(i == 3 * KT - 1))
                                        i += 1
                            mm.then_inc(pv_done, 1)

                        def project(i, n):
                            pe.wait_ge(pv_copied, 2 * i + 2)
                            wait(pe, o_added, i)
                            for h in range(HALVES):
                                mm = pe.matmul(OB[:, 0:DIM], pcT[n][:, h, :], wv_sb[:, h, :],
                                               start=(h == 0), stop=(h == HALVES - 1))
                            mm.then_inc(o_done, 1)

                        def step(base, half, c):
                            if exists(base, c):
                                scores(base, c)
                            if c % 2 == 1 and exists(base, c - 3):
                                project(half + c // 2 - 1, (c // 2 - 1) % TWO)
                            if exists(base, c + 1):
                                turn(base, c + 1)
                            if exists(base, c - 1):
                                weigh(base, c - 1)

                        pe.wait_ge(ident16_set, 1)
                        steps(pe, step)
                        project(BATCH // 2 - 1, (BATCH // 2 - 1) % TWO)

        end_of_stage()

        with ExitStack() as st:
            in_w = sb(st, "in_w", [P, HALVES, 2 * INNER])
            cw = sb(st, "cw", [P, Q, TAPS])
            cb = sb(st, "cb", [P, Q])
            bc_w = sb(st, "bc_w", [P, Q, 2 * STATE])
            dt_row = sb(st, "dt_row", [P, Q, P])
            a_neg = sb(st, "a_neg", [P, Q, STATE])
            dpar = sb(st, "dpar", [P, Q])
            dtw = sb(st, "dtw", [P, Q])
            dtb = sb(st, "dtb", [P, Q])
            out_w = sb(st, "out_w", [P, Q, DIM])
            lng = sb(st, "lng", [P, Q])
            lnb = sb(st, "lnb", [P, Q])
            d_diag = sb(st, "d_diag", [P, Q, P])
            mean_w = sb(st, "mean_w", [P, P])
            sel = sb(st, "sel", [6 * STATE, 2 * STATE, P // 2], U32)
            weights_in, small_set, a_exp, a_done = sem("mamba_weights_in"), sem("small_set"), sem("a_exp"), sem("a_done")
            ln_st = ExitStack()
            vec, sca, ten, _ = layernorm("b", ln_st)
            loads = [(in_w, in_w_t.rearrange("(h p) e -> p h e", p=P)),
                     (cw, conv_w.rearrange("(q p) k -> p q k", p=P)), (cb, conv_b.rearrange("(q p) -> p q", p=P)),
                     (bc_w, bc_w_t.rearrange("(q p) n -> p q n", p=P)),
                     (dt_row, dt_row_t.rearrange("(q p) n -> p q n", p=P)),
                     (a_neg, a_log.rearrange("(q p) n -> p q n", p=P)), (dpar, d_param.rearrange("(q p) -> p q", p=P)),
                     (dtw, dt_w.rearrange("(q p) o -> p (q o)", p=P)), (dtb, dt_b.rearrange("(q p) -> p q", p=P)),
                     (out_w, out_w_t.rearrange("(q p) d -> p q d", p=P)),
                     (lng, ln_g.rearrange("(q p) -> p q", p=P)), (lnb, ln_b.rearrange("(q p) -> p q", p=P)),
                     (sel, sel_in)]
            with nc.Block() as block:
                @block.sync
                def _(sp):
                    for dst, src in loads:
                        with nc.allow_non_contiguous_dma("a few small vectors"):
                            sp.dma_start(dst[tuple([slice(None)] * len(dst.shape))], src).then_inc(weights_in, 16)
                    sp.wait_ge(weights_in, 16 * len(loads))

                @block.vector
                def _(dve):
                    vec(dve)
                    dve.memset(mean_w[:, :], 1.0 / INNER).then_inc(small_set, 1)
                    dve.wait_ge(weights_in, 16 * len(loads))
                    for q in range(Q):
                        dve.tensor_scalar(d_diag[:, q, :], ident[:, :], dpar[:, q:q + 1], None, ALU.mult).then_inc(small_set, 1)

                @block.scalar
                def _(act):
                    sca(act)
                    act.wait_ge(weights_in, 16 * len(loads))
                    act.activation(a_neg[:, :, :], a_neg[:, :, :], ACT.Exp).then_inc(a_exp, 1)
                    act.wait_ge(a_exp, 1)
                    act.mul(a_neg[:, :, :], a_neg[:, :, :], -1.0).then_inc(a_done, 1)

                @block.tensor
                def _(pe):
                    ten(pe)
            ln_st.close()

            xpad = sb(st, "xpad", [P, Q, CB, PADDED])
            xb = sb(st, "xb", [P, Q, CHUNK])
            sz = sb(st, "sz", [P, Q, CHUNK])
            dt = sb(st, "dt", [P, 2, Q, CHUNK])
            xdt = sb(st, "xdt", [P, 2, Q, CHUNK])
            yc = sb(st, "yc", [P, Q, CHUNK])
            sq = sb(st, "sq", [P, Q, CHUNK])
            y_inv = sb(st, "y_inv", [P, CHUNK])
            bc_parts = sb(st, "bc_parts", [6 * STATE, 2, CHUNK], BF16)
            bc_mid = sb(st, "bc_mid", [2 * STATE, CHUNK], BF16)
            bc_rest = sb(st, "bc_rest", [2 * STATE, CHUNK])
            b_sb = [sb(st, f"b_sb{s}", [P, CHUNK]) for s in range(4)]
            dA = [sb(st, f"dA{s}", [P, Q, CB, SEQ]) for s in range(2)]
            u = [sb(st, f"u{s}", [P, Q, CHUNK]) for s in range(4)]
            sel16 = sel[:, :, :].bitcast(BF16)
            CC, BB, WORK, YY = banks[0:2], banks[2], banks[3], banks[4:8]

            padded = sem("padding_zeroed")
            act_turn, pool_turn, dve_turn = sem("act_turn"), sem("pool_turn"), sem("dve_turn")
            in_done, in_copied = sem("in_proj_done"), sem("in_proj_copied")
            z_done, z_copied, z_silu = sem("z_done"), sem("z_copied"), sem("z_silu")
            conv_part, conv_done, xb_ready = sem("conv_part"), sem("conv_done"), sem("xb_ready")
            dt_done, bc_done = sem("dt_product_done"), sem("bc_product_done")
            dt_abs, dt_relu = sem("dt_abs"), sem("dt_relu")
            dt_z, dt_w, dt_r, dt_log = sem("dt_z"), sem("dt_one_plus_z"), sem("dt_rounding"), sem("dt_log")
            dt_log1p, dt_ready, xdt_ready = sem("dt_log1p"), sem("dt_ready"), sem("xdt_ready")
            part_step, parts_ready = sem("bc_part_step"), sem("bc_parts_ready")
            dx_done, y_copied = sem("dx_done"), sem("y_copied")
            b_done, c_done, b_copied = sem("b_spread"), sem("c_spread"), sem("b_copied")
            dA_ready, xs_ready, h_ready = sem("dA_ready"), sem("xs_ready"), sem("h_ready")
            hc_ready, hc_used = sem("hc_ready"), sem("hc_used")
            mean_done, yc_ready, sq_ready, var_done = sem("mean_done"), sem("yc_ready"), sem("sq_ready"), sem("var_done")
            ystd, yrstd, ynorm, yaff, yfin = sem("y_std"), sem("y_rstd"), sem("y_norm"), sem("y_affine"), sem("y_final")
            op_done, op_added = sem("out_proj_done"), sem("out_proj_added")

            def wait(engine, semaphore, n):
                if not (isinstance(n, int) and n <= 0):
                    engine.wait_ge(semaphore, n)

            def steps(engine, step):
                step(-1, False, True, False)
                step(0, True, True, False)
                with engine.Fori(1, CHUNKS - 1) as c:
                    step(c, True, True, True)
                step(CHUNKS - 1, True, False, True)
                step(CHUNKS, False, False, True)

            def z_slot(core):
                return 8 if core else 5

            def of(c, q):
                return (slice(None), bass.ds((c % 2) * Q + q, 1), slice(None))

            def flat(view):
                return view.rearrange("p o l -> p (o l)")

            def all_of(buffer, c):
                return buffer[:, bass.ds(c % 2, 1), :, :].rearrange("p s q l -> p (s q) l")

            dt_flat, xdt_flat = (v[:, :, :, :].rearrange("p s q l -> p (s q) l") for v in (dt, xdt))

            zero = sb(st, "zero", [P, DIM])
            zero_set, xs_zeroed = sem("zero_set"), sem("xs_zeroed")

            def add_log1p(engine, turn, c, q):
                log1p, step_q = flat(xdt_flat[of(c, q)]), flat(dt_flat[of(c, q)])
                engine.wait_ge(dt_log, c + 1)
                engine.sem_inc(turn, 1)
                engine.tensor_tensor(log1p, sq[:, q, :], log1p, ALU.subtract).then_inc(dt_log1p, 1)
                engine.wait_ge(dt_relu, Q * c + q + 1)
                engine.wait_ge(dt_log1p, Q * c + q + 1)
                engine.sem_inc(turn, 1)
                engine.tensor_tensor(step_q, step_q, log1p, ALU.add).then_inc(dt_ready, 1)

            with nc.Block() as block:
                @block.sync
                def _(sp):
                    sp.wait_ge(zero_set, 1)
                    sp.dma_start(xs_rows.rearrange("(p r) d -> p r d", p=P),
                                 zero[:, :].unsqueeze(1).broadcast_to([P, SLOT_TILES * SLOTS // P, DIM])).then_inc(xs_zeroed, 16)
                    sp.wait_ge(xs_zeroed, 16)

                @block.tensor
                def _(pe):
                    def parts(c):
                        return bc_parts[:, bass.ds(c % 2, 1), :].rearrange("k o l -> k (o l)")

                    def spread_b(c, n):
                        if n == 0:
                            pe.wait_ge(parts_ready, c + 1)
                        wait(pe, b_copied, STATE * c + n)
                        pe.matmul(BB[:, :], sel16[:, n, :], parts(c), start=True, stop=True).then_inc(b_done, 1)

                    def spread_c(c, n):
                        wait(pe, hc_ready, Q * (STATE * c + n) - Q)
                        pe.matmul(CC[n % 2][:, :], sel16[:, n + STATE, :], parts(c), start=True, stop=True).then_inc(c_done, 1)

                    def gather(c, n):
                        m = STATE * c + n
                        for q in range(Q):
                            pe.wait_ge(hc_ready, Q * m + q + 1)
                            pe.matmul(YY[q][:, :], ident[:, :], u[n % 4][:, q, :], start=False, stop=(n == STATE - 1),
                                      skip_group_check=True).then_inc(hc_used, 1)

                    def skip(c):
                        pe.wait_ge(xb_ready, Q * c + Q)
                        for q in range(Q):
                            wait(pe, y_copied, Q * c - Q + q + 1)
                            pe.matmul(YY[q][:, :], d_diag[:, q, :], xb[:, q, :], start=True, stop=False,
                                      skip_group_check=True).then_inc(dx_done, 1)

                    def in_proj(c, k, done, bank=WORK):
                        for h in range(HALVES):
                            mm = pe.matmul(bank[:, :], in_w[:, h, k * P:(k + 1) * P],
                                           xnT[:, h, bass.ds(c * CHUNK, CHUNK)], start=(h == 0), stop=(h == HALVES - 1))
                        mm.then_inc(done, 1)

                    def channels(weight, rows, values):
                        for q in range(Q):
                            mm = pe.matmul(WORK[0:rows, :], weight(q), values[:, q, :], start=(q == 0), stop=(q == Q - 1))
                        return mm

                    def out_proj(c, pair):
                        for t in range(2 * pair, 2 * pair + 2):
                            for q in range(Q):
                                mm = pe.matmul(WORK[:, t % 2 * DIM:(t % 2 + 1) * DIM], yc[:, q, t * P:(t + 1) * P],
                                               out_w[:, q, :], start=(q == 0), stop=(q == Q - 1))
                        mm.then_inc(op_done, 1)

                    def step(c, core, pre, post):
                        z0 = z_slot(core)
                        for n in range(STATE):
                            if core:
                                if n == 0:
                                    skip(c)
                                gather(c, n)
                            if n < STATE - 3 and core:
                                spread_b(c, n + 3)
                            if n >= STATE - 3 and pre:
                                spread_b(c + 1, n + 3 - STATE)
                            if n < STATE - 2 and core:
                                spread_c(c, n + 2)
                            if n >= STATE - 2 and pre:
                                spread_c(c + 1, n + 2 - STATE)
                            if pre and n < Q:
                                if n > 0:
                                    pe.wait_ge(in_copied, Q * c + Q + n)
                                in_proj(c + 1, n, in_done)
                            if post and n == 4:
                                if pre:
                                    pe.wait_ge(in_copied, Q * c + 2 * Q)
                                if not core:
                                    pe.wait_ge(op_added, 2 * c - 2)
                                pe.wait_ge(y_copied, Q * c)
                                channels(lambda q: mean_w[:, :], P, yc).then_inc(mean_done, 1)
                            if pre and n == 5:
                                if post:
                                    pe.wait_ge(yc_ready, Q * c)
                                pe.wait_ge(in_copied, Q * c + 2 * Q)
                                pe.wait_ge(xb_ready, Q * c + 2 * Q)
                                channels(lambda q: bc_w[:, q, :], 2 * STATE, xb).then_inc(bc_done, 1)
                            if pre and n == 6:
                                pe.wait_ge(part_step, 5 * c + 5 + 2)
                                channels(lambda q: dt_row[:, q, :], P, xb).then_inc(dt_done, 1)
                            if post and n == 7:
                                if pre:
                                    pe.wait_ge(dt_abs, Q * c + 2 * Q)
                                    pe.wait_ge(dt_relu, Q * c + 2 * Q)
                                pe.wait_ge(sq_ready, Q * c)
                                channels(lambda q: mean_w[:, :], P, sq).then_inc(var_done, 1)
                            if post and z0 <= n < z0 + Q:
                                if core and n == z0:
                                    pe.wait_ge(ystd, c)
                                elif core:
                                    pe.wait_ge(z_copied, Q * c - Q + n - z0)
                                in_proj(c - 1, Q + n - z0, z_done, WORK if core else YY[n - z0])
                            if post and n == 13:
                                pe.wait_ge(z_copied, Q * c)
                                pe.wait_ge(yfin, Q * c)
                                out_proj(c - 1, 0)
                            if post and n == 14:
                                pe.wait_ge(op_added, 2 * c - 1)
                                out_proj(c - 1, 1)

                    pe.wait_ge(small_set, 1 + Q)
                    steps(pe, step)

                @block.scalar
                def _(act):
                    def copy_b(c, n):
                        m = STATE * c + n
                        act.wait_ge(b_done, m + 1)
                        wait(act, xs_ready, Q * (m - 3))
                        act.copy(b_sb[n % 4][:, :], BB[:, :]).then_inc(b_copied, 1)

                    def decays(c, n):
                        m = STATE * c + n
                        if n == 0:
                            act.wait_ge(dt_ready, Q * c + Q)
                        wait(act, h_ready, Q * m - Q)
                        act.sem_inc(act_turn, 1)
                        for q in range(Q):
                            act.activation(dA[n % 2][:, q, :, 1:SEQ],
                                           flat(dt_flat[of(c, q)]).rearrange("p (b l) -> p b l", l=SEQ)[:, :, 1:SEQ],
                                           ACT.Exp, scale=a_neg[:, q, n:n + 1]).then_inc(dA_ready, 1)

                    def step(c, core, pre, post):
                        z0 = z_slot(core)
                        for n in range(STATE):
                            if post and n == 0:
                                for q in range(Q):
                                    act.wait_ge(hc_used, Q * (STATE * c - 1) + q + 1)
                                    act.copy(yc[:, q, :], YY[q][:, :]).then_inc(y_copied, 1)
                            if n < STATE - 2 and core:
                                copy_b(c, n + 2)
                            if n >= STATE - 2 and pre:
                                copy_b(c + 1, n + 2 - STATE)
                            if n < STATE - 1 and core:
                                decays(c, n + 1)
                            if n == STATE - 1 and pre:
                                decays(c + 1, 0)
                            if pre and 1 <= n <= Q:
                                q = n - 1
                                act.wait_ge(in_done, Q * c + Q + n)
                                wait(act, conv_done, Q * c + n)
                                act.copy(xpad[:, q, :, TAPS - 1:PADDED],
                                         WORK[:, :].rearrange("p (b l) -> p b l", l=SEQ)).then_inc(in_copied, 1)
                            if pre and n == 5:
                                for q in range(Q):
                                    act.wait_ge(conv_done, Q * c + Q + q + 1)
                                    act.activation(xb[:, q, :], xb[:, q, :], ACT.Silu).then_inc(xb_ready, 1)
                            if post and n == 6:
                                wait(act, dt_log1p, Q * c + Q if pre else Q * CHUNKS)
                                for q in range(Q):
                                    act.wait_ge(yc_ready, Q * c - Q + q + 1)
                                    act.activation(sq[:, q, :], yc[:, q, :], ACT.Square).then_inc(sq_ready, 1)
                            if pre and n == 7:
                                act.wait_ge(dt_done, c + 2)
                                wait(act, xs_ready, Q * STATE * c)
                                wait(act, dA_ready, Q * STATE * c)
                                act.sem_inc(act_turn, 1)
                                for q in range(Q):
                                    act.activation(flat(xdt_flat[of(c + 1, q)]), WORK[:, :], ACT.Abs, bias=dtb[:, q:q + 1],
                                                   scale=dtw[:, q:q + 1]).then_inc(dt_abs, 1)
                                    act.activation(flat(dt_flat[of(c + 1, q)]), WORK[:, :], ACT.Relu, bias=dtb[:, q:q + 1],
                                                   scale=dtw[:, q:q + 1]).then_inc(dt_relu, 1)
                            if pre and n == 8:
                                act.wait_ge(dt_abs, Q * c + 2 * Q)
                                act.sem_inc(act_turn, 1)
                                z = all_of(xdt, c + 1)
                                act.activation(z, z, ACT.Exp, scale=-1.0).then_inc(dt_z, 1)
                            if post and n == 8:
                                act.wait_ge(var_done, c)
                                act.activation(y_inv[:, :], WORK[:, :], ACT.Sqrt, bias=epsc[:, 0:1]).then_inc(ystd, 1)
                            if post and z0 < n <= z0 + Q:
                                act.wait_ge(z_done, Q * c - Q + n - z0)
                                act.copy(sz[:, n - z0 - 1, :], (WORK if core else YY[n - z0 - 1])[:, :]).then_inc(z_copied, 1)
                            if pre and n == 10:
                                act.wait_ge(dt_r, c + 2)
                                act.activation(sq[:, :, :], sq[:, :, :], ACT.Ln).then_inc(dt_log, 1)
                            if post and n == 10:
                                for q in range(Q):
                                    act.wait_ge(ynorm, Q * c - Q + q + 1)
                                    act.activation(yc[:, q, :], yc[:, q, :], ACT.Identity, bias=lnb[:, q:q + 1],
                                                   scale=lng[:, q:q + 1]).then_inc(yaff, 1)
                            if post and n == z0 + Q:
                                act.wait_ge(z_copied, Q * c)
                                act.activation(sz[:, :, :], sz[:, :, :], ACT.Silu).then_inc(z_silu, 1)

                    act.wait_ge(padded, 3)
                    steps(act, step)

                @block.vector
                def _(dve):
                    dve.memset(xpad[:, :, :, 0:TAPS - 1], 0.0).then_inc(padded, 1)
                    dve.memset(zero[:, :], 0.0).then_inc(zero_set, 1)
                    for s in range(2):
                        dve.memset(dA[s][:, :, :, 0:1], 0.0).then_inc(padded, 1)

                    def scans(c, n):
                        m = STATE * c + n
                        for q in range(Q):
                            dve.wait_ge(dA_ready, Q * m + q + 1)
                            dve.wait_ge(xs_ready, Q * m + q + 1)
                            dve.tensor_tensor_scan(u[n % 4][:, q, :], dA[n % 2][:, q, :, :].rearrange("p b l -> p (b l)"),
                                                   u[n % 4][:, q, :], 0.0, ALU.mult, ALU.add).then_inc(h_ready, 1)

                    def times_c(c, n):
                        m = STATE * c + n
                        dve.wait_ge(c_done, m + 1)
                        for q in range(Q):
                            dve.wait_ge(h_ready, Q * m + q + 1)
                            dve.tensor_tensor(u[n % 4][:, q, :], u[n % 4][:, q, :], CC[n % 2][:, :], ALU.mult).then_inc(hc_ready, 1)

                    def convolve(c, q):
                        dve.wait_ge(in_copied, Q * c + q + 1)
                        row = xb[:, q, :].rearrange("p (b l) -> p b l", l=SEQ)
                        if q == 0:
                            wait(dve, dx_done, Q * c)
                            wait(dve, xdt_ready, Q * c)
                        dve.tensor_scalar(row, xpad[:, q, :, 0:SEQ], cw[:, q, 0:1], cb[:, q:q + 1],
                                          ALU.mult, ALU.add).then_inc(conv_part, 1)
                        for k in range(1, TAPS):
                            dve.wait_ge(conv_part, (Q * c + q) * (TAPS - 1) + k)
                            dve.scalar_tensor_tensor(row, xpad[:, q, :, k:k + SEQ], cw[:, q, k:k + 1], row,
                                                     ALU.mult, ALU.add).then_inc(conv_part if k < TAPS - 1 else conv_done, 1)

                    def split(c):
                        dve.wait_ge(bc_done, c + 1)
                        wait(dve, c_done, STATE * c - STATE)
                        bank = WORK[0:2 * STATE, :]
                        hi, mid, lo = (bc_parts[2 * STATE * k:2 * STATE * (k + 1), bass.ds(c % 2, 1), :].rearrange("k o l -> k (o l)")
                                       for k in range(3))
                        base = 5 * c
                        dve.tensor_copy(hi, bank).then_inc(part_step, 1)
                        dve.wait_ge(part_step, base + 1)
                        dve.tensor_tensor(bc_rest[:, :], bank, hi, ALU.subtract).then_inc(part_step, 1)
                        dve.wait_ge(part_step, base + 2)
                        dve.tensor_copy(bc_mid[:, :], bc_rest[:, :]).then_inc(part_step, 1)
                        dve.wait_ge(part_step, base + 3)
                        dve.tensor_copy(mid, bc_mid[:, :]).then_inc(part_step, 1)
                        dve.tensor_tensor(bc_rest[:, :], bc_rest[:, :], bc_mid[:, :], ALU.subtract).then_inc(part_step, 1)
                        dve.wait_ge(part_step, base + 5)
                        dve.tensor_copy(lo, bc_rest[:, :]).then_inc(parts_ready, 1)

                    def add(c, pair):
                        dve.wait_ge(op_done, 2 * c + pair + 1)
                        rows = xres[:, bass.ds(CHUNK // P * c + 2 * pair, 2), :].rearrange("p t d -> p (t d)")
                        dve.tensor_tensor(rows, rows, WORK[:, :], ALU.add).then_inc(op_added, 1)

                    def step(c, core, pre, post):
                        for n in range(STATE):
                            if core:
                                scans(c, n)
                            if post and n == 5:
                                dve.wait_ge(mean_done, c)
                                for q in range(Q):
                                    dve.tensor_tensor(yc[:, q, :], yc[:, q, :], WORK[:, :], ALU.subtract).then_inc(yc_ready, 1)
                            if core:
                                times_c(c, n)
                            if pre and n == 2:
                                convolve(c + 1, 0)
                            if pre and 2 <= n <= Q:
                                convolve(c + 1, n - 1)
                            if pre and n == 6:
                                split(c + 1)
                            if post and n == 9:
                                dve.wait_ge(ystd, c)
                                dve.reciprocal(y_inv[:, :], y_inv[:, :]).then_inc(yrstd, 1)
                                dve.wait_ge(yrstd, c)
                                dve.wait_ge(sq_ready, Q * c)
                                for q in range(Q):
                                    dve.tensor_tensor(yc[:, q, :], yc[:, q, :], y_inv[:, :], ALU.mult).then_inc(ynorm, 1)
                            if pre and n == 9:
                                z = all_of(xdt, c + 1)
                                dve.wait_ge(dt_z, c + 2)
                                if post:
                                    dve.wait_ge(var_done, c)
                                wait(dve, dt_log1p, Q * c + Q)
                                dve.tensor_scalar(sq[:, :, :], z, 1.0, None, ALU.add).then_inc(dt_w, 1)
                                dve.wait_ge(dt_w, c + 2)
                                dve.scalar_tensor_tensor(z, sq[:, :, :], -1.0, z, ALU.add, ALU.subtract).then_inc(dt_r, 1)
                            if post and n == 13:
                                dve.wait_ge(z_silu, c)
                                for q in range(Q):
                                    dve.wait_ge(yaff, Q * c - Q + q + 1)
                                    dve.tensor_tensor(yc[:, q, :], yc[:, q, :], sz[:, q, :], ALU.mult).then_inc(yfin, 1)
                            if post and n == 14:
                                add(c - 1, 0)
                            if pre and not core and n == 14:
                                for q in range(Q):
                                    add_log1p(dve, dve_turn, c + 1, q)
                            if pre and n == 14:
                                for q in range(Q):
                                    dve.wait_ge(dt_ready, Q * c + Q + q + 1)
                                    dve.tensor_tensor(flat(xdt_flat[of(c + 1, q)]), xb[:, q, :], flat(dt_flat[of(c + 1, q)]),
                                                      ALU.mult).then_inc(xdt_ready, 1)
                            if post and n == 15:
                                add(c - 1, 1)

                    steps(dve, step)

                @block.gpsimd
                def _(pool):
                    def states(c, n):
                        m = STATE * c + n
                        if n == 0:
                            pool.wait_ge(xdt_ready, Q * c + Q)
                        pool.wait_ge(b_copied, m + 1)
                        wait(pool, hc_used, Q * (m - 3))
                        pool.sem_inc(pool_turn, 1)
                        for q in range(Q):
                            pool.tensor_tensor(u[n % 4][:, q, :], flat(xdt_flat[of(c, q)]), b_sb[n % 4][:, :],
                                               ALU.mult).then_inc(xs_ready, 1)

                    def step(c, core, pre, post):
                        for n in range(STATE):
                            if n < STATE - 2 and core:
                                states(c, n + 2)
                            if n >= STATE - 2 and pre:
                                states(c + 1, n + 2 - STATE)
                            if pre and core and 10 <= n < 10 + Q:
                                add_log1p(pool, pool_turn, c + 1, n - 10)

                    steps(pool, step)

        end_of_stage()

        with ExitStack() as st:
            X = EXPERTS
            gate_w = sb(st, "gate_w", [P, HALVES, X])
            consts = sb(st, "consts", [P, 2 * SLOT_TILES + X])
            tri = sb(st, "tri", [P, P])
            ones = sb(st, "ones", [P, P])
            pos_u = [sb(st, f"pos{k}", [P, TILES], U32) for k in range(TOPK)]
            share = [sb(st, f"share{k}", [P, TILES]) for k in range(TOPK)]
            eid_u = sb(st, "eid_u", [P, SLOT_TILES], U32)
            xh = [sb(st, f"xn_{n}", [P, HALVES, TOKENS], F16) for n in ("hi", "lo")]
            raw = [sb(st, f"raw_gu{h}", [P, 2 * FG * FP]) for h in range(HALVES)] + [sb(st, "raw_down", [FP, FG, DIM])]
            gu = [[sb(st, f"gu_{n}{w}", [P, HALVES, 2 * FG * FP], F16) for n in ("hi", "lo")] for w in range(2)]
            down = [[sb(st, f"down_{n}{w}", [FP, FG, DIM], F16) for n in ("hi", "lo")] for w in range(2)]
            consts_in, xsplit = sem("router_constants_in"), sem("xn_split")
            eids_ready, one_set = sem("slot_experts_known"), sem("ones_set")
            raw_in = [sem(f"raw_in{k}") for k in range(3)]
            w_hi = [sem(f"weights_hi{k}") for k in range(3)]
            w_lo = [sem(f"weights_lo{k}") for k in range(3)]
            scattered = sem("rows_scattered")
            small_st = ExitStack()
            vec, sca, ten, ln_copied = layernorm("c", st)
            xn = ten_rows[0]
            wide_ = [P, TILES, X]
            probs = sb(small_st, "probs", wide_)
            hot = [sb(small_st, f"hot{k}", wide_) for k in range(TOPK)]
            work = sb(small_st, "work", wide_)
            chosen = sb(small_st, "chosen", wide_)
            slot_of = sb(small_st, "slot_of", wide_)
            lmax = sb(small_st, "lmax", [P, TILES])
            top = sb(small_st, "top", [P, TILES, 8])
            topi = sb(small_st, "topi", [P, TILES, 8], U32)
            topf = sb(small_st, "topf", [P, TILES, 8])
            shifted = sb(small_st, "shifted", [P, X, TILES])
            carry = sb(small_st, "carry", [P, X, TILES])
            before = sb(small_st, "before", [P, X, TILES])
            count = sb(small_st, "count", [P, X])
            cmp = sb(small_st, "cmp", [P, SLOT_TILES, X])
            tiles_of = sb(small_st, "tiles_of", [P, X])
            tiles_sh = sb(small_st, "tiles_sh", [P, X])
            first_tile = sb(small_st, "first_tile", [P, X])
            end_tile = sb(small_st, "end_tile", [P, X])
            eid = sb(small_st, "eid", [P, SLOT_TILES])
            ones_x = sb(small_st, "ones_x", [P, X])
            logits_done, rstep, expd = sem("logits_done"), sem("router_step"), sem("router_exp")
            chosen_ready, ranks_done = sem("chosen_ready"), sem("ranks_done")
            BIG = 2 * FG * FP

            def load_raw(sp, k, row):
                if k < HALVES:
                    sp.dma_start(raw[k][:, :], gu_t[bass.ds(row * DIM + k * P, P), :]).then_inc(raw_in[k], 16)
                else:
                    sp.dma_start(raw[2][:, :, :], down_t[bass.ds(row * FG * FP, FG * FP), :]
                                 .rearrange("(g p) d -> p g d", p=FP)).then_inc(raw_in[2], 16)

            with nc.Block() as block:
                @block.sync
                def _(sp):
                    sp.dma_start(gate_w[:, :, :], gate_w_t.rearrange("(h p) e -> p h e", p=P)).then_inc(consts_in, 16)
                    sp.dma_start(consts[:, :], consts_t).then_inc(consts_in, 16)
                    sp.dma_start(tri[:, :], tri_in).then_inc(consts_in, 16)
                    for k in range(3):
                        load_raw(sp, k, 0)
                    for k in range(3):
                        sp.wait_ge(raw_in[k], 16)
                    sp.wait_ge(consts_in, 48)

                @block.gpsimd
                def _(pool):
                    for k in range(HALVES):
                        pool.wait_ge(raw_in[k], 16)
                        pool.tensor_scalar(gu[0][0][:, k, :], raw[k][:, :], GU_SCALE, None, ALU.mult).then_inc(w_hi[k], 1)

                @block.tensor
                def _(pe):
                    ten(pe)
                    pe.wait_ge(consts_in, 48)
                    pe.wait_ge(ln_copied, TILES // 2)
                    for t in range(TILES):
                        for h in range(HALVES):
                            mm = pe.matmul(banks[2][:, t * X:(t + 1) * X], xnT[:, h, t * P:(t + 1) * P],
                                           gate_w[:, h, :], start=(h == 0), stop=(h == HALVES - 1))
                    mm.then_inc(logits_done, 1)
                    pe.wait_ge(chosen_ready, 1)
                    pe.wait_ge(one_set, 1)
                    flat = chosen[:, :, :].rearrange("p t e -> p (t e)")
                    pe.matmul(banks[3][:, 0:TILES * X], tri[:, :], flat, start=True, stop=True)
                    pe.matmul(banks[4][:, 0:TILES * X], ones[:, :], flat, start=True, stop=True).then_inc(ranks_done, 1)

                @block.scalar
                def _(act):
                    sca(act)
                    act.wait_ge(rstep, 2)
                    act.activation(probs[:, :, :], probs[:, :, :], ACT.Exp).then_inc(expd, 1)

                @block.vector
                def _(dve):
                    dve.memset(ones[:, :], 1.0).then_inc(one_set, 1)
                    vec(dve)
                    step = Count(rstep)

                    def do(instruction):
                        dve.wait_ge(rstep, step.inc(instruction))

                    def wide(a):
                        return a.unsqueeze(2).broadcast_to(wide_)

                    logits = banks[2][:, 0:TILES * X].rearrange("p (t e) -> p t e", e=X)
                    for g in range(TILES // 2):
                        cols = slice(g * 2 * P, (g + 1) * 2 * P)
                        dve.wait_ge(ln_copied, g + 1)
                        dve.tensor_copy(xh[0][:, :, cols], xnT[:, :, cols]).then_inc(xsplit, 1)
                        dve.wait_ge(xsplit, g + 1)
                        dve.tensor_tensor(xh[1][:, :, cols], xnT[:, :, cols], xh[0][:, :, cols], ALU.subtract)
                    for k in range(HALVES):
                        dve.wait_ge(w_hi[k], 1)
                        dve.scalar_tensor_tensor(gu[0][1][:, k, :], raw[k][:, :], GU_SCALE, gu[0][0][:, k, :],
                                                 ALU.mult, ALU.subtract).then_inc(w_lo[k], 1)
                    dve.wait_ge(logits_done, 1)
                    do(dve.tensor_reduce(lmax[:, :], logits, AX.X, ALU.max))
                    do(dve.tensor_tensor(probs[:, :, :], logits, wide(lmax[:, :]), ALU.subtract))
                    dve.wait_ge(expd, 1)
                    do(dve.tensor_reduce(lmax[:, :], probs[:, :, :], AX.X, ALU.add))
                    do(dve.reciprocal(lmax[:, :], lmax[:, :]))
                    do(dve.tensor_tensor(probs[:, :, :], probs[:, :, :], wide(lmax[:, :]), ALU.mult))
                    for t in range(TILES):
                        step.inc(dve.max(top[:, t, :], probs[:, t, :]))
                    dve.wait_ge(rstep, step.n)
                    for t in range(TILES):
                        step.inc(dve.max_index(topi[:, t, :], top[:, t, :], probs[:, t, :]))
                    dve.wait_ge(rstep, step.n)
                    do(dve.tensor_copy(topf[:, :, :], topi[:, :, :]))
                    do(dve.tensor_tensor(lmax[:, :], top[:, :, 0], top[:, :, 1], ALU.add))
                    do(dve.tensor_scalar(lmax[:, :], lmax[:, :], 1e-8, None, ALU.add))
                    do(dve.reciprocal(lmax[:, :], lmax[:, :]))
                    nums = consts[:, 0:X].unsqueeze(1).broadcast_to(wide_)
                    for k in range(TOPK):
                        do(dve.tensor_tensor(share[k][:, :], top[:, :, k], lmax[:, :], ALU.mult))
                        do(dve.tensor_tensor(hot[k][:, :, :], nums, wide(topf[:, :, k]), ALU.is_equal))
                    dve.tensor_tensor(chosen[:, :, :], hot[0][:, :, :], hot[1][:, :, :], ALU.add).then_inc(chosen_ready, 1)
                    ranks = banks[3][:, 0:TILES * X].rearrange("p (t e) -> p t e", e=X)
                    totals = banks[4][:, 0:TILES * X].rearrange("p (t e) -> p e t", e=X)
                    do(dve.memset(shifted[:, :, 0:1], 0.0))
                    do(dve.memset(carry[:, :, 1:TILES], 1.0))
                    do(dve.memset(carry[:, :, 0:1], 0.0))
                    do(dve.memset(ones_x[:, :], 1.0))
                    do(dve.memset(tiles_sh[:, :], 0.0))
                    dve.wait_ge(ranks_done, 1)
                    do(dve.tensor_copy(shifted[:, :, 1:TILES], totals[:, :, 0:TILES - 1]))
                    do(dve.tensor_tensor_scan(before[:, :, :].rearrange("p e t -> p (e t)"),
                                              carry[:, :, :].rearrange("p e t -> p (e t)"),
                                              shifted[:, :, :].rearrange("p e t -> p (e t)"), 0.0, ALU.mult, ALU.add))
                    do(dve.tensor_tensor(count[:, :], before[:, :, TILES - 1], totals[:, :, TILES - 1], ALU.add))
                    do(dve.tensor_tensor(cmp[:, 0:X, :], count[:, :].unsqueeze(2).broadcast_to([P, X, X]),
                                         consts[:, 2 * SLOT_TILES:].unsqueeze(1).broadcast_to([P, X, X]), ALU.is_gt))
                    do(dve.tensor_reduce(tiles_of[:, :], cmp[:, 0:X, :], AX.X, ALU.add))
                    do(dve.tensor_copy(tiles_sh[:, 1:X], tiles_of[:, 0:X - 1]))
                    do(dve.tensor_tensor_scan(first_tile[:, :], ones_x[:, :], tiles_sh[:, :], 0.0, ALU.mult, ALU.add))
                    do(dve.tensor_tensor(end_tile[:, :], first_tile[:, :], tiles_of[:, :], ALU.add))
                    do(dve.tensor_tensor(slot_of[:, :, :], ranks, before[:, :, :].rearrange("p e t -> p t e"), ALU.add))
                    do(dve.tensor_scalar(first_tile[:, :], first_tile[:, :], float(SLOTS), None, ALU.mult))
                    do(dve.tensor_tensor(slot_of[:, :, :], slot_of[:, :, :], first_tile[:, :].unsqueeze(1).broadcast_to(wide_), ALU.add))
                    for k in range(TOPK):
                        do(dve.tensor_tensor(work[:, :, :], slot_of[:, :, :], hot[k][:, :, :], ALU.mult))
                        do(dve.tensor_reduce(lmax[:, :], work[:, :, :], AX.X, ALU.add))
                        do(dve.tensor_copy(pos_u[k][:, :], lmax[:, :]))
                    both = [P, SLOT_TILES, X]
                    do(dve.tensor_tensor(cmp[:, :, :], end_tile[:, :].unsqueeze(1).broadcast_to(both),
                                         consts[:, 0:SLOT_TILES].unsqueeze(2).broadcast_to(both), ALU.is_le))
                    do(dve.tensor_reduce(eid[:, :], cmp[:, :, :], AX.X, ALU.add))
                    do(dve.tensor_scalar(eid[:, :], eid[:, :], float(X - 1), 1.0, ALU.min, ALU.add))
                    dve.tensor_copy(eid_u[:, :], eid[:, :]).then_inc(eids_ready, 1)
                    dve.wait_ge(eids_ready, 1)
            small_st.close()

            xs_in_sb = [sb(st, f"xs_in{p}", [P, 2, DIM]) for p in range(2)]
            xsT = [[sb(st, f"xsT_{n}{p}", [P, HALVES, SLOTS], F16) for n in ("hi", "lo")] for p in range(2)]
            sg = [sb(st, f"sg{b}", [FP, 2, SLOTS]) for b in range(2)]
            h32 = [sb(st, f"h32_{b}", [FP, 2, SLOTS]) for b in range(2)]
            hh = [[sb(st, f"h_{n}{p}", [FP, FG, SLOTS], F16) for n in ("hi", "lo")] for p in range(2)]
            ysb = [sb(st, f"ysb{p}", [P, 2, DIM]) for p in range(2)]
            AHEAD = 8
            yg = [sb(st, f"yg{b}", [P, DIM]) for b in range(AHEAD)]
            xs_in = [sem(f"xs_in{p}") for p in range(2)]
            xs_turned = [sem(f"xs_turned{p}") for p in range(2)]
            xs_hi = [sem(f"xs_hi{p}") for p in range(2)]
            xs_lo = [sem(f"xs_lo{p}") for p in range(2)]
            g_done = [sem(f"gate_up_done{b}") for b in range(2)]
            sg_ready = [sem(f"gate_silu{b}") for b in range(2)]
            h32_ready = [sem(f"hidden{b}") for b in range(2)]
            h_hi = [sem(f"hidden_hi{b}") for b in range(2)]
            h_lo = [sem(f"hidden_lo{b}") for b in range(2)]
            d_done = [sem(f"down_done{t}") for t in range(2)]
            d_taken = [sem(f"down_taken{t}") for t in range(2)]
            ys_out = [sem(f"ys_out{p}") for p in range(2)]
            y_in = [sem(f"y_gathered{b}") for b in range(AHEAD)]
            y_added, stored = sem("y_added"), sem("stored")
            GB, UB, DB, TB = banks[0:2], banks[2:4], banks[4:6], banks[6:8]
            PASSES = ((0, 0), (0, 1), (1, 0))
            PAIRS_F = FG // 2
            SH = TOKENS // SLOTS // 2
            E0, E1 = SH, SH + SLOT_TILES
            LAST = E1 + SH
            COMBINED = {E1 + 1: (0, 2, 5, 8), E1 + 2: (10, 13, 16, 18), E1 + 3: (20, 22, 24, 26)}

            def place(m):
                unit = 0 if m < E0 else min(m, E1) - SH + 1
                return m % 2, unit, unit % 2

            def slot_tiles_to(half, p):
                return half - (E0 if E0 % 2 == p else E0 + 1) // 2

            def windows(window):
                def kind(m):
                    return "slot" if E0 <= m < E1 else "shared"

                def one(m):
                    p, u, w = place(m)
                    window(m, m // 2, p, u, w, kind(m), kind(m - 1) if m else None, kind(m + 1) if m + 1 < LAST else None,
                           m in (0, E1) or kind(m) == "slot", m)
                for m in range(E0 + 1):
                    one(m)
                pairs = (E1 - 1 - (E0 + 1)) // 2
                return one, pairs

            def run_windows(engine, window):
                one, pairs = windows(window)
                with engine.Fori(0, pairs) as k:
                    for s in range(2):
                        m0 = E0 + 1 + s
                        m = 2 * k + m0
                        window(m, k + m0 // 2, m0 % 2, m - SH + 1, (m0 - SH + 1) % 2, "slot", "slot", "slot", True, None)
                for m in range(E0 + 1 + 2 * pairs, LAST):
                    one(m)

            with nc.Block() as block:
                @block.sync
                def _(sp):
                    def load_rows(j, p):
                        sp.dma_start(xs_in_sb[p][:, :, :], xs_rows[bass.ds(j * SLOTS, SLOTS), :]
                                     .rearrange("(t p) d -> p t d", p=P)).then_inc(xs_in[p], 16)

                    def window(m, half, p, u, w, kind, prev, nxt, opens, static):
                        def expert(unit):
                            return sp.value_load(eid_u[0:1, bass.ds(unit - 1, 1)], min_val=1, max_val=EXPERTS)

                        if opens:
                            own = 0 if static in (0, E1) else expert(u)
                            nxt_own = 0 if static in (E1 - 1, E1) else expert(u + 1)
                            if static != 0:
                                sp.wait_ge(w_lo[2], u)
                                load_raw(sp, 2, own)
                            if static != E1:
                                for h in range(HALVES):
                                    sp.wait_ge(w_lo[h], u + 1)
                                    load_raw(sp, h, nxt_own)
                        if static is None or E0 <= static + 2 < E1:
                            if static == E0 - 2:
                                sp.wait_ge(scattered, 16 * TILES * TOPK)
                            if static is None or static + 2 >= E0 + 2:
                                sp.wait_ge(xs_turned[p], slot_tiles_to(half, p) + 1)
                            load_rows(m + 2 - SH, p)

                    run_windows(sp, window)
                    for a, b in ((0, TILES // 2), (TILES // 2, TILES - 2), (TILES - 2, TILES)):
                        sp.wait_ge(y_added, TOPK * b)
                        if b > TILES // 2:
                            for t in range(2):
                                sp.wait_ge(d_taken[t], LAST - (b < TILES))
                        sp.dma_start(out[a * P:b * P, :].rearrange("(i p) d -> p i d", p=P), xres[:, a:b, :]).then_inc(stored, 16)
                    sp.wait_ge(stored, 48)

                @block.tensor
                def _(pe):
                    def wait(semaphore, n):
                        if not (isinstance(n, int) and n <= 0):
                            pe.wait_ge(semaphore, n)

                    def turn(c, p):
                        pe.wait_ge(xs_in[p], 16 * c + 16)
                        wait(xs_lo[p], c)
                        for h in range(HALVES):
                            for t in range(2):
                                at = (h * 2 + t) * P
                                mm = pe.transpose(TB[p][:, at:at + P], xs_in_sb[p][:, t, h * P:(h + 1) * P], ident[:, :])
                        mm.then_inc(xs_turned[p], 1)

                    def hidden(m, half, p, u, w, kind, opens):
                        if opens:
                            for k in range(HALVES):
                                pe.wait_ge(w_lo[k], u + 1)
                        if kind == "slot":
                            pe.wait_ge(xs_lo[p], slot_tiles_to(half, p) + 1)
                            rows = [x[:, :, :] for x in xsT[p]]
                        else:
                            at = (m if m < E0 else m - SLOT_TILES) * SLOTS
                            rows = [x[:, :, at:at + SLOTS] for x in xh]
                        for g in range(PAIRS_F):
                            b = g % 2
                            wait(h32_ready[b], 2 * m + g // 2)
                            for bank, off in ((GB[b], 0), (UB[b], FG * FP)):
                                for f in range(2):
                                    col = off + (2 * g + f) * FP
                                    n = 0
                                    for h in range(HALVES):
                                        for wp, xp in PASSES:
                                            mm = pe.matmul(bank[0:FP, f * SLOTS:(f + 1) * SLOTS], gu[w][wp][:, h, col:col + FP],
                                                           rows[xp][:, h, :], start=(n == 0), stop=(n == 3 * HALVES - 1))
                                            n += 1
                            mm.then_inc(g_done[b], 1)

                    def project(m, p, u, w):
                        pe.wait_ge(w_lo[2], u + 1)
                        for b in range(2):
                            pe.wait_ge(h_lo[b], 2 * m + 2)
                        for t in range(2):
                            wait(d_taken[t], m)
                            n = 0
                            for g in range(FG):
                                for wp, hp in PASSES:
                                    mm = pe.matmul(DB[t][:, 0:DIM], hh[p][hp][:, g, t * P:(t + 1) * P], down[w][wp][:, g, :],
                                                   start=(n == 0), stop=(n == 3 * FG - 1))
                                    n += 1
                            mm.then_inc(d_done[t], 1)

                    def window(m, half, p, u, w, kind, prev, nxt, opens, static):
                        if nxt == "slot":
                            turn(slot_tiles_to(half + p, 1 - p), 1 - p)
                        hidden(m, half, p, u, w, kind, opens)
                        if prev:
                            pp, pu, pw = place(m - 1) if static is not None else (1 - p, u - 1, 1 - w)
                            project(m - 1, pp, pu, pw)

                    run_windows(pe, window)
                    project(LAST - 1, *place(LAST - 1))

                @block.scalar
                def _(act):
                    def wait(semaphore, n):
                        if not (isinstance(n, int) and n <= 0):
                            act.wait_ge(semaphore, n)

                    def split_hi(k, u, w):
                        act.wait_ge(raw_in[k], 16 * u + 16)
                        if k < HALVES:
                            act.mul(gu[w][0][:, k, :], raw[k][:, :], GU_SCALE).then_inc(w_hi[k], 1)
                        else:
                            act.mul(down[w][0][:, :, :], raw[2][:, :, :], DOWN_SCALE).then_inc(w_hi[2], 1)

                    def take(m, half, p):
                        for t in range(2):
                            act.wait_ge(d_done[t], m + 1)
                            if t == 0:
                                wait(ys_out[p], 16 * slot_tiles_to(half, p))
                            act.mul(ysb[p][:, t, :], DB[t][:, 0:DIM], 1.0 / (GU_SCALE * DOWN_SCALE)).then_inc(d_taken[t], 1)

                    def window(m, half, p, u, w, kind, prev, nxt, opens, static):
                        if nxt == "slot":
                            c = slot_tiles_to(half + p, 1 - p)
                            act.wait_ge(xs_turned[1 - p], c + 1)
                            act.copy(xsT[1 - p][0][:, :, :], TB[1 - p][:, :].rearrange("p (h t) -> p h t", h=HALVES)
                                     ).then_inc(xs_hi[1 - p], 1)
                        for g in range(PAIRS_F):
                            b = g % 2
                            n = 2 * m + g // 2
                            act.wait_ge(g_done[b], n + 1)
                            wait(h32_ready[b], n)
                            act.activation(sg[b][:, :, :], GB[b][0:FP, :].rearrange("p (f s) -> p f s", f=2), ACT.Silu,
                                           scale=1.0 / GU_SCALE).then_inc(sg_ready[b], 1)
                            if opens:
                                if g == 1:
                                    wait(d_done[1], 0 if static in (0, E0) else m - 1)
                                    split_hi(2, u, w)
                                elif g >= 2 and static != E1:
                                    split_hi(g - 2, u + 1, 1 - w)
                            act.wait_ge(h32_ready[b], n + 1)
                            if g == 0:
                                wait(d_done[1], m - 1)
                            act.copy(hh[p][0][:, 2 * g:2 * g + 2, :], h32[b][:, :, :]).then_inc(h_hi[b], 1)
                        if prev == "slot":
                            take(m - 1, half - 1 + p, 1 - p)

                    run_windows(act, window)

                @block.vector
                def _(dve):
                    def wait(semaphore, n):
                        if not (isinstance(n, int) and n <= 0):
                            dve.wait_ge(semaphore, n)

                    def split_lo(k, u, w):
                        dve.wait_ge(w_hi[k], u + 1)
                        if k < HALVES:
                            dve.scalar_tensor_tensor(gu[w][1][:, k, :], raw[k][:, :], GU_SCALE, gu[w][0][:, k, :],
                                                     ALU.mult, ALU.subtract).then_inc(w_lo[k], 1)
                        else:
                            dve.scalar_tensor_tensor(down[w][1][:, :, :], raw[2][:, :, :], DOWN_SCALE, down[w][0][:, :, :],
                                                     ALU.mult, ALU.subtract).then_inc(w_lo[2], 1)

                    def combine(upto, m):
                        for n in range(combined[0], upto):
                            t, k = n // TOPK, n % TOPK
                            wait(y_added, n)
                            if k == 0:
                                dve.wait_ge(d_taken[t % 2], m - 1)
                            dve.wait_ge(y_in[n % AHEAD], 16 * (n // AHEAD + 1))
                            dve.scalar_tensor_tensor(xres[:, t, :], yg[n % AHEAD][:, :], share[k][:, t:t + 1], xres[:, t, :],
                                                     ALU.mult, ALU.add).then_inc(y_added, 1)
                        combined[0] = upto

                    combined = [0]

                    def add_shared(m):
                        wait(y_added, combined[0])
                        tile = 2 * (m if m < E0 else m - SLOT_TILES)
                        for t in range(2):
                            dve.wait_ge(d_done[t], m + 1)
                            dve.scalar_tensor_tensor(xres[:, tile + t, :], DB[t][:, 0:DIM], 1.0 / (GU_SCALE * DOWN_SCALE),
                                                     xres[:, tile + t, :], ALU.mult, ALU.add).then_inc(d_taken[t], 1)

                    def window(m, half, p, u, w, kind, prev, nxt, opens, static):
                        if nxt == "slot":
                            c = slot_tiles_to(half + p, 1 - p)
                            dve.wait_ge(xs_hi[1 - p], c + 1)
                            dve.tensor_tensor(xsT[1 - p][1][:, :, :], TB[1 - p][:, :].rearrange("p (h t) -> p h t", h=HALVES),
                                              xsT[1 - p][0][:, :, :], ALU.subtract).then_inc(xs_lo[1 - p], 1)
                        for g in range(PAIRS_F):
                            b = g % 2
                            n = 2 * m + g // 2
                            dve.wait_ge(sg_ready[b], n + 1)
                            dve.tensor_tensor(h32[b][:, :, :], sg[b][:, :, :], UB[b][0:FP, :].rearrange("p (f s) -> p f s", f=2),
                                              ALU.mult).then_inc(h32_ready[b], 1)
                            if opens:
                                if g == 1:
                                    split_lo(2, u, w)
                                elif g >= 2 and static != E1:
                                    split_lo(g - 2, u + 1, 1 - w)
                            dve.wait_ge(h_hi[b], n + 1)
                            dve.tensor_tensor(hh[p][1][:, 2 * g:2 * g + 2, :], h32[b][:, :, :], hh[p][0][:, 2 * g:2 * g + 2, :],
                                              ALU.subtract).then_inc(h_lo[b], 1)
                            if static in COMBINED:
                                combine(COMBINED[static][g], m)
                        if prev == "shared":
                            add_shared(m - 1)
                    run_windows(dve, window)
                    combine(TILES * TOPK, LAST)
                    add_shared(LAST - 1)

                @block.gpsimd
                def _(pool):
                    def store(m, p):
                        for t in range(2):
                            pool.wait_ge(d_taken[t], m + 1)
                        pool.dma_start(ys_rows[bass.ds((m - SH) * SLOTS, SLOTS), :].rearrange("(t p) d -> p t d", p=P),
                                       ysb[p][:, :, :]).then_inc(ys_out[p], 16)

                    for t in range(TILES):
                        for k in range(TOPK):
                            pool.indirect_dma_start(out=xs_rows, out_offset=bass.IndirectOffsetOnAxis(ap=pos_u[k][:, t:t + 1], axis=0),
                                                    in_=xn[:, t, :], in_offset=None).then_inc(scattered, 16)
                    store(E0, E0 % 2)
                    with pool.Fori(0, (SLOT_TILES - 1) // 2) as k:
                        for s in range(2):
                            store(2 * k + E0 + 1 + s, (E0 + 1 + s) % 2)
                    pool.wait_ge(ys_out[E0 % 2], 16 * ((SLOT_TILES + 1) // 2))
                    pool.wait_ge(ys_out[1 - E0 % 2], 16 * (SLOT_TILES // 2))
                    for n in range(TILES * TOPK):
                        t, k = n // TOPK, n % TOPK
                        if n >= AHEAD:
                            pool.wait_ge(y_added, n - AHEAD + 1)
                        pool.indirect_dma_start(out=yg[n % AHEAD][:, :], out_offset=None, in_=ys_rows,
                                                in_offset=bass.IndirectOffsetOnAxis(ap=pos_u[k][:, t:t + 1], axis=0)
                                                ).then_inc(y_in[n % AHEAD], 16)


def kernel(**inputs):
    import concourse.bacc as bacc
    from concourse.bass_utils import run_bass_kernel_spmd

    a = {k: np.asarray(v) for k, v in inputs.items()}
    gate_up = np.concatenate([a["L0_ffn_shared_gate_up"][None], a["L0_ffn_experts_gate_up"]])
    down = np.concatenate([a["L0_ffn_shared_down"][None], a["L0_ffn_experts_down"]])
    gu_t = np.zeros((EXPERTS + 1, DIM, 2, FG * FP), np.float32)
    gu_t[:, :, :, 0:FF] = gate_up.reshape(EXPERTS + 1, 2, FF, DIM).transpose(0, 3, 1, 2)
    down_t = np.zeros((EXPERTS + 1, FG * FP, DIM), np.float32)
    down_t[:, 0:FF, :] = down.transpose(0, 2, 1)
    xp = a["L0_attn_x_proj_w"]
    sel = np.zeros((3, 2 * STATE, 2 * STATE, P // 2), np.uint32)
    for n in range(2 * STATE):
        sel[:, n, n, :] = 0x3F803F80
    laid = {
        "x": a["x"].reshape(TOKENS, DIM),
        "ctx_rows": a["ctx_1024"].reshape(BATCH * CTX, DIM),
        "mask_t": a["mask_BxSxS2_bk0"].transpose(0, 2, 1).reshape(BATCH * CTX, SEQ).view(np.uint32),
        "wq": a["L0_xattn_Wq"], "wk": a["L0_xattn_Wk"], "wv_t": a["L0_xattn_Wv"].T,
        "in_w_t": a["L0_attn_in_proj_w"].T, "conv_w": a["L0_attn_conv_w"], "conv_b": a["L0_attn_conv_b"],
        "bc_w_t": xp[1:].T, "dt_row_t": np.repeat(xp[0:1].T, P, axis=1),
        "a_log": a["L0_attn_A_log"], "d_param": a["L0_attn_D_param"], "dt_w": a["L0_attn_dt_w"], "dt_b": a["L0_attn_dt_b"],
        "out_w_t": a["L0_attn_out_w"].T, "ln_g": a["L0_attn_ln_g"], "ln_b": a["L0_attn_ln_b"],
        "gate_w_t": a["L0_ffn_gate_weight"].T,
        "gu_t": gu_t.reshape((EXPERTS + 1) * DIM, 2 * FG * FP), "down_t": down_t.reshape((EXPERTS + 1) * FG * FP, DIM),
        "ident_in": np.eye(P, dtype=np.float32),
        "sel_in": sel.reshape(6 * STATE, 2 * STATE, P // 2),
        "consts_t": np.tile(np.concatenate([np.arange(2 * SLOT_TILES), SLOTS * np.arange(EXPERTS)]).astype(np.float32), (P, 1)),
        "tri_in": np.triu(np.ones((P, P), np.float32), 1),
    }
    nc = bacc.Bacc("TRN2", target_bir_lowering=False, num_devices=1)
    arrays, args = {}, []
    for name, array in laid.items():
        arrays[name] = np.ascontiguousarray(array)
        args.append(nc.dram_tensor(name, array.shape, mybir.dt.from_np(array.dtype), kind="ExternalInput").ap())
    out = nc.dram_tensor("out", (TOKENS, DIM), F32, kind="ExternalOutput").ap()
    build(nc, *args, out)
    result = run_bass_kernel_spmd(nc, [arrays], core_ids=[0])
    return result.results[0]["out"].reshape(BATCH, SEQ, DIM)
```
